# Optimizing a Trainium2 kernel written in Bass

```python
import numpy as np
import jax
import jax.numpy as jnp

def _softmax(x, axis=-1):
    return jax.nn.softmax(x, axis=axis)

def _gelu(x):
    return jax.nn.gelu(x, approximate=True)

def _silu(x):
    return jax.nn.silu(x)

def _sigmoid(x):
    return jax.nn.sigmoid(x)

def _layernorm(x, axis=-1, eps=1e-05):
    m = jnp.mean(x, axis=axis, keepdims=True)
    v = jnp.var(x, axis=axis, keepdims=True)
    return (x - m) / jnp.sqrt(v + eps)

def _scatter_add(tgt, idx, src, axis=0):
    return tgt.at[idx].add(src)

def _segment_sum(src, seg, n):
    return jax.ops.segment_sum(src, seg, n)
kernel_name = 'mk_gnn_ffn_d1_gnn_r8_d18d3a'

def setup_inputs(seed: int=0):
    np.random.seed(seed)
    _w = jnp.asarray

    def _rec_inputs():
        import jax
        import jax.numpy as jnp
        _gk = jax.random.key(seed)
        x = -0.0003713 + 1 * jax.random.normal(jax.random.fold_in(_gk, 1), (12500, 256), jnp.float32)
        src = jax.random.randint(jax.random.fold_in(_gk, 2), (200000,), 0, 12500, jnp.int32)
        dst = jax.random.randint(jax.random.fold_in(_gk, 3), (200000,), 0, 12500, jnp.int32)
        _o = jnp.argsort(dst, stable=True)
        src = src[_o]
        dst = dst[_o]
        edge_weight = jax.random.uniform(jax.random.fold_in(_gk, 12), (200000,), jnp.float32, 0.0, 0.999998)
        return (x, src, dst, edge_weight)
    x, src, dst, edge_weight = _rec_inputs()

    def _L0_gnn_setup():
        import jax, jax.numpy as jnp
        import numpy as np
        EPS = 1e-05

        def _bn(x, gamma, beta):
            m = jnp.mean(x, axis=0)
            v = jnp.mean((x - m) ** 2, axis=0)
            return gamma * (x - m) * jax.lax.rsqrt(v + EPS) + beta

        def _hconv(x, src, dst, ew, w1, b1, w2, b2, g, b):
            h = jax.nn.relu(x @ w1 + b1)
            msg = ew[:, None] * h[src]
            agg = jax.ops.segment_sum(msg, dst, num_segments=x.shape[0])
            h = agg @ w2 + b2
            return jax.nn.relu(_bn(h, g, b))
        N, C, E = (6250, 256, 37500)
        key = jax.random.key(seed)
        ks = jax.random.split(key, 16)
        s = 1.0 / np.sqrt(C)
        inp = {'x': jax.random.normal(ks[0], (N, C), dtype=jnp.float32), 'hyperedge_index': jax.random.randint(ks[1], (2, E), 0, N, dtype=jnp.int32), 'hyperedge_weight': jax.random.uniform(ks[2], (E,), dtype=jnp.float32), 'c1_w1': jax.random.normal(ks[3], (C, C), dtype=jnp.float32) * s, 'c1_b1': jnp.zeros((C,), jnp.float32), 'c1_w2': jax.random.normal(ks[4], (C, C), dtype=jnp.float32) * s, 'c1_b2': jnp.zeros((C,), jnp.float32), 'c1_g': jnp.ones((C,), jnp.float32), 'c1_b': jnp.zeros((C,), jnp.float32), 'bn1_g': jnp.ones((C,), jnp.float32), 'bn1_b': jnp.zeros((C,), jnp.float32), 'c2_w1': jax.random.normal(ks[5], (C, C), dtype=jnp.float32) * s, 'c2_b1': jnp.zeros((C,), jnp.float32), 'c2_w2': jax.random.normal(ks[6], (C, C), dtype=jnp.float32) * s, 'c2_b2': jnp.zeros((C,), jnp.float32), 'c2_g': jnp.ones((C,), jnp.float32), 'c2_b': jnp.zeros((C,), jnp.float32), 'bn2_g': jnp.ones((C,), jnp.float32), 'bn2_b': jnp.zeros((C,), jnp.float32)}
        return inp
    _L0_gnn_all = _L0_gnn_setup()
    _L0_gnn_in = {k: v for k, v in _L0_gnn_all.items() if k in ('c1_w1', 'c1_b1', 'c1_w2', 'c1_b2', 'c1_g', 'c1_b', 'bn1_g', 'bn1_b', 'c2_w1', 'c2_b1', 'c2_w2', 'c2_b2', 'c2_g', 'c2_b', 'bn2_g', 'bn2_b')}
    del _L0_gnn_all

    def _L0_ffn_setup():
        import jax, jax.numpy as jnp
        import numpy as np
        E = 8
        K = 2
        D = 256
        H = 512
        DOUT = 256
        EPS = 1e-05
        key = jax.random.key(seed)
        ks = jax.random.split(key, 9)
        s = 0.02
        return {'x': jax.random.normal(ks[0], (4, 1024, D), jnp.float32), 'gamma': 1.0 + 0.05 * jax.random.normal(ks[1], (D,), jnp.float32), 'beta': 0.05 * jax.random.normal(ks[2], (D,), jnp.float32), 'Wr': 0.01 * jax.random.normal(ks[3], (D, E), jnp.float32), 'br': jnp.zeros((E,), jnp.float32), 'W1': s * jax.random.normal(ks[4], (E, D, H), jnp.float32), 'b1': s * jax.random.normal(ks[5], (E, H), jnp.float32), 'W2': s * jax.random.normal(ks[6], (E, H, DOUT), jnp.float32), 'b2': s * jax.random.normal(ks[7], (E, DOUT), jnp.float32)}
    _L0_ffn_all = _L0_ffn_setup()
    _L0_ffn_in = {k: v for k, v in _L0_ffn_all.items() if k in ('gamma', 'beta', 'Wr', 'br', 'W1', 'b1', 'W2', 'b2')}
    del _L0_ffn_all
    return {'x': x, 'src': src, 'dst': dst, 'edge_weight': edge_weight, 'L0_gnn_c1_w1': _L0_gnn_in['c1_w1'], 'L0_gnn_c1_b1': _L0_gnn_in['c1_b1'], 'L0_gnn_c1_w2': _L0_gnn_in['c1_w2'], 'L0_gnn_c1_b2': _L0_gnn_in['c1_b2'], 'L0_gnn_c1_g': _L0_gnn_in['c1_g'], 'L0_gnn_c1_b': _L0_gnn_in['c1_b'], 'L0_gnn_bn1_g': _L0_gnn_in['bn1_g'], 'L0_gnn_bn1_b': _L0_gnn_in['bn1_b'], 'L0_gnn_c2_w1': _L0_gnn_in['c2_w1'], 'L0_gnn_c2_b1': _L0_gnn_in['c2_b1'], 'L0_gnn_c2_w2': _L0_gnn_in['c2_w2'], 'L0_gnn_c2_b2': _L0_gnn_in['c2_b2'], 'L0_gnn_c2_g': _L0_gnn_in['c2_g'], 'L0_gnn_c2_b': _L0_gnn_in['c2_b'], 'L0_gnn_bn2_g': _L0_gnn_in['bn2_g'], 'L0_gnn_bn2_b': _L0_gnn_in['bn2_b'], 'L0_ffn_gamma': _L0_ffn_in['gamma'], 'L0_ffn_beta': _L0_ffn_in['beta'], 'L0_ffn_Wr': _L0_ffn_in['Wr'], 'L0_ffn_br': _L0_ffn_in['br'], 'L0_ffn_W1': _L0_ffn_in['W1'], 'L0_ffn_b1': _L0_ffn_in['b1'], 'L0_ffn_W2': _L0_ffn_in['W2'], 'L0_ffn_b2': _L0_ffn_in['b2']}

def reference(x, src, dst, edge_weight, L0_gnn_c1_w1, L0_gnn_c1_b1, L0_gnn_c1_w2, L0_gnn_c1_b2, L0_gnn_c1_g, L0_gnn_c1_b, L0_gnn_bn1_g, L0_gnn_bn1_b, L0_gnn_c2_w1, L0_gnn_c2_b1, L0_gnn_c2_w2, L0_gnn_c2_b2, L0_gnn_c2_g, L0_gnn_c2_b, L0_gnn_bn2_g, L0_gnn_bn2_b, L0_ffn_gamma, L0_ffn_beta, L0_ffn_Wr, L0_ffn_br, L0_ffn_W1, L0_ffn_b1, L0_ffn_W2, L0_ffn_b2):
    import jax
    import jax.numpy as jnp

    def _L0_gnn_ref(x, hyperedge_index, hyperedge_weight, c1_w1, c1_b1, c1_w2, c1_b2, c1_g, c1_b, bn1_g, bn1_b, c2_w1, c2_b1, c2_w2, c2_b2, c2_g, c2_b, bn2_g, bn2_b):
        import jax, jax.numpy as jnp
        import numpy as np
        EPS = 1e-05

        def _bn(x, gamma, beta):
            m = jnp.mean(x, axis=0)
            v = jnp.mean((x - m) ** 2, axis=0)
            return gamma * (x - m) * jax.lax.rsqrt(v + EPS) + beta

        def _hconv(x, src, dst, ew, w1, b1, w2, b2, g, b):
            h = jax.nn.relu(x @ w1 + b1)
            msg = ew[:, None] * h[src]
            agg = jax.ops.segment_sum(msg, dst, num_segments=x.shape[0])
            h = agg @ w2 + b2
            return jax.nn.relu(_bn(h, g, b))
        src, dst = (hyperedge_index[0], hyperedge_index[1])
        residual = x
        h = _hconv(x, src, dst, hyperedge_weight, c1_w1, c1_b1, c1_w2, c1_b2, c1_g, c1_b)
        h = jax.nn.relu(_bn(h, bn1_g, bn1_b))
        h = _hconv(h, src, dst, hyperedge_weight, c2_w1, c2_b1, c2_w2, c2_b2, c2_g, c2_b)
        h = _bn(h, bn2_g, bn2_b)
        return jax.nn.relu(h + residual)

    def _L0_ffn_ref(x, gamma, beta, Wr, br, W1, b1, W2, b2):
        import jax, jax.numpy as jnp
        import numpy as np
        E = 8
        K = 2
        D = 256
        H = 512
        DOUT = 256
        EPS = 1e-05
        mu = jnp.mean(x, axis=-1, keepdims=True)
        var = jnp.mean(jnp.square(x - mu), axis=-1, keepdims=True)
        xn = (x - mu) * jax.lax.rsqrt(var + EPS) * gamma + beta
        logits = jnp.einsum('bsd,de->bse', xn, Wr) + br
        top_vals, top_idx = jax.lax.top_k(logits, K)
        w = jax.nn.softmax(top_vals, axis=-1)
        w_full = jnp.einsum('bsk,bske->bse', w, jax.nn.one_hot(top_idx, E, dtype=w.dtype))
        y = jnp.zeros(x.shape[:-1] + (DOUT,), x.dtype)
        for e in range(E):
            h = jax.nn.gelu(jnp.einsum('bsd,dh->bsh', xn, W1[e]) + b1[e], approximate=False)
            y_e = jnp.einsum('bsh,hd->bsd', h, W2[e]) + b2[e]
            y = y + y_e * w_full[..., e, None]
        return y
    edge_index = jnp.stack([src, dst])
    x = x + _L0_gnn_ref(_layernorm(x, axis=-1), edge_index, edge_weight, L0_gnn_c1_w1, L0_gnn_c1_b1, L0_gnn_c1_w2, L0_gnn_c1_b2, L0_gnn_c1_g, L0_gnn_c1_b, L0_gnn_bn1_g, L0_gnn_bn1_b, L0_gnn_c2_w1, L0_gnn_c2_b1, L0_gnn_c2_w2, L0_gnn_c2_b2, L0_gnn_c2_g, L0_gnn_c2_b, L0_gnn_bn2_g, L0_gnn_bn2_b)
    x = x + _L0_ffn_ref(_layernorm(x, axis=-1)[None], L0_ffn_gamma, L0_ffn_beta, L0_ffn_Wr, L0_ffn_br, L0_ffn_W1, L0_ffn_b1, L0_ffn_W2, L0_ffn_b2)[0]
    return x

_drawn_inputs = setup_inputs


def setup_inputs(seed=0):
    import zlib

    import numpy as np

    out = dict(_drawn_inputs(seed))
    spreads = {'L0_gnn_c1_b1': (0.0, 0.1),
     'L0_gnn_c1_b2': (0.0, 0.8),
     'L0_gnn_c1_g': (1.0, 0.6),
     'L0_gnn_c1_b': (0.0, 0.298),
     'L0_gnn_bn1_g': (1.0, 0.2),
     'L0_gnn_bn1_b': (0.0, 0.1),
     'L0_gnn_c2_b1': (0.0, 0.1),
     'L0_gnn_c2_b2': (0.0, 0.8),
     'L0_gnn_c2_g': (1.0, 0.6),
     'L0_gnn_c2_b': (0.0, 0.318),
     'L0_gnn_bn2_g': (1.0, 0.2),
     'L0_gnn_bn2_b': (0.0, 0.1),
     'L0_ffn_br': (0.0, 0.1)}
    factors = {'L0_ffn_gamma': 8.0, 'L0_ffn_beta': 8.0, 'L0_ffn_b1': 8.0, 'L0_ffn_b2': 7.45}
    for name, (base, spread) in spreads.items():
        noise = np.random.default_rng([zlib.crc32(name.encode()), seed]).standard_normal(out[name].shape)
        drawn = base * np.exp(spread * noise) if base else spread * noise
        out[name] = jnp.asarray(drawn.astype(out[name].dtype))
    for name, factor in factors.items():
        out[name] = (out[name] * factor).astype(out[name].dtype)
    return out
```

```python
from contextlib import ExitStack, contextmanager

import concourse.bass as bass
from concourse import mybir

ALU = mybir.AluOpType
ACT = mybir.ActivationFunctionType
F32 = mybir.dt.float32
BF16 = mybir.dt.bfloat16
I32 = mybir.dt.int32
U32 = mybir.dt.uint32

P = 128
EPS = 1e-5
NODES = 12500
C = 256
CG = C // P
NODE_TILES = -(-NODES // P)
NODES_PAD = NODE_TILES * P
EDGES = 200000
EDGE_TILES = -(-EDGES // P)
STEPS = EDGE_TILES + NODE_TILES - 1
STEP_CHUNKS = -(-STEPS // P)
EDGE_ROWS = STEP_CHUNKS * P

RING = 20
HALF = RING // 2
SUM_BANKS = 4
LEAD = 4
ROUNDS = STEPS // RING
assert ROUNDS * RING == STEPS and RING % SUM_BANKS == 0 and RING % LEAD == 0

COLS = 512
CHUNKS = NODES // COLS
REST = NODES - CHUNKS * COLS

GROUP = 7
GROUPS = NODE_TILES // GROUP
assert GROUPS * GROUP == NODE_TILES and GROUPS % 2 == 0

EXPERTS = 8
HIDDEN = 512
HG = HIDDEN // P
PAIRS = 2 * NODES_PAD
FFN_TILES = PAIRS // P + EXPERTS
FFN_UNROLL = 4
assert FFN_TILES % FFN_UNROLL == 0
FFN_LIST = FFN_TILES + 8
TABLE_TILES = EXPERTS * NODE_TILES + 16
TABLE_ROWS = TABLE_TILES * P
OUT_ROWS = NODES_PAD + P


def gate(eng, sem, value, passed):
    eng.wait_ge(sem, value)
    eng.sem_inc(passed, 1)


@contextmanager
def phase(nc, name):
    held = []

    def semaphore(n):
        held.append(nc.alloc_semaphore(name=f"{name}_{n}"))
        return held[-1]

    with ExitStack() as ctx:
        yield (lambda n, shape, dt: ctx.enter_context(nc.sbuf_tensor(f"{name}_{n}", shape, dt)),
               lambda n, shape, dt: ctx.enter_context(nc.psum_tensor(f"{name}_{n}", shape, dt)),
               semaphore, ctx)
    nc.clear_and_free_semaphores(held)
    nc.all_engine_barrier()


def plan_steps(nc, d, t):
    with phase(nc, "pl") as (sb, ps, sem, ctx):
        K = STEP_CHUNKS
        last_dst = sb("last_dst", [P, K], I32)
        block_of_last = sb("block_of_last", [P, K], I32)
        tile_no_i = sb("tile_no_i", [P, K], I32)
        tile_no = sb("tile_no", [P, K], F32)
        entry = sb("entry", [P, K], F32)
        step_row_i = sb("step_row_i", [P, K * P], I32)
        step_row = sb("step_row", [P, K * P], F32)
        entered = sb("entered", [P, K, K * P], BF16)
        ones_bf = sb("ones_bf", [P, 1], BF16)
        step_tile = sb("step_tile", [P, K], F32)
        step_tile_i = sb("step_tile_i", [P, K], I32)
        step_no = sb("step_no", [P, K], F32)
        step_node = sb("step_node", [P, K], F32)
        step_node_i = sb("step_node_i", [P, K], I32)
        g_src = sb("g_src", [P, K, P], I32)
        g_dst = sb("g_dst", [P, K, P], I32)
        g_ew = sb("g_ew", [P, K, P], F32)
        f_src = sb("f_src", [P, K, P], F32)
        f_dst = sb("f_dst", [P, K, P], F32)
        count = ps("count", [P, 512], F32)
        turned = ps("turned", [P, 4, 512], F32)

        s_in = sem("in")
        s_iota = sem("iota")
        s_chain = sem("chain")
        s_entered = sem("entered")
        s_count = sem("count")
        s_tile = sem("tile")
        s_node = sem("node")
        s_list = sem("list")
        s_row = sem("row")
        s_rows = [sem(f"rows{a}") for a in range(3)]
        s_float = [sem(f"float{a}") for a in range(2)]
        s_turned = sem("turned")
        s_out = sem("out")
        s_ident = sem("ident")
        s_pad = sem("pad")
        s_mask = sem("mask")
        s_table = sem("table")
        s_columns = sem("columns")

        groups = [(a, c, min(c + 4, K)) for a in range(3) for c in range(0, K, 4)]
        block = ctx.enter_context(nc.Block())

        @block.sync
        def _(sp):
            with nc.allow_non_contiguous_dma(reason="one word of each row, 1664 in all"):
                sp.dma_start(last_dst[:], d["dst"].rearrange("(c p) e -> p c e", p=P)[:, :, P - 1]).then_inc(s_in, 16)
            with nc.allow_non_contiguous_dma(reason="256 words, one for each channel"):
                sp.dma_start(t["gamma"][:], d["gamma"].rearrange("(k p) -> p k", p=P)).then_inc(s_columns, 16)
                sp.dma_start(t["beta"][:], d["beta"].rearrange("(k p) -> p k", p=P)).then_inc(s_columns, 16)
            sp.wait_ge(s_node, 1)
            with nc.allow_non_contiguous_dma(reason="1664 words"):
                sp.dma_start(d["step_list"].rearrange("(c p) -> p c", p=P), step_node_i[:]).then_inc(s_list, 16)
            sp.wait_ge(s_list, 16)
            sp.dma_start(t["step_nodes"][0:1, :], d["step_list"].rearrange("(a n) -> a n", a=1)).then_inc(s_row, 16)
            sp.wait_ge(s_mask, 2)
            sp.dma_start(d["table"].rearrange("(p b) w -> p b w", p=P), t["pad_slots"][:]).then_inc(s_table, 16)
            sp.wait_ge(s_pad, 1)
            sp.dma_start(d["tokens"][NODES_PAD:OUT_ROWS, :], t["zeros"][:]).then_inc(s_table, 16)
            sp.dma_start(d["out"][NODES_PAD:OUT_ROWS, :], t["zeros"][:]).then_inc(s_table, 16)
            sp.wait_ge(s_row, 16)
            sp.wait_ge(s_table, 48)
            sp.wait_ge(s_columns, 32)

        @block.gpsimd
        def _(pool):
            pool.iota(tile_no_i[:], [[P, K]], base=1, channel_multiplier=1).then_inc(s_iota, 1)
            pool.iota(step_row_i[:], [[1, K * P]], base=0, channel_multiplier=0).then_inc(s_iota, 1)
            pool.memset(t["ident"][:], 0.0).then_inc(s_ident, 1)
            pool.wait_ge(s_ident, 1)
            pool.affine_select(out=t["ident"][:], in_=t["ident"][:], compare_op=ALU.not_equal, fill=1.0, base=0,
                               pattern=[[-1, P]], channel_multiplier=1).then_inc(s_ident, 1)
            pool.iota(t["pad_slots"][:, :, 0], [[1, TABLE_ROWS // P]], base=0,
                      channel_multiplier=TABLE_ROWS // P).then_inc(s_iota, 1)
            pool.memset(t["pad_slots"][:, :, 1], 0).then_inc(s_iota, 1)
            pool.iota(t["iota_i"][:], [[1, P]], base=0, channel_multiplier=0).then_inc(s_iota, 1)
            pool.memset(t["zeros"][:], 0.0).then_inc(s_pad, 1)
            pool.memset(t["minus_half"][:], -0.5)
            pool.memset(t["ones"][:], 1.0).then_inc(s_pad, 1)
            pool.wait_ge(s_pad, 2)
            pool.affine_select(out=t["before"][:], in_=t["ones"][:], compare_op=ALU.is_gt, fill=0.0, base=0,
                               pattern=[[1, P]], channel_multiplier=-1).then_inc(s_pad, 1)
            pool.wait_ge(s_tile, 2)
            for c in range(K):
                for a, (rows, dest) in enumerate(((d["src"], g_src), (d["dst"], g_dst), (d["ew"], g_ew))):
                    pool.indirect_dma_start(dest[:, c, :], None, rows,
                                            bass.IndirectOffsetOnAxis(ap=step_tile_i[:, c:c + 1], axis=0)
                                            ).then_inc(s_rows[a], 16)

        @block.vector
        def _(dve):
            n = [0]

            def link(ins):
                n[0] += 1
                ins.then_inc(s_chain, 1)
                dve.wait_ge(s_chain, n[0])

            dve.memset(ones_bf[:], 1.0).then_inc(s_entered, 1)
            dve.wait_ge(s_in, 16)
            link(dve.tensor_scalar(block_of_last[:], last_dst[:], 7, None, ALU.logical_shift_right))
            dve.wait_ge(s_iota, 5)
            link(dve.tensor_copy(tile_no[:], tile_no_i[:]))
            dve.tensor_copy(step_row[:], step_row_i[:]).then_inc(s_chain, 1)
            n[0] += 1
            link(dve.tensor_tensor(entry[:], block_of_last[:], tile_no[:], ALU.add))
            for c in range(K):
                dve.tensor_scalar(entered[:, c, :], step_row[:], entry[:, c:c + 1], None,
                                  ALU.is_ge).then_inc(s_entered, 1)
            dve.tensor_copy(t["iota"][:], t["iota_i"][:]).then_inc(s_mask, 1)
            dve.tensor_scalar(t["pad_slots"][:, :, 0], t["pad_slots"][:, :, 0], P - 1, NODES_PAD,
                              ALU.bitwise_and, ALU.bitwise_or).then_inc(s_mask, 1)
            link(dve.tensor_scalar(step_no[:], tile_no[:], -1.0, None, ALU.add))
            dve.wait_ge(s_count, 1)
            dve.tensor_copy(step_tile[:], count[:, 0:K]).then_inc(s_tile, 1)
            dve.tensor_copy(step_tile_i[:], count[:, 0:K]).then_inc(s_tile, 1)
            dve.wait_ge(s_tile, 2)
            link(dve.tensor_tensor(step_node[:], step_no[:], step_tile[:], ALU.subtract))
            link(dve.tensor_scalar(step_node[:], step_node[:], float(P), None, ALU.mult))
            dve.tensor_copy(step_node_i[:], step_node[:]).then_inc(s_node, 1)
            dve.wait_ge(s_rows[0], 16 * K)
            dve.tensor_copy(f_src[:], g_src[:]).then_inc(s_float[0], 1)
            dve.wait_ge(s_rows[1], 16 * K)
            for c in range(K):
                dve.tensor_scalar(f_dst[:, c, :], g_dst[:, c, :], step_node[:, c:c + 1], None,
                                  ALU.subtract).then_inc(s_float[1], 1)
            for g, (a, c0, c1) in enumerate(groups):
                dve.wait_ge(s_turned, g + 1)
                dest = (t["edge_src"], t["edge_dst"], t["edge_w"])[a]
                dve.tensor_copy(dest[:, c0 * P:c1 * P], turned[:, g % 4, 0:(c1 - c0) * P]).then_inc(s_out, 1)

        @block.tensor
        def _(pe):
            pe.wait_ge(s_entered, 1 + K)
            for c in range(K):
                for k in range(K):
                    last = pe.matmul(count[:, c:c + 1], entered[:, k, c * P:(c + 1) * P], ones_bf[:],
                                     start=(k == 0), stop=(k == K - 1))
            last.then_inc(s_count, 1)
            pe.wait_ge(s_ident, 2)
            for g, (a, c0, c1) in enumerate(groups):
                if g == 0:
                    pe.wait_ge(s_float[0], 1)
                if c0 == 0 and a == 1:
                    pe.wait_ge(s_float[1], K)
                if c0 == 0 and a == 2:
                    pe.wait_ge(s_rows[2], 16 * K)
                if g >= 4:
                    pe.wait_ge(s_out, g - 3)
                rows = (f_src, f_dst, g_ew)[a]
                for c in range(c0, c1):
                    last = pe.transpose(turned[:, g % 4, (c - c0) * P:(c - c0 + 1) * P], rows[:, c, :], t["ident"][:])
                last.then_inc(s_turned, 1)


def project_input(nc, d, t):
    with phase(nc, "pi") as (sb, ps, sem, ctx):
        U = 2
        x = sb("x", [P, U, C], F32)
        stats = sb("stats", [P, U, 6], F32)
        xn = sb("xn", [P, U, C], F32)
        xnT = sb("xnT", [P, U, C], F32)
        hb = sb("hb", [P, U, C], F32)
        w1 = sb("w1", [P, CG, C], F32)
        b1 = sb("b1", [P, C], F32)
        psT = ps("psT", [P, U, 512], F32)
        psH = ps("psH", [P, U, 512], F32)
        s_w = sem("w")
        s_x = [sem(f"x{u}") for u in range(U)]
        s_xn = sem("s_xn")
        s_T = sem("s_T")
        s_xT = sem("s_xT")
        s_H = sem("s_H")
        s_hb = sem("s_hb")
        s_h = sem("s_h")
        s_st = [sem(f"st{u}") for u in range(U)]
        s_var = sem("s_var")
        s_rstd = sem("s_rstd")
        chain = sem("chain")
        passed = sem("passed")
        x_view = d["x"].rearrange("(n p) c -> p n c", p=P)
        h_view = d["h"].rearrange("(n p) c -> p n c", p=P)
        block = ctx.enter_context(nc.Block())
        R = NODE_TILES // U
        LINKS = 2

        @block.sync
        def _(sp):
            sp.dma_start(w1[:], d["c1_w1"].rearrange("(k p) c -> p k c", p=P)).then_inc(s_w, 16)
            sp.dma_start(b1[:], d["c1_b1"].partition_broadcast(P)).then_inc(s_w, 16)
            sp.sem_inc(s_xn, U)
            with sp.Fori(0, R) as i:
                for u in range(U):
                    sp.wait_ge(s_xn, i * U + u + 1)
                    sp.dma_start(x[:, u, :], x_view[:, bass.ds(i * U + u, 1), :].rearrange("p a c -> p (a c)")
                                 ).then_inc(s_x[u], 16)

        @block.vector
        def _(dve):
            dve.wait_ge(s_w, 32)
            with dve.Fori(0, R) as i:
                for u in range(U):
                    n = i * U + u
                    links = n * LINKS
                    dve.wait_ge(s_x[u], i * 16 + 16)
                    dve.bn_stats(stats[:, u, :], x[:, u, :]).then_inc(chain, 1)
                    gate(dve, chain, links + 1, passed)
                    mv = t["node_mean"][:, u, :]
                    dve.bn_aggr(mv, stats[:, u, :]).then_inc(chain, 1)
                    dve.wait_ge(chain, links + 2)
                    rstd = t["node_mean"][:, u, 1:2]
                    dve.tensor_scalar(rstd, rstd, EPS, None, ALU.add).then_inc(s_var, 1)
                    dve.wait_ge(s_T, n + 1)
                    dve.wait_ge(s_rstd, n + 1)
                    dve.tensor_scalar(xn[:, u, :], x[:, u, :], mv[:, 0:1], rstd, ALU.subtract,
                                      ALU.mult).then_inc(s_xn, 1)
                    dve.tensor_copy(t["node_stats"][:, bass.ds(n * 2, 2)], mv)
                    dve.wait_ge(s_H, n + 1)
                    gate(dve, s_st[u], i * 16 + 16, passed)
                    dve.tensor_tensor(hb[:, u, :], psH[:, u, 0:C], b1[:], ALU.add).then_inc(s_hb, 1)

        @block.tensor
        def _(pe):
            pe.wait_ge(s_w, 32)
            pe.sem_inc(s_T, U)
            pe.sem_inc(s_hb, U)
            with pe.Fori(0, R) as i:
                for u in range(U):
                    n = i * U + u
                    pe.wait_ge(s_xn, U + n + 1)
                    for k in range(CG):
                        last = pe.transpose(psT[:, u, k * P:(k + 1) * P], xn[:, u, k * P:(k + 1) * P], t["ident"][:])
                    last.then_inc(s_T, 1)
                    pe.wait_ge(s_xT, n + 1)
                    pe.wait_ge(s_hb, n + 1)
                    for k in range(CG):
                        last = pe.matmul(psH[:, u, 0:C], xnT[:, u, k * P:(k + 1) * P], w1[:, k, :],
                                         start=(k == 0), stop=(k == CG - 1))
                    last.then_inc(s_H, 1)

        @block.scalar
        def _(act):
            for u in range(U):
                act.sem_inc(s_st[u], 16)
            act.preload_act_table(ACT.Relu)
            with act.Fori(0, R) as i:
                for u in range(U):
                    n = i * U + u
                    act.wait_ge(s_T, U + n + 1)
                    act.activation(xnT[:, u, :], psT[:, u, 0:C], ACT.Copy).then_inc(s_xT, 1)
                    act.wait_ge(s_hb, U + n + 1)
                    act.activation(hb[:, u, :], hb[:, u, :], ACT.Relu).then_inc(s_h, 1)
                    act.wait_ge(s_h, n + 1)
                    act.dma_start(h_view[:, bass.ds(n, 1), :].rearrange("p a c -> p (a c)"), hb[:, u, :]
                                  ).then_inc(s_st[u], 16)
            for u in range(U):
                act.wait_ge(s_st[u], 16 * (R + 1))

        @block.gpsimd
        def _(pool):
            with pool.Fori(0, R) as i:
                for u in range(U):
                    pool.wait_ge(s_var, i * U + u + 1)
                    rstd = t["node_mean"][:, u, 1:2]
                    pool.tensor_tensor(rstd, rstd, t["minus_half"][:], ALU.pow).then_inc(s_rstd, 1)


def sum_messages(nc, d, t, source, layer):
    with phase(nc, layer) as (sb, ps, sem, ctx):
        messages = sb("messages", [P, RING, C], F32)
        indices = sb("indices", [P, 2, HALF], I32)
        onehot = sb("onehot", [P, LEAD, P], F32)
        partial = ps("partial", [P, SUM_BANKS, 512], F32)
        s_message = [sem(f"s_message{k}") for k in range(RING)]
        s_index = sem("s_index")
        s_onehot = sem("s_onehot")
        s_multiplied = sem("s_multiplied")
        s_added = sem("s_added")
        s_zero = sem("s_zero")
        passed = sem("passed")
        sums = t["sums"]
        block = ctx.enter_context(nc.Block())

        @block.scalar
        def _(act):
            with act.Fori(0, ROUNDS) as i:
                for half in range(2):
                    first = i * RING + half * HALF
                    gate(act, s_multiplied, first + HALF, passed)
                    act.activation(indices[:, half, :], t["edge_src"][:, bass.ds(first, HALF)],
                                   ACT.Copy).then_inc(s_index, 1)

        @block.gpsimd
        def _(pool):
            with pool.Fori(0, ROUNDS) as i:
                for k in range(RING):
                    if k % HALF == 0:
                        gate(pool, s_index, i * 2 + k // HALF + 1, passed)
                    pool.indirect_dma_start(messages[:, k, :], None, source,
                                            bass.IndirectOffsetOnAxis(ap=indices[:, k // HALF, k % HALF:k % HALF + 1],
                                                                      axis=0)).then_inc(s_message[k], 16)

        @block.tensor
        def _(pe):
            pe.sem_inc(s_multiplied, RING)
            with pe.Fori(0, ROUNDS) as i:
                for k in range(RING):
                    n = i * RING + k
                    pe.wait_ge(s_onehot, n + 1)
                    pe.wait_ge(s_added, n + 1)
                    pe.wait_ge(s_message[k], i * 16 + 16)
                    for g in range(CG):
                        last = pe.matmul(partial[:, k % SUM_BANKS, g * P:(g + 1) * P],
                                         messages[:, k, g * P:(g + 1) * P], onehot[:, k % LEAD, :],
                                         start=True, stop=True)
                    last.then_inc(s_multiplied, 1)

        @block.vector
        def _(dve):
            def build(slot, step):
                return dve.tensor_scalar(onehot[:, slot, :], t["iota"][:], t["edge_dst"][:, bass.ds(step, 1)],
                                         t["edge_w"][:, bass.ds(step, 1)], ALU.is_equal, ALU.mult)

            dve.sem_inc(s_added, SUM_BANKS)
            for k in range(LEAD):
                build(k, k).then_inc(s_onehot, 1)
            dve.memset(sums[:], 0.0).then_inc(s_zero, 1)
            dve.wait_ge(s_zero, 1)
            regs = [dve.alloc_register(f"{layer}_node{k}") for k in range(4)]
            with dve.Fori(0, ROUNDS) as i:
                for k in range(RING):
                    n = i * RING + k
                    if k % 4 == 0:
                        dve.load(regs, t["step_nodes"][0:1, bass.ds(n, 4)])
                        nodes = [dve.snap(r, min_val=0, max_val=NODES_PAD - P) for r in regs]
                    where = sums[:, :, bass.ds(nodes[k % 4], P)]
                    dve.wait_ge(s_multiplied, RING + n + 1)
                    dve.wait_ge(s_added, SUM_BANKS + n)
                    dve.tensor_tensor(where, where, partial[:, k % SUM_BANKS, 0:C].rearrange("p (g n) -> p g n", g=CG),
                                      ALU.add).then_inc(s_added, 1)
                    build(k % LEAD, n + LEAD).then_inc(s_onehot, 1)


def normalize_sums(nc, d, t, layer):
    with phase(nc, layer + "_ns") as (sb, ps, sem, ctx):
        U = 2
        sums = t["sums"]
        w2 = sb("w2", [P, CG, C], F32)
        b2 = sb("b2", [P, CG], F32)
        gains = sb("gains", [P, 2, CG], F32)
        shifts = sb("shifts", [P, 2, CG], F32)
        stats = sb("stats", [P, CG, CHUNKS + 1, 6], F32)
        moments = sb("moments", [P, CG, 2], F32)
        scale = sb("scale", [P, CG], F32)
        shift = sb("shift", [P, CG], F32)
        product = sb("product", [P, CG], F32)
        z = ps("z", [P, U * CG, 512], F32)
        s_w = sem("s_w")
        s_z = sem("s_z")
        s_biased = sem("s_biased")
        s_stats = sem("s_stats")
        s_var = sem("s_var")
        s_rstd = sem("s_rstd")
        s_chain = sem("s_chain")
        s_first = sem("s_first")
        s_relu = sem("s_relu")
        passed = sem("passed")
        block = ctx.enter_context(nc.Block())

        def over_chunks(eng, body):
            with eng.Fori(0, CHUNKS // U) as i:
                for u in range(U):
                    body(i * U + u, u, (i * U + u) * COLS, COLS)
            body(CHUNKS, 0, CHUNKS * COLS, REST)

        @block.sync
        def _(sp):
            sp.dma_start(w2[:], d[layer + "_w2"].rearrange("(k p) c -> p k c", p=P)).then_inc(s_w, 16)
            with nc.allow_non_contiguous_dma(reason="256 words, one for each channel"):
                sp.dma_start(b2[:], d[layer + "_b2"].rearrange("(k p) -> p k", p=P)).then_inc(s_w, 16)
                for n, bn in enumerate((layer, {"c1": "bn1", "c2": "bn2"}[layer])):
                    sp.dma_start(gains[:, n, :], d[bn + "_g"].rearrange("(k p) -> p k", p=P)).then_inc(s_w, 16)
                    sp.dma_start(shifts[:, n, :], d[bn + "_b"].rearrange("(k p) -> p k", p=P)).then_inc(s_w, 16)
            sp.wait_ge(s_w, 96)

        @block.tensor
        def _(pe):
            pe.wait_ge(s_w, 96)

            def product_of(chunk, u, col, cols):
                pe.wait_ge(s_biased, (chunk + 1) * CG)
                for co in range(CG):
                    for k in range(CG):
                        last = pe.matmul(z[:, u * CG + co, 0:cols], w2[:, k, co * P:(co + 1) * P],
                                         sums[:, k, bass.ds(col, cols)], start=(k == 0), stop=(k == CG - 1))
                last.then_inc(s_z, 1)

            over_chunks(pe, product_of)

        @block.scalar
        def _(act):
            act.preload_act_table(ACT.Relu)
            act.sem_inc(s_biased, U * CG)
            act.wait_ge(s_w, 96)

            def add_bias(chunk, u, col, cols):
                gate(act, s_z, chunk + 1, passed)
                for co in range(CG):
                    act.activation(sums[:, co, bass.ds(col, cols)], z[:, u * CG + co, 0:cols], ACT.Identity,
                                   bias=b2[:, co:co + 1]).then_inc(s_biased, 1)

            def first_norm(chunk, u, col, cols):
                for co in range(CG):
                    v = sums[:, co, bass.ds(col, cols)]
                    act.activation(v, v, ACT.Relu, bias=shift[:, co:co + 1],
                                   scale=scale[:, co:co + 1]).then_inc(s_relu, 1)

            over_chunks(act, add_bias)
            act.wait_ge(s_first, 1)
            over_chunks(act, first_norm)

        @block.gpsimd
        def _(pool):
            for n in range(2):
                pool.wait_ge(s_var, n + 1)
                for co in range(CG):
                    pool.tensor_tensor(moments[:, co, 1:2], moments[:, co, 1:2], t["minus_half"][:],
                                       ALU.pow).then_inc(s_rstd, 1)

        @block.vector
        def _(dve):
            n = [0]

            def link(ins):
                n[0] += 1
                ins.then_inc(s_chain, 1)
                dve.wait_ge(s_chain, n[0])

            def statistics(ready, counted_from):
                def of_chunk(chunk, u, col, cols):
                    for co in range(CG):
                        gate(dve, ready, chunk * CG + (counted_from + co + 1), passed)
                        dve.bn_stats(stats[:, co, bass.ds(chunk, 1), :].rearrange("p a s -> p (a s)"),
                                     sums[:, co, bass.ds(col, cols)]).then_inc(s_stats, 1)
                return of_chunk

            def coefficients(which, to_scale, to_shift):
                dve.wait_ge(s_stats, (which + 1) * CG * (CHUNKS + 1))
                for co in range(CG):
                    link(dve.bn_aggr(moments[:, co, :], stats[:, co, :, :].rearrange("p a s -> p (a s)")))
                dve.tensor_scalar(moments[:, :, 1], moments[:, :, 1], EPS, None, ALU.add).then_inc(s_var, 1)
                dve.wait_ge(s_rstd, (which + 1) * CG)
                link(dve.tensor_tensor(to_scale, gains[:, which, :], moments[:, :, 1], ALU.mult))
                link(dve.tensor_tensor(product[:], moments[:, :, 0], to_scale, ALU.mult))
                return dve.tensor_tensor(to_shift, shifts[:, which, :], product[:], ALU.subtract)

            over_chunks(dve, statistics(s_biased, U * CG))
            dve.wait_ge(s_w, 96)
            coefficients(0, scale[:], shift[:]).then_inc(s_first, 1)
            over_chunks(dve, statistics(s_relu, 0))
            coefficients(1, t["bn_scale"][:], t["bn_shift"][:])


def project_hidden(nc, d, t):
    with phase(nc, "ph") as (sb, ps, sem, ctx):
        U = 2
        TILES = 4
        a = sb("a", [P, U, CG, COLS], F32)
        biased = sb("biased", [P, U, TILES, C], F32)
        h = sb("h", [P, U, TILES, C], F32)
        w1 = sb("w1", [P, CG, C], F32)
        b1 = sb("b1", [P, C], F32)
        product = ps("product", [P, TILES, 512], F32)
        s_w = sem("s_w")
        s_a = sem("s_a")
        s_product = sem("s_product")
        s_biased = sem("s_biased")
        s_h = sem("s_h")
        s_stored = [sem(f"s_stored{u}") for u in range(U)]
        passed = sem("passed")
        h_view = d["h2"].rearrange("(n p) c -> p n c", p=P)
        LAST = NODE_TILES - CHUNKS * TILES
        block = ctx.enter_context(nc.Block())

        def over_chunks(eng, body):
            with eng.Fori(0, CHUNKS // U) as i:
                for u in range(U):
                    body(i, i * U + u, u, TILES)
            body(CHUNKS // U, CHUNKS, 0, LAST)

        @block.sync
        def _(sp):
            sp.dma_start(w1[:], d["c2_w1"].rearrange("(k p) c -> p k c", p=P)).then_inc(s_w, 16)
            sp.dma_start(b1[:], d["c2_b1"].partition_broadcast(P)).then_inc(s_w, 16)
            for u in range(U):
                sp.sem_inc(s_stored[u], 16)

            def store(i, chunk, u, tiles):
                sp.wait_ge(s_h, (chunk + 1) * TILES if tiles == TILES else CHUNKS * TILES + LAST)
                sp.dma_start(h_view[:, bass.ds(chunk * TILES, tiles), :], h[:, u, 0:tiles, :]
                             ).then_inc(s_stored[u], 16)

            over_chunks(sp, store)
            sp.wait_ge(s_stored[0], 16 * (CHUNKS // U + 2))
            sp.wait_ge(s_stored[1], 16 * (CHUNKS // U + 1))
            sp.wait_ge(s_w, 32)

        @block.scalar
        def _(act):
            act.preload_act_table(ACT.Relu)

            def norm(i, chunk, u, tiles):
                gate(act, s_product, (chunk + 1) * TILES, passed)
                for k in range(CG):
                    act.activation(a[:, u, k, 0:tiles * P], t["sums"][:, k, bass.ds(chunk * COLS, tiles * P)],
                                   ACT.Relu, bias=t["bn_shift"][:, k:k + 1],
                                   scale=t["bn_scale"][:, k:k + 1]).then_inc(s_a, 1)

            over_chunks(act, norm)

        @block.tensor
        def _(pe):
            pe.wait_ge(s_w, 32)
            pe.sem_inc(s_product, U * TILES)

            def multiply(i, chunk, u, tiles):
                for j in range(tiles):
                    n = chunk * TILES + j
                    if j == 0:
                        pe.wait_ge(s_a, (chunk + 1) * CG)
                    pe.wait_ge(s_biased, n + 1)
                    for k in range(CG):
                        last = pe.matmul(product[:, j, 0:C], a[:, u, k, j * P:(j + 1) * P], w1[:, k, :],
                                         start=(k == 0), stop=(k == CG - 1))
                    last.then_inc(s_product, 1)

            over_chunks(pe, multiply)

        @block.vector
        def _(dve):
            dve.wait_ge(s_w, 32)
            dve.sem_inc(s_biased, TILES)

            def bias(i, chunk, u, tiles):
                for j in range(tiles):
                    n = chunk * TILES + j
                    dve.wait_ge(s_product, U * TILES + n + 1)
                    if j == 0:
                        dve.wait_ge(s_stored[u], i * 16 + 16)
                    dve.tensor_tensor(biased[:, u, j, :], product[:, j, 0:C], b1[:], ALU.add).then_inc(s_biased, 1)

            over_chunks(dve, bias)

        @block.gpsimd
        def _(pool):
            def relu(i, chunk, u, tiles):
                for j in range(tiles):
                    gate(pool, s_biased, TILES + chunk * TILES + j + 1, passed)
                    if j == 0:
                        gate(pool, s_stored[u], i * 16 + 16, passed)
                    pool.tensor_scalar(h[:, u, j, :], biased[:, u, j, :], 0.0, None, ALU.max).then_inc(s_h, 1)

            over_chunks(pool, relu)


def route_tokens(nc, d, t):
    with phase(nc, "rt") as (sb, ps, sem, ctx):
        G, E = GROUP, EXPERTS
        x = sb("x", [P, 2, G, C], F32)
        y = sb("y", [P, 2, CG, P], F32)
        residual = sb("residual", [P, G, C], F32)
        x1 = sb("x1", [P, G, C], F32)
        l1 = sb("l1", [P, G, C], F32)
        tokens = sb("tokens", [P, G, C], F32)
        affine = sb("affine", [P, 2, CG, P], F32)
        stats = sb("stats", [P, G, 6], F32)
        moments = sb("moments", [P, 2, G, 2], F32)
        down = sb("down", [P, 2, G], F32)
        wr = sb("wr", [P, CG, E], F32)
        br = sb("br", [P, G, E], F32)
        minus_half = sb("minus_half", [P, G], F32)
        logits = sb("logits", [P, G, E], F32)
        top = sb("top", [P, G, E], F32)
        which = sb("which", [P, G, E], U32)
        which_f = sb("which_f", [P, G, E], F32)
        experts_i = sb("experts_i", [P, G, E], I32)
        experts = sb("experts", [P, G, E], F32)
        slots_of = sb("slots_of", [P, G, E], F32)
        chosen = sb("chosen", [P, 2, G, E], F32)
        both = sb("both", [P, G, E], F32)
        before_tile = sb("before_tile", [P, G + 1, E], F32)
        place = sb("place", [P, G, E], F32)
        picked = sb("picked", [P, 2, G, E], F32)
        slot_f = sb("slot_f", [P, 2, G], F32)
        slot = sb("slot", [P, 2, 2, G], I32)
        gap = sb("gap", [P, G], F32)
        ratio = sb("ratio", [P, G], F32)
        total = sb("total", [P, G], F32)
        token_i = sb("token_i", [P, G], I32)
        entry = sb("entry", [P, 2, 2, G, 2], I32)
        primer = sb("primer", [P, 2, 2], I32)
        ps_y = ps("ps_y", [P, 2, 512], F32)
        ps_t = ps("ps_t", [P, 2, 512], F32)
        ps_l = ps("ps_l", [P, 512], F32)
        ps_c = ps("ps_c", [P, 512], F32)

        s_w = sem("s_w")
        s_const = sem("s_const")
        s_const2 = sem("s_const2")
        s_x = [sem("s_x_in0"), sem("s_x_in1")]
        s_y = sem("s_y")
        s_turned = sem("s_turned")
        s_read = sem("s_read")
        s_res = sem("s_res")
        s_added = sem("s_added")
        s_x1 = sem("s_x1")
        s_x1_stored = sem("s_x1_stored")
        s_stat = sem("s_stat")
        s_aggr = sem("s_aggr")
        s_var = sem("s_var")
        s_rstd = sem("s_rstd")
        s_down = sem("s_down")
        s_l1 = sem("s_l1")
        s_token = sem("s_token")
        s_token_stored = sem("s_token_stored")
        s_back = sem("s_back")
        s_affine = sem("s_affine")
        s_logit = sem("s_logit")
        s_chain = sem("s_chain")
        s_gap = sem("s_gap")
        s_ratio = sem("s_ratio")
        s_both = sem("s_both")
        s_place = sem("s_place")
        s_entry = sem("s_entry")
        s_scatter = [sem("s_scatter0"), sem("s_scatter1")]
        passed = sem("passed")
        x_view = d["x"].rearrange("(n p) c -> p n c", p=P)
        out_view = d["out"].rearrange("(n p) c -> p n c", p=P)
        token_view = d["tokens"].rearrange("(n p) c -> p n c", p=P)
        block = ctx.enter_context(nc.Block())

        def over_groups(eng, body):
            with eng.Fori(0, GROUPS // 2) as i:
                for u in range(2):
                    body(i, i * 2 + u, u)

        @block.sync
        def _(sp):
            sp.dma_start(wr[:], d["wr"].rearrange("(k p) e -> p k e", p=P)).then_inc(s_w, 16)
            for g in range(G):
                sp.dma_start(br[:, g, :], d["br"].partition_broadcast(P)).then_inc(s_w, 16)
            sp.sem_inc(s_x1, 2 * G)
            sp.sem_inc(s_x1_stored, 16)
            sp.sem_inc(s_token_stored, 16)

            def move(g, u):
                sp.wait_ge(s_x1, (g + 1) * G)
                sp.dma_start(x[:, u, :, :], x_view[:, bass.ds(g * G, G), :]).then_inc(s_x[u], 16)

            def store(g):
                sp.wait_ge(s_x1, 2 * G + (g + 1) * G)
                sp.dma_start(out_view[:, bass.ds(g * G, G), :], x1[:]).then_inc(s_x1_stored, 16)
                sp.wait_ge(s_token, (g + 1) * G)
                sp.dma_start(token_view[:, bass.ds(g * G, G), :], tokens[:]).then_inc(s_token_stored, 16)

            move(0, 0)
            with sp.Fori(0, GROUPS // 2 - 1) as i:
                move(i * 2 + 1, 1)
                store(i * 2)
                move(i * 2 + 2, 0)
                store(i * 2 + 1)
            move(GROUPS - 1, 1)
            store(GROUPS - 2)
            store(GROUPS - 1)
            sp.wait_ge(s_x1_stored, 16 * (GROUPS + 1))
            sp.wait_ge(s_token_stored, 16 * (GROUPS + 1))

        @block.scalar
        def _(act):
            act.wait_ge(s_w, 16 * (G + 1))

            def body(i, g, u):
                for j in range(G):
                    n = g * G + j
                    q = j % 2
                    gate(act, s_turned, n + 1, passed)
                    for k in range(CG):
                        act.activation(y[:, (u + j) % 2, k, :], t["sums"][:, k, bass.ds(n * P, P)], ACT.Identity,
                                       bias=t["bn_shift"][:, k:k + 1], scale=t["bn_scale"][:, k:k + 1]
                                       ).then_inc(s_y, 1)
                for j in range(G):
                    if j == 0:
                        act.wait_ge(s_down, g * 2 + 1)
                    act.activation(l1[:, j, :], x1[:, j, :], ACT.Identity, bias=down[:, 0, j:j + 1],
                                   scale=moments[:, 0, j, 1:2]).then_inc(s_l1, 1)
                for j in range(G):
                    if j == 0:
                        act.wait_ge(s_down, g * 2 + 2)
                        gate(act, s_token_stored, g * 16 + 16, passed)
                    act.activation(tokens[:, j, :], l1[:, j, :], ACT.Identity, bias=down[:, 1, j:j + 1],
                                   scale=moments[:, 1, j, 1:2]).then_inc(s_token, 1)
                    if j > 0:
                        turn_affine(g, u, j - 1)
                turn_affine(g, u, G - 1)
                act.wait_ge(s_gap, g + 1)
                act.activation(ratio[:], gap[:], ACT.Exp).then_inc(s_ratio, 1)

            def turn_affine(g, u, j):
                n = g * G + j
                act.wait_ge(s_back, 2 + n + 1)
                for k in range(CG):
                    act.activation(affine[:, (u + j) % 2, k, :], ps_t[:, (u + j) % 2, k * P:(k + 1) * P], ACT.Identity,
                                   bias=t["beta"][:, k:k + 1], scale=t["gamma"][:, k:k + 1]).then_inc(s_affine, 1)

            act.preload_act_table(ACT.Exp)
            over_groups(act, body)

        @block.tensor
        def _(pe):
            pe.wait_ge(s_w, 16 * (G + 1))
            pe.sem_inc(s_turned, 2)
            pe.sem_inc(s_back, 2)

            def logit(g, u, j):
                n = g * G + j
                pe.wait_ge(s_affine, (n + 1) * CG)
                for k in range(CG):
                    last = pe.matmul(ps_l[:, j * E:(j + 1) * E], affine[:, (u + j) % 2, k, :], wr[:, k, :],
                                     start=(k == 0), stop=(k == CG - 1))
                last.then_inc(s_logit, 1)

            def body(i, g, u):
                for j in range(G):
                    n = g * G + j
                    pe.wait_ge(s_y, (n + 1) * CG)
                    pe.wait_ge(s_read, n + 1)
                    for k in range(CG):
                        last = pe.transpose(ps_y[:, (u + j) % 2, k * P:(k + 1) * P], y[:, (u + j) % 2, k, :],
                                            t["ident"][:])
                    last.then_inc(s_turned, 1)
                for j in range(G):
                    n = g * G + j
                    pe.wait_ge(s_token, n + 1)
                    if j == 0:
                        pe.wait_ge(s_both, g + 1)
                    if j > 1:
                        pe.wait_ge(s_affine, (n - 1) * CG)
                    for k in range(CG):
                        last = pe.transpose(ps_t[:, (u + j) % 2, k * P:(k + 1) * P],
                                            tokens[:, j, k * P:(k + 1) * P], t["ident"][:])
                    last.then_inc(s_back, 1)
                    if j > 0:
                        logit(g, u, j - 1)
                logit(g, u, G - 1)
                pe.wait_ge(s_both, g + 2)
                pe.matmul(ps_c[:, 0:G * E], t["before"][:], both[:].rearrange("p g e -> p (g e)"),
                          start=True, stop=False)
                pe.matmul(ps_c[:, 0:G * E], t["ones"][:], before_tile[:, 0:G, :].rearrange("p g e -> p (g e)"),
                          start=False, stop=True).then_inc(s_place, 1)

            over_groups(pe, body)

        @block.gpsimd
        def _(pool):
            pool.iota(experts_i[:], [[0, G], [1, E]], base=0, channel_multiplier=0).then_inc(s_const, 1)
            pool.iota(token_i[:], [[P, G]], base=-GROUP * P, channel_multiplier=1).then_inc(s_const, 1)
            pool.memset(minus_half[:], -0.5).then_inc(s_const, 1)
            pool.memset(before_tile[:], 0.0).then_inc(s_const, 1)
            pool.wait_ge(s_const, 4)
            for u in range(2):
                pool.dma_start(primer[:, u, :], d["src"][0:P, 0:2]).then_inc(s_scatter[u], 16 * 2 * G)

            def body(i, g, u):
                for norm in range(2):
                    gate(pool, s_var, g * 2 + norm + 1, passed)
                    pool.tensor_tensor(moments[:, norm, :, 1], moments[:, norm, :, 1], minus_half[:],
                                       ALU.pow).then_inc(s_rstd, 1)
                gate(pool, s_entry, g + 1, passed)
                for j in range(G):
                    for c in range(2):
                        pool.indirect_dma_start(d["table"], bass.IndirectOffsetOnAxis(ap=slot[:, u, c, j:j + 1], axis=0),
                                                entry[:, u, c, j, :], None).then_inc(s_scatter[u], 16)

            over_groups(pool, body)
            for u in range(2):
                pool.wait_ge(s_scatter[u], 16 * 2 * G * (GROUPS // 2 + 1))

        @block.vector
        def _(dve):
            dve.wait_ge(s_const, 4)
            dve.tensor_copy(experts[:], experts_i[:]).then_inc(s_const2, 1)
            dve.wait_ge(s_const2, 1)
            dve.tensor_scalar(slots_of[:], experts[:], float(NODES_PAD), None, ALU.mult).then_inc(s_const2, 1)
            dve.wait_ge(s_const2, 2)
            dve.sem_inc(s_both, 1)
            dve.sem_inc(s_read, 2)
            links = LINKS_ROUTE

            def body(i, g, u):
                n = [0]

                def link(ins):
                    n[0] += 1
                    ins.then_inc(s_chain, 1)
                    gate(dve, s_chain, g * links + n[0], passed)

                gate(dve, s_x[u], i * 16 + 16, passed)
                for j in range(G):
                    node = g * G + j
                    dve.tensor_scalar(residual[:, j, :], x[:, u, j, :], t["node_stats"][:, bass.ds(node * 2, 1)],
                                      t["node_stats"][:, bass.ds(node * 2 + 1, 1)], ALU.subtract,
                                      ALU.mult).then_inc(s_res, 1)
                for j in range(G):
                    node = g * G + j
                    dve.wait_ge(s_res, node + 1)
                    dve.wait_ge(s_turned, 2 + node + 1)
                    dve.tensor_tensor(residual[:, j, :], ps_y[:, (u + j) % 2, 0:C], residual[:, j, :],
                                      ALU.add).then_inc(s_read, 1)
                gate(dve, s_x1_stored, g * 16 + 16, passed)
                for j in range(G):
                    node = g * G + j
                    dve.wait_ge(s_read, 2 + node + 1)
                    dve.scalar_tensor_tensor(x1[:, j, :], residual[:, j, :], 0.0, x[:, u, j, :], ALU.max,
                                             ALU.add).then_inc(s_x1, 1)

                def norm(which, ready, counted_from, rows):
                    for j in range(G):
                        gate(dve, ready, counted_from + g * G + j + 1, passed)
                        dve.bn_stats(stats[:, j, :], rows[:, j, :]).then_inc(s_stat, 1)
                    for j in range(G):
                        gate(dve, s_stat, g * 2 * G + which * G + j + 1, passed)
                        dve.bn_aggr(moments[:, which, j, :], stats[:, j, :]).then_inc(s_aggr, 1)
                    gate(dve, s_aggr, (g * 2 + which + 1) * G, passed)
                    var = moments[:, which, :, 1]
                    dve.tensor_scalar(var, var, EPS, None, ALU.add).then_inc(s_var, 1)
                    dve.wait_ge(s_rstd, g * 2 + which + 1)
                    dve.scalar_tensor_tensor(down[:, which, :], moments[:, which, :, 0], -1.0, var, ALU.mult,
                                             ALU.mult).then_inc(s_down, 1)

                norm(0, s_x1, 2 * G, x1)
                norm(1, s_l1, 0, l1)
                gate(dve, s_logit, (g + 1) * G, passed)
                link(dve.tensor_tensor(logits[:], ps_l[:, 0:G * E].rearrange("p (g e) -> p g e", g=G), br[:], ALU.add))
                for j in range(G):
                    dve.max(top[:, j, :], logits[:, j, :]).then_inc(s_chain, 1)
                    n[0] += 1
                gate(dve, s_chain, g * links + n[0], passed)
                for j in range(G):
                    dve.max_index(which[:, j, :], top[:, j, :], logits[:, j, :]).then_inc(s_chain, 1)
                    n[0] += 1
                dve.tensor_tensor(gap[:], top[:, :, 1], top[:, :, 0], ALU.subtract).then_inc(s_gap, 1)
                gate(dve, s_chain, g * links + n[0], passed)
                link(dve.tensor_copy(which_f[:], which[:]))
                for c in range(2):
                    link(dve.tensor_tensor(chosen[:, c, :, :], experts[:],
                                           which_f[:, :, c:c + 1].to_broadcast([P, G, E]), ALU.is_equal))
                for j in range(G):
                    link(dve.tensor_tensor(both[:, j, :], chosen[:, 0, j, :], chosen[:, 1, j, :], ALU.add))
                    if j == 0:
                        link(dve.tensor_copy(before_tile[:, 0, :], before_tile[:, G, :]))
                    add = dve.tensor_tensor(before_tile[:, j + 1, :], before_tile[:, j, :], both[:, j, :], ALU.add)
                    if j < G - 1:
                        link(add)
                add.then_inc(s_both, 1)
                dve.wait_ge(s_ratio, g + 1)
                dve.wait_ge(s_both, g + 2)
                link(dve.tensor_scalar(total[:], ratio[:], 1.0, None, ALU.add))
                gate(dve, s_scatter[u], (i + 1) * (16 * 2 * G), passed)
                weight = entry[:, u, :, :, :].bitcast(F32)
                link(dve.reciprocal(weight[:, 0, :, 1], total[:]))
                link(dve.tensor_tensor(weight[:, 1, :, 1], weight[:, 0, :, 1], ratio[:], ALU.mult))
                link(dve.tensor_scalar(token_i[:], token_i[:], float(G * P), None, ALU.add))
                for c in range(2):
                    link(dve.tensor_copy(entry[:, u, c, :, 0], token_i[:]))
                dve.wait_ge(s_place, g + 1)
                link(dve.tensor_tensor(place[:], ps_c[:, 0:G * E].rearrange("p (g e) -> p g e", g=G), slots_of[:],
                                       ALU.add))
                for c in range(2):
                    link(dve.tensor_tensor(picked[:, c, :, :], place[:], chosen[:, c, :, :], ALU.mult))
                    link(dve.tensor_reduce(slot_f[:, c, :], picked[:, c, :, :], mybir.AxisListType.X, ALU.add))
                dve.tensor_copy(slot[:, u, :, :], slot_f[:]).then_inc(s_entry, 1)
                assert n[0] == links, n[0]

            over_groups(dve, body)
            dve.tensor_copy(t["chosen_by"][:], before_tile[:, G, :]).then_inc(s_const2, 1)
            dve.wait_ge(s_const2, 3)


LINKS_ROUTE = 15 + 4 * GROUP


def list_tiles(nc, d, t):
    with phase(nc, "lt") as (sb, ps, sem, ctx):
        E, L = EXPERTS, FFN_LIST
        counts_ps = ps("counts_ps", [P, 512], F32)
        counts = sb("counts", [P, E], I32)
        tiles_i = sb("tiles_i", [P, E], I32)
        tiles = sb("tiles", [P, E], F32)
        base = sb("base", [P, E], F32)
        tile_i = sb("tile_i", [P, L], I32)
        tile_no = sb("tile_no", [P, L], F32)
        within = sb("within", [P, L], F32)
        entered = sb("entered", [P, L], F32)
        expert = sb("expert", [P, L], F32)
        first = sb("first", [P, L], F32)
        s_counts = sem("s_counts")
        s_iota = sem("s_iota")
        s_chain = sem("s_chain")
        block = ctx.enter_context(nc.Block())

        @block.tensor
        def _(pe):
            pe.matmul(counts_ps[:, 0:E], t["ones"][:], t["chosen_by"][:], start=True, stop=True).then_inc(s_counts, 1)

        @block.gpsimd
        def _(pool):
            pool.iota(tile_i[:], [[1, L]], base=0, channel_multiplier=0).then_inc(s_iota, 1)

        @block.vector
        def _(dve):
            n = [0]

            def link(ins):
                n[0] += 1
                ins.then_inc(s_chain, 1)
                dve.wait_ge(s_chain, n[0])

            dve.wait_ge(s_counts, 1)
            link(dve.tensor_scalar(counts[:], counts_ps[:, 0:E], float(P - 1), None, ALU.add))
            link(dve.tensor_scalar(tiles_i[:], counts[:], 7, None, ALU.logical_shift_right))
            link(dve.tensor_copy(tiles[:], tiles_i[:]))
            dve.wait_ge(s_iota, 1)
            link(dve.tensor_copy(tile_no[:], tile_i[:]))
            link(dve.tensor_copy(within[:], tile_i[:]))
            link(dve.memset(expert[:], 0.0))
            link(dve.memset(base[:], 0.0))
            for e in range(1, E):
                link(dve.tensor_tensor(base[:, e:e + 1], base[:, e - 1:e], tiles[:, e - 1:e], ALU.add))
                link(dve.tensor_scalar(entered[:], tile_no[:], base[:, e:e + 1], None, ALU.is_ge))
                link(dve.tensor_tensor(expert[:], expert[:], entered[:], ALU.add))
                link(dve.tensor_scalar(entered[:], entered[:], tiles[:, e - 1:e], None, ALU.mult))
                link(dve.tensor_tensor(within[:], within[:], entered[:], ALU.subtract))
            link(dve.tensor_scalar(first[:], within[:], float(P), None, ALU.mult))
            link(dve.scalar_tensor_tensor(first[:], expert[:], float(NODES_PAD), first[:], ALU.mult, ALU.add))
            link(dve.tensor_copy(t["tile_slot"][:], first[0:1, :]))
            link(dve.tensor_copy(t["tile_expert"][:], expert[0:1, :]))


TABLES = 12
ROWS_HELD = 6
GATHER_AHEAD = 4
TABLE_AHEAD = 6
FFN_ROUNDS = FFN_TILES // TABLES
assert FFN_ROUNDS * TABLES == FFN_TILES


def run_experts(nc, d, t):
    with phase(nc, "ffn") as (sb, ps, sem, ctx):
        E = EXPERTS
        w1 = sb("w1", [P, E * CG * HIDDEN], F32)
        w2 = sb("w2", [P, E * HG * C], F32)
        b1 = sb("b1", [P, E * HIDDEN], F32)
        b2 = sb("b2", [P, E * C], F32)
        table = sb("table", [P, TABLES, 2], I32)
        rows = sb("rows", [P, ROWS_HELD, C], F32)
        xT = sb("xT", [P, 2, CG, P], F32)
        pre = sb("pre", [P, 2, HIDDEN], F32)
        hidden = sb("hidden", [P, 2, HIDDEN], F32)
        hT = sb("hT", [P, 2, HIDDEN], F32)
        yb = sb("yb", [P, 2, C], F32)
        result = sb("result", [P, 2, C], F32)
        primer = sb("primer", [P, 2], I32)
        ps_x = ps("ps_x", [P, 512], F32)
        ps_1 = ps("ps_1", [P, 2, 512], F32)
        ps_h = ps("ps_h", [P, 2, 512], F32)
        ps_2 = ps("ps_2", [P, 2, 512], F32)
        s_w = sem("s_w")
        s_table = [sem(f"s_table{k}") for k in range(TABLES)]
        s_rows = [sem(f"s_rows{k}") for k in range(ROWS_HELD)]
        s_xturn = sem("s_xturn")
        s_xT = sem("s_xT")
        s_one = sem("s_one")
        s_pre = sem("s_pre")
        s_hidden = sem("s_hidden")
        s_hturn = sem("s_hturn")
        s_hT = sem("s_hT")
        s_two = sem("s_two")
        s_yb = sem("s_yb")
        s_result = sem("s_result")
        s_scatter = sem("s_scatter")
        s_free = sem("s_free")
        passed = sem("passed")
        block = ctx.enter_context(nc.Block())
        F = TABLES
        W = 16 * 4

        @block.sync
        def _(sp):
            sp.dma_start(w1[:].rearrange("p (e k h) -> p e k h", e=E, k=CG),
                         d["w1"].rearrange("e (k p) h -> p e k h", p=P)).then_inc(s_w, 16)
            sp.dma_start(b1[:], d["b1"].rearrange("e h -> (e h)").partition_broadcast(P)).then_inc(s_w, 16)
            sp.dma_start(w2[:].rearrange("p (e k c) -> p e k c", e=E, k=HG),
                         d["w2"].rearrange("e (k p) c -> p e k c", p=P)).then_inc(s_w, 16)
            sp.dma_start(b2[:], d["b2"].rearrange("e c -> (e c)").partition_broadcast(P)).then_inc(s_w, 16)

            def load(tile, k):
                first = sp.value_load(t["tile_slot"][0:1, bass.ds(tile, 1)], min_val=0, max_val=TABLE_ROWS - P)
                sp.dma_start(table[:, k, :], d["table"][bass.ds(first, P), :]).then_inc(s_table[k], 16)

            for k in range(TABLE_AHEAD):
                load(k, k)
            with sp.Fori(0, FFN_ROUNDS) as i:
                for k in range(F):
                    s = i * F + k
                    gate(sp, s_free, s + TABLE_AHEAD + 2, passed)
                    load(s + TABLE_AHEAD, (k + TABLE_AHEAD) % F)
            for k in range(F):
                sp.wait_ge(s_table[k], 16 * (FFN_ROUNDS + (1 if k < TABLE_AHEAD else 0)))

        @block.gpsimd
        def _(pool):
            def gather(k, round_, row_slot):
                gate(pool, s_table[k], round_ * 16 + 16, passed)
                pool.indirect_dma_start(rows[:, row_slot, :], None, d["tokens"],
                                        bass.IndirectOffsetOnAxis(ap=table[:, k, 0:1], axis=0)
                                        ).then_inc(s_rows[row_slot], 16)

            pool.dma_start(primer[:], d["src"][0:P, 0:2]).then_inc(s_scatter, 16)
            pool.sem_inc(s_free, TABLES)
            for k in range(GATHER_AHEAD):
                gather(k, 0, k)
            with pool.Fori(0, FFN_ROUNDS) as i:
                for k in range(F):
                    s = i * F + k
                    ahead = k + GATHER_AHEAD
                    gate(pool, s_xturn, s + GATHER_AHEAD + 1, passed)
                    gather(ahead % F, i + ahead // F, ahead % ROWS_HELD)
                    gate(pool, s_scatter, (s + 1) * 16, s_free)
                    gate(pool, s_result, 2 + s + 1, passed)
                    pool.indirect_dma_start(d["out"], bass.IndirectOffsetOnAxis(ap=table[:, k, 0:1], axis=0),
                                            result[:, k % 2, :], None, compute_op=ALU.add).then_inc(s_scatter, 16)
            pool.wait_ge(s_scatter, 16 * (1 + FFN_TILES))
            for k in range(ROWS_HELD):
                pool.wait_ge(s_rows[k], 16 * (2 * FFN_ROUNDS + (1 if k < GATHER_AHEAD else 0)))

        @block.tensor
        def _(pe):
            def turn_rows(s, k, round_):
                pe.wait_ge(s_rows[k % ROWS_HELD], round_ * 16 + 16)
                if not isinstance(s, int) or s > 0:
                    pe.wait_ge(s_xT, s * CG)
                for g in range(CG):
                    last = pe.transpose(ps_x[:, g * P:(g + 1) * P], rows[:, k % ROWS_HELD, g * P:(g + 1) * P],
                                        t["ident"][:])
                last.then_inc(s_xturn, 1)

            def first_product(s, q):
                e = pe.value_load(t["tile_expert"][0:1, bass.ds(s, 1)], min_val=0, max_val=E - 1)
                pe.wait_ge(s_xT, (s + 1) * CG)
                pe.wait_ge(s_pre, s + 1)
                for g in range(CG):
                    last = pe.matmul(ps_1[:, q, :], xT[:, q, g, :],
                                     w1[:, bass.ds(e * (CG * HIDDEN) + g * HIDDEN, HIDDEN)],
                                     start=(g == 0), stop=(g == CG - 1))
                last.then_inc(s_one, 1)

            def turn_hidden(s, q):
                pe.wait_ge(s_hidden, 2 + s + 1)
                for g in range(HG):
                    last = pe.transpose(ps_h[:, q, g * P:(g + 1) * P], hidden[:, q, g * P:(g + 1) * P], t["ident"][:])
                last.then_inc(s_hturn, 1)

            def second_product(s, q):
                e = pe.value_load(t["tile_expert"][0:1, bass.ds(s, 1)], min_val=0, max_val=E - 1)
                pe.wait_ge(s_hT, s + 1)
                pe.wait_ge(s_yb, s + 1)
                for g in range(HG):
                    last = pe.matmul(ps_2[:, q, 0:C], hT[:, q, g * P:(g + 1) * P],
                                     w2[:, bass.ds(e * (HG * C) + g * C, C)], start=(g == 0), stop=(g == HG - 1))
                last.then_inc(s_two, 1)

            pe.wait_ge(s_w, W)
            pe.sem_inc(s_xturn, ROWS_HELD)
            pe.sem_inc(s_one, 2)
            pe.sem_inc(s_two, 2)
            turn_rows(0, 0, 0)
            turn_rows(1, 1, 0)
            first_product(0, 0)
            with pe.Fori(0, FFN_ROUNDS) as i:
                for k in range(F):
                    s = i * F + k
                    turn_hidden(s, k % 2)
                    first_product(s + 1, (k + 1) % 2)
                    turn_rows(s + 2, k + 2, i * 2 + (k + 2) // ROWS_HELD)
                    second_product(s, k % 2)

        @block.scalar
        def _(act):
            act.wait_ge(s_w, W)
            act.sem_inc(s_hidden, 2)
            act.sem_inc(s_result, 2)
            act.preload_act_table(ACT.Gelu)

            def scale_rows(s, q):
                gate(act, s_xturn, ROWS_HELD + s + 1, passed)
                gate(act, s_one, s + 1, passed)
                for g in range(CG):
                    act.activation(xT[:, q, g, :], ps_x[:, g * P:(g + 1) * P], ACT.Identity,
                                   bias=t["beta"][:, g:g + 1], scale=t["gamma"][:, g:g + 1]).then_inc(s_xT, 1)

            def activate(s, q):
                gate(act, s_pre, 2 + s + 1, passed)
                act.activation(hidden[:, q, :], pre[:, q, :], ACT.Gelu).then_inc(s_hidden, 1)

            scale_rows(0, 0)
            scale_rows(1, 1)
            activate(0, 0)
            with act.Fori(0, FFN_ROUNDS) as i:
                for k in range(F):
                    s = i * F + k
                    q = k % 2
                    gate(act, s_hturn, s + 1, passed)
                    gate(act, s_two, s + 1, passed)
                    act.activation(hT[:, q, :], ps_h[:, q, :], ACT.Copy).then_inc(s_hT, 1)
                    scale_rows(s + 2, q)
                    activate(s + 1, 1 - q)
                    gate(act, s_yb, 2 + s + 1, passed)
                    gate(act, s_free, s + TABLES, passed)
                    act.activation(result[:, q, :], yb[:, q, :], ACT.Copy,
                                   scale=table[:, k, 1:2].bitcast(F32)).then_inc(s_result, 1)

        @block.vector
        def _(dve):
            dve.wait_ge(s_w, W)
            dve.sem_inc(s_pre, 2)
            dve.sem_inc(s_yb, 2)

            def bias_one(s, q):
                e = dve.value_load(t["tile_expert"][0:1, bass.ds(s, 1)], min_val=0, max_val=E - 1)
                gate(dve, s_one, 2 + s + 1, passed)
                gate(dve, s_hidden, s + 1, passed)
                dve.tensor_tensor(pre[:, q, :], ps_1[:, q, :], b1[:, bass.ds(e * HIDDEN, HIDDEN)],
                                  ALU.add).then_inc(s_pre, 1)

            bias_one(0, 0)
            with dve.Fori(0, FFN_ROUNDS) as i:
                for k in range(F):
                    s = i * F + k
                    q = k % 2
                    bias_one(s + 1, (k + 1) % 2)
                    e = dve.value_load(t["tile_expert"][0:1, bass.ds(s, 1)], min_val=0, max_val=E - 1)
                    gate(dve, s_two, 2 + s + 1, passed)
                    gate(dve, s_result, s + 1, passed)
                    dve.tensor_tensor(yb[:, q, :], ps_2[:, q, 0:C], b2[:, bass.ds(e * C, C)],
                                      ALU.add).then_inc(s_yb, 1)


def kernel_program(nc, d):
    with ExitStack() as ctx:
        sb = lambda n, s, dt: ctx.enter_context(nc.sbuf_tensor(n, s, dt))
        t = {
            "ident": sb("ident", [P, P], F32),
            "ones": sb("ones", [P, P], F32),
            "before": sb("before", [P, P], F32),
            "minus_half": sb("minus_half", [P, 1], F32),
            "zeros": sb("zeros", [P, C], F32),
            "iota_i": sb("iota_i", [P, P], I32),
            "iota": sb("iota", [P, P], F32),
            "bn_scale": sb("bn_scale", [P, CG], F32),
            "bn_shift": sb("bn_shift", [P, CG], F32),
            "gamma": sb("gamma", [P, CG], F32),
            "beta": sb("beta", [P, CG], F32),
            "chosen_by": sb("chosen_by", [P, EXPERTS], F32),
            "tile_slot": sb("tile_slot", [1, FFN_LIST], I32),
            "tile_expert": sb("tile_expert", [1, FFN_LIST], I32),
            "node_mean": sb("node_mean", [P, 2, 2], F32),
            "node_stats": sb("node_stats", [P, NODE_TILES * 2], F32),
        }
        with ExitStack() as edges:
            for name, dt in (("edge_src", I32), ("edge_dst", F32), ("edge_w", F32)):
                t[name] = edges.enter_context(nc.sbuf_tensor(name, [P, EDGE_ROWS], dt))
            t["step_nodes"] = edges.enter_context(nc.sbuf_tensor("step_nodes", [1, EDGE_ROWS], I32))
            with nc.sbuf_tensor("pad_slots", [P, TABLE_ROWS // P, 2], I32) as pad:
                t["pad_slots"] = pad
                plan_steps(nc, d, t)
            project_input(nc, d, t)
            t["sums"] = edges.enter_context(nc.sbuf_tensor("sums", [P, CG, NODES_PAD], F32))
            sum_messages(nc, d, t, d["h"], "c1")
            normalize_sums(nc, d, t, "c1")
            project_hidden(nc, d, t)
            sum_messages(nc, d, t, d["h2"], "c2")
            normalize_sums(nc, d, t, "c2")
            route_tokens(nc, d, t)
        list_tiles(nc, d, t)
        run_experts(nc, d, t)


INPUTS = {
    "x": "x", "src": "src", "dst": "dst", "ew": "edge_weight",
    "c1_w1": "L0_gnn_c1_w1", "c1_b1": "L0_gnn_c1_b1", "c1_w2": "L0_gnn_c1_w2", "c1_b2": "L0_gnn_c1_b2",
    "c1_g": "L0_gnn_c1_g", "c1_b": "L0_gnn_c1_b", "bn1_g": "L0_gnn_bn1_g", "bn1_b": "L0_gnn_bn1_b",
    "c2_w1": "L0_gnn_c2_w1", "c2_b1": "L0_gnn_c2_b1", "c2_w2": "L0_gnn_c2_w2", "c2_b2": "L0_gnn_c2_b2",
    "c2_g": "L0_gnn_c2_g", "c2_b": "L0_gnn_c2_b", "bn2_g": "L0_gnn_bn2_g", "bn2_b": "L0_gnn_bn2_b",
    "gamma": "L0_ffn_gamma", "beta": "L0_ffn_beta", "wr": "L0_ffn_Wr", "br": "L0_ffn_br",
    "w1": "L0_ffn_W1", "b1": "L0_ffn_b1", "w2": "L0_ffn_W2", "b2": "L0_ffn_b2",
}


def kernel(**inputs):
    import numpy as np
    import concourse.bacc as bacc
    from concourse.bass_utils import run_bass_kernel_spmd

    nc = bacc.Bacc("TRN2", target_bir_lowering=False, num_devices=1)
    arrays, d = {}, {}
    pad_edges = EDGE_ROWS * P - EDGES
    for name, key in INPUTS.items():
        a = np.asarray(inputs[key])
        if name == "x":
            a = np.concatenate([a, np.zeros((NODES_PAD - NODES, C), a.dtype)])
        if name in ("src", "ew"):
            a = np.concatenate([a, np.zeros(pad_edges, a.dtype)]).reshape(EDGE_ROWS, P)
        if name == "dst":
            a = np.concatenate([a, np.full(pad_edges, NODES_PAD - 1, a.dtype)]).reshape(EDGE_ROWS, P)
        a = np.ascontiguousarray(a)
        arrays[f"in_{name}"] = a
        d[name] = nc.dram_tensor(f"in_{name}", a.shape, mybir.dt.from_np(a.dtype), kind="ExternalInput").ap()
    scratch = {
        "h": ((NODES_PAD, C), F32), "h2": ((NODES_PAD, C), F32), "step_list": ((EDGE_ROWS,), I32),
        "table": ((TABLE_ROWS, 2), I32), "tokens": ((OUT_ROWS, C), F32),
    }
    for name, (shape, dt) in scratch.items():
        d[name] = nc.dram_tensor(name, shape, dt, kind="Internal").ap()
    d["out"] = nc.dram_tensor("out", (OUT_ROWS, C), F32, kind="ExternalOutput").ap()
    kernel_program(nc, d)
    r = run_bass_kernel_spmd(nc, [arrays], core_ids=[0])
    return r.results[0]["out"][:NODES]
```

```python
from contextlib import ExitStack, contextmanager

import concourse.bass as bass
from concourse import mybir

ALU = mybir.AluOpType
ACT = mybir.ActivationFunctionType
F32 = mybir.dt.float32
BF16 = mybir.dt.bfloat16
I32 = mybir.dt.int32
U32 = mybir.dt.uint32

P = 128
EPS = 1e-5
NODES = 12500
C = 256
CG = C // P
NODE_TILES = -(-NODES // P)
NODES_PAD = NODE_TILES * P
EDGES = 200000
EDGE_TILES = -(-EDGES // P)
STEPS = EDGE_TILES + NODE_TILES - 1
STEP_CHUNKS = -(-STEPS // P)
EDGE_ROWS = STEP_CHUNKS * P

RING = 20
HALF = RING // 2
SUM_BANKS = 4
LEAD = 4
ROUNDS = STEPS // RING
assert ROUNDS * RING == STEPS and RING % SUM_BANKS == 0 and RING % LEAD == 0

COLS = 512
CHUNKS = NODES // COLS
REST = NODES - CHUNKS * COLS

GROUP = 7
GROUPS = NODE_TILES // GROUP
assert GROUPS * GROUP == NODE_TILES and GROUPS % 2 == 0

EXPERTS = 8
HIDDEN = 512
HG = HIDDEN // P
PAIRS = 2 * NODES_PAD
FFN_TILES = PAIRS // P + EXPERTS
FFN_UNROLL = 4
assert FFN_TILES % FFN_UNROLL == 0
FFN_LIST = FFN_TILES + 8
TABLE_TILES = EXPERTS * NODE_TILES + 16
TABLE_ROWS = TABLE_TILES * P
OUT_ROWS = NODES_PAD + P


def gate(eng, sem, value, passed):
    eng.wait_ge(sem, value)
    eng.sem_inc(passed, 1)


@contextmanager
def phase(nc, name):
    held = []

    def semaphore(n):
        held.append(nc.alloc_semaphore(name=f"{name}_{n}"))
        return held[-1]

    with ExitStack() as ctx:
        yield (lambda n, shape, dt: ctx.enter_context(nc.sbuf_tensor(f"{name}_{n}", shape, dt)),
               lambda n, shape, dt: ctx.enter_context(nc.psum_tensor(f"{name}_{n}", shape, dt)),
               semaphore, ctx)
    nc.clear_and_free_semaphores(held)
    nc.all_engine_barrier()


def plan_steps(nc, d, t):
    with phase(nc, "pl") as (sb, ps, sem, ctx):
        K = STEP_CHUNKS
        last_dst = sb("last_dst", [P, K], I32)
        block_of_last = sb("block_of_last", [P, K], I32)
        tile_no_i = sb("tile_no_i", [P, K], I32)
        tile_no = sb("tile_no", [P, K], F32)
        entry = sb("entry", [P, K], F32)
        step_row_i = sb("step_row_i", [P, K * P], I32)
        step_row = sb("step_row", [P, K * P], F32)
        entered = sb("entered", [P, K, K * P], BF16)
        ones_bf = sb("ones_bf", [P, 1], BF16)
        step_tile = sb("step_tile", [P, K], F32)
        step_tile_i = sb("step_tile_i", [P, K], I32)
        step_no = sb("step_no", [P, K], F32)
        step_node = sb("step_node", [P, K], F32)
        step_node_i = sb("step_node_i", [P, K], I32)
        g_src = sb("g_src", [P, K, P], I32)
        g_dst = sb("g_dst", [P, K, P], I32)
        g_ew = sb("g_ew", [P, K, P], F32)
        f_src = sb("f_src", [P, K, P], F32)
        f_dst = sb("f_dst", [P, K, P], F32)
        count = ps("count", [P, 512], F32)
        turned = ps("turned", [P, 4, 512], F32)

        s_in = sem("in")
        s_iota = sem("iota")
        s_chain = sem("chain")
        s_entered = sem("entered")
        s_count = sem("count")
        s_tile = sem("tile")
        s_node = sem("node")
        s_list = sem("list")
        s_row = sem("row")
        s_rows = [sem(f"rows{a}") for a in range(3)]
        s_float = [sem(f"float{a}") for a in range(2)]
        s_turned = sem("turned")
        s_out = sem("out")
        s_ident = sem("ident")
        s_pad = sem("pad")
        s_mask = sem("mask")
        s_table = sem("table")
        s_columns = sem("columns")

        groups = [(a, c, min(c + 4, K)) for a in range(3) for c in range(0, K, 4)]
        block = ctx.enter_context(nc.Block())

        @block.sync
        def _(sp):
            with nc.allow_non_contiguous_dma(reason="one word of each row, 1664 in all"):
                sp.dma_start(last_dst[:], d["dst"].rearrange("(c p) e -> p c e", p=P)[:, :, P - 1]).then_inc(s_in, 16)
            with nc.allow_non_contiguous_dma(reason="256 words, one for each channel"):
                sp.dma_start(t["gamma"][:], d["gamma"].rearrange("(k p) -> p k", p=P)).then_inc(s_columns, 16)
                sp.dma_start(t["beta"][:], d["beta"].rearrange("(k p) -> p k", p=P)).then_inc(s_columns, 16)
            sp.wait_ge(s_node, 1)
            with nc.allow_non_contiguous_dma(reason="1664 words"):
                sp.dma_start(d["step_list"].rearrange("(c p) -> p c", p=P), step_node_i[:]).then_inc(s_list, 16)
            sp.wait_ge(s_list, 16)
            sp.dma_start(t["step_nodes"][0:1, :], d["step_list"].rearrange("(a n) -> a n", a=1)).then_inc(s_row, 16)
            sp.wait_ge(s_mask, 2)
            sp.dma_start(d["table"].rearrange("(p b) w -> p b w", p=P), t["pad_slots"][:]).then_inc(s_table, 16)
            sp.wait_ge(s_pad, 1)
            sp.dma_start(d["tokens"][NODES_PAD:OUT_ROWS, :], t["zeros"][:]).then_inc(s_table, 16)
            sp.dma_start(d["out"][NODES_PAD:OUT_ROWS, :], t["zeros"][:]).then_inc(s_table, 16)
            sp.wait_ge(s_row, 16)
            sp.wait_ge(s_table, 48)
            sp.wait_ge(s_columns, 32)

        @block.gpsimd
        def _(pool):
            pool.iota(tile_no_i[:], [[P, K]], base=1, channel_multiplier=1).then_inc(s_iota, 1)
            pool.iota(step_row_i[:], [[1, K * P]], base=0, channel_multiplier=0).then_inc(s_iota, 1)
            pool.memset(t["ident"][:], 0.0).then_inc(s_ident, 1)
            pool.wait_ge(s_ident, 1)
            pool.affine_select(out=t["ident"][:], in_=t["ident"][:], compare_op=ALU.not_equal, fill=1.0, base=0,
                               pattern=[[-1, P]], channel_multiplier=1).then_inc(s_ident, 1)
            pool.iota(t["pad_slots"][:, :, 0], [[1, TABLE_ROWS // P]], base=0,
                      channel_multiplier=TABLE_ROWS // P).then_inc(s_iota, 1)
            pool.memset(t["pad_slots"][:, :, 1], 0).then_inc(s_iota, 1)
            pool.iota(t["iota_i"][:], [[1, P]], base=0, channel_multiplier=0).then_inc(s_iota, 1)
            pool.memset(t["zeros"][:], 0.0).then_inc(s_pad, 1)
            pool.memset(t["minus_half"][:], -0.5)
            pool.memset(t["ones"][:], 1.0).then_inc(s_pad, 1)
            pool.wait_ge(s_pad, 2)
            pool.affine_select(out=t["before"][:], in_=t["ones"][:], compare_op=ALU.is_gt, fill=0.0, base=0,
                               pattern=[[1, P]], channel_multiplier=-1).then_inc(s_pad, 1)
            pool.wait_ge(s_tile, 2)
            for c in range(K):
                for a, (rows, dest) in enumerate(((d["src"], g_src), (d["dst"], g_dst), (d["ew"], g_ew))):
                    pool.indirect_dma_start(dest[:, c, :], None, rows,
                                            bass.IndirectOffsetOnAxis(ap=step_tile_i[:, c:c + 1], axis=0)
                                            ).then_inc(s_rows[a], 16)

        @block.vector
        def _(dve):
            n = [0]

            def link(ins):
                n[0] += 1
                ins.then_inc(s_chain, 1)
                dve.wait_ge(s_chain, n[0])

            dve.memset(ones_bf[:], 1.0).then_inc(s_entered, 1)
            dve.wait_ge(s_in, 16)
            link(dve.tensor_scalar(block_of_last[:], last_dst[:], 7, None, ALU.logical_shift_right))
            dve.wait_ge(s_iota, 5)
            link(dve.tensor_copy(tile_no[:], tile_no_i[:]))
            dve.tensor_copy(step_row[:], step_row_i[:]).then_inc(s_chain, 1)
            n[0] += 1
            link(dve.tensor_tensor(entry[:], block_of_last[:], tile_no[:], ALU.add))
            for c in range(K):
                dve.tensor_scalar(entered[:, c, :], step_row[:], entry[:, c:c + 1], None,
                                  ALU.is_ge).then_inc(s_entered, 1)
            dve.tensor_copy(t["iota"][:], t["iota_i"][:]).then_inc(s_mask, 1)
            dve.tensor_scalar(t["pad_slots"][:, :, 0], t["pad_slots"][:, :, 0], P - 1, NODES_PAD,
                              ALU.bitwise_and, ALU.bitwise_or).then_inc(s_mask, 1)
            link(dve.tensor_scalar(step_no[:], tile_no[:], -1.0, None, ALU.add))
            dve.wait_ge(s_count, 1)
            dve.tensor_copy(step_tile[:], count[:, 0:K]).then_inc(s_tile, 1)
            dve.tensor_copy(step_tile_i[:], count[:, 0:K]).then_inc(s_tile, 1)
            dve.wait_ge(s_tile, 2)
            link(dve.tensor_tensor(step_node[:], step_no[:], step_tile[:], ALU.subtract))
            link(dve.tensor_scalar(step_node[:], step_node[:], float(P), None, ALU.mult))
            dve.tensor_copy(step_node_i[:], step_node[:]).then_inc(s_node, 1)
            dve.wait_ge(s_rows[0], 16 * K)
            dve.tensor_copy(f_src[:], g_src[:]).then_inc(s_float[0], 1)
            dve.wait_ge(s_rows[1], 16 * K)
            for c in range(K):
                dve.tensor_scalar(f_dst[:, c, :], g_dst[:, c, :], step_node[:, c:c + 1], None,
                                  ALU.subtract).then_inc(s_float[1], 1)
            for g, (a, c0, c1) in enumerate(groups):
                dve.wait_ge(s_turned, g + 1)
                dest = (t["edge_src"], t["edge_dst"], t["edge_w"])[a]
                dve.tensor_copy(dest[:, c0 * P:c1 * P], turned[:, g % 4, 0:(c1 - c0) * P]).then_inc(s_out, 1)

        @block.tensor
        def _(pe):
            pe.wait_ge(s_entered, 1 + K)
            for c in range(K):
                for k in range(K):
                    last = pe.matmul(count[:, c:c + 1], entered[:, k, c * P:(c + 1) * P], ones_bf[:],
                                     start=(k == 0), stop=(k == K - 1))
            last.then_inc(s_count, 1)
            pe.wait_ge(s_ident, 2)
            for g, (a, c0, c1) in enumerate(groups):
                if g == 0:
                    pe.wait_ge(s_float[0], 1)
                if c0 == 0 and a == 1:
                    pe.wait_ge(s_float[1], K)
                if c0 == 0 and a == 2:
                    pe.wait_ge(s_rows[2], 16 * K)
                if g >= 4:
                    pe.wait_ge(s_out, g - 3)
                rows = (f_src, f_dst, g_ew)[a]
                for c in range(c0, c1):
                    last = pe.transpose(turned[:, g % 4, (c - c0) * P:(c - c0 + 1) * P], rows[:, c, :], t["ident"][:])
                last.then_inc(s_turned, 1)


def project_input(nc, d, t):
    with phase(nc, "pi") as (sb, ps, sem, ctx):
        G = GROUP
        x = sb("x", [P, 2, G, C], F32)
        stats = sb("stats", [P, G, 6], F32)
        moments = sb("moments", [P, G, 2], F32)
        xn = sb("xn", [P, 2, G, C], F32)
        xnT = sb("xnT", [P, G, C], F32)
        biased = sb("biased", [P, 2, G, C], F32)
        h = sb("h", [P, 2, G, C], F32)
        w1 = sb("w1", [P, CG, C], F32)
        b1 = sb("b1", [P, C], F32)
        minus_half = sb("minus_half", [P, G], F32)
        turned = ps("turned", [P, 3, 512], F32)
        product = ps("product", [P, 4, 512], F32)
        s_w = sem("s_w")
        s_x = [sem("s_x0"), sem("s_x1")]
        s_stat = sem("s_stat")
        s_aggr = sem("s_aggr")
        s_var = sem("s_var")
        s_rstd = sem("s_rstd")
        s_kept = sem("s_kept")
        s_xn = sem("s_xn")
        s_turned = sem("s_turned")
        s_xnT = sem("s_xnT")
        s_product = sem("s_product")
        s_biased = sem("s_biased")
        s_h = sem("s_h")
        s_stored = [sem("s_stored0"), sem("s_stored1")]
        s_half = sem("s_half")
        passed = sem("passed")
        x_view = d["x"].rearrange("(n p) c -> p n c", p=P)
        h_view = d["h"].rearrange("(n p) c -> p n c", p=P)
        block = ctx.enter_context(nc.Block())

        @block.sync
        def _(sp):
            sp.dma_start(w1[:], d["c1_w1"].rearrange("(k p) c -> p k c", p=P)).then_inc(s_w, 16)
            sp.dma_start(b1[:], d["c1_b1"].partition_broadcast(P)).then_inc(s_w, 16)
            sp.sem_inc(s_xn, 2 * G)
            with sp.Fori(0, GROUPS // 2) as i:
                for u in range(2):
                    sp.wait_ge(s_xn, (i * 2 + u + 1) * G)
                    sp.dma_start(x[:, u, :, :], x_view[:, bass.ds((i * 2 + u) * G, G), :]).then_inc(s_x[u], 16)
            sp.wait_ge(s_w, 32)

        @block.vector
        def _(dve):
            dve.wait_ge(s_w, 32)
            dve.sem_inc(s_biased, 4)

            def normalize(i, g, u):
                gate(dve, s_x[u], i * 16 + 16, passed)
                for j in range(G):
                    dve.bn_stats(stats[:, j, :], x[:, u, j, :]).then_inc(s_stat, 1)
                for j in range(G):
                    gate(dve, s_stat, g * G + j + 1, passed)
                    dve.bn_aggr(moments[:, j, :], stats[:, j, :]).then_inc(s_aggr, 1)
                gate(dve, s_aggr, (g + 1) * G, passed)
                dve.tensor_scalar(moments[:, :, 1], moments[:, :, 1], EPS, None, ALU.add).then_inc(s_var, 1)

            def scale(i, g, u):
                gate(dve, s_rstd, g + 1, passed)
                dve.tensor_copy(t["node_stats"][:, bass.ds(g * (2 * G), 2 * G)],
                                moments[:].rearrange("p g s -> p (g s)")).then_inc(s_kept, 1)
                for j in range(G):
                    dve.tensor_scalar(xn[:, u, j, :], x[:, u, j, :], moments[:, j, 0:1], moments[:, j, 1:2],
                                      ALU.subtract, ALU.mult).then_inc(s_xn, 1)
                gate(dve, s_kept, g + 1, passed)
                gate(dve, s_xn, (g + 3) * G, passed)

            def bias(g, u):
                for j in range(G):
                    n = g * G + j
                    dve.wait_ge(s_product, G + n + 1)
                    dve.wait_ge(s_h, n + 1)
                    dve.tensor_tensor(biased[:, u, j, :], product[:, j % 4, 0:C], b1[:], ALU.add).then_inc(s_biased, 1)

            normalize(0, 0, 0)
            scale(0, 0, 0)
            with dve.Fori(0, GROUPS // 2 - 1) as i:
                normalize(i, i * 2 + 1, 1)
                bias(i * 2, 0)
                scale(i, i * 2 + 1, 1)
                normalize(i + 1, i * 2 + 2, 0)
                bias(i * 2 + 1, 1)
                scale(i + 1, i * 2 + 2, 0)
            normalize(GROUPS // 2 - 1, GROUPS - 1, 1)
            bias(GROUPS - 2, 0)
            scale(GROUPS // 2 - 1, GROUPS - 1, 1)
            bias(GROUPS - 1, 1)

        @block.gpsimd
        def _(pool):
            pool.memset(minus_half[:], -0.5).then_inc(s_half, 1)
            pool.wait_ge(s_half, 1)
            with pool.Fori(0, GROUPS) as g:
                gate(pool, s_var, g + 1, passed)
                pool.tensor_tensor(moments[:, :, 1], moments[:, :, 1], minus_half[:], ALU.pow).then_inc(s_rstd, 1)

        @block.tensor
        def _(pe):
            pe.wait_ge(s_w, 32)
            pe.sem_inc(s_product, G)

            def multiply(g, u, j):
                n = g * G + j
                pe.wait_ge(s_xnT, 3 + n + 1)
                pe.wait_ge(s_biased, bank_free(g, j))
                for k in range(CG):
                    last = pe.matmul(product[:, j % 4, 0:C], xnT[:, j, k * P:(k + 1) * P], w1[:, k, :],
                                     start=(k == 0), stop=(k == CG - 1))
                last.then_inc(s_product, 1)

            def bank_free(g, j):
                return 4 + g * G + (j - 3 if j > 3 else 0)

            with pe.Fori(0, GROUPS // 2) as i:
                for u in range(2):
                    g = i * 2 + u
                    for j in range(G):
                        n = g * G + j
                        pe.wait_ge(s_xn, 2 * G + n + 1)
                        pe.wait_ge(s_xnT, 3 + g * G + (j - 2 if j > 2 else 0))
                        for k in range(CG):
                            last = pe.transpose(turned[:, j % 3, k * P:(k + 1) * P], xn[:, u, j, k * P:(k + 1) * P],
                                                t["ident"][:])
                        last.then_inc(s_turned, 1)
                        if j > 0:
                            multiply(g, u, j - 1)
                    multiply(g, u, G - 1)

        @block.scalar
        def _(act):
            act.preload_act_table(ACT.Relu)
            act.sem_inc(s_xnT, 3)
            act.sem_inc(s_h, 2 * G)
            for u in range(2):
                act.sem_inc(s_stored[u], 16)

            def relu(i, g, u, j):
                n = g * G + j
                act.wait_ge(s_biased, 4 + n + 1)
                act.activation(h[:, u, j, :], biased[:, u, j, :], ACT.Relu).then_inc(s_h, 1)

            def copy_out(g, j):
                n = g * G + j
                act.wait_ge(s_turned, n + 1)
                act.wait_ge(s_product, n + 1)
                act.activation(xnT[:, j, :], turned[:, j % 3, 0:C], ACT.Copy).then_inc(s_xnT, 1)

            def store(g, u):
                act.wait_ge(s_h, (g + 3) * G)
                act.dma_start(h_view[:, bass.ds(g * G, G), :], h[:, u, :, :]).then_inc(s_stored[u], 16)

            def group(i, g, u, former):
                for j in range(G):
                    copy_out(g, j)
                if former is not None:
                    gate(act, s_stored[1 - u], former * 16 + 16, passed)
                    for j in range(G):
                        relu(i, g - 1, 1 - u, j)
                    store(g - 1, 1 - u)

            group(0, 0, 0, None)
            with act.Fori(0, GROUPS // 2 - 1) as i:
                group(i, i * 2 + 1, 1, i)
                group(i, i * 2 + 2, 0, i)
            group(0, GROUPS - 1, 1, GROUPS // 2 - 1)
            gate(act, s_stored[1], (GROUPS // 2 - 1) * 16 + 16, passed)
            for j in range(G):
                relu(0, GROUPS - 1, 1, j)
            store(GROUPS - 1, 1)
            for u in range(2):
                act.wait_ge(s_stored[u], 16 * (GROUPS // 2 + 1))


def sum_messages(nc, d, t, source, layer):
    with phase(nc, layer) as (sb, ps, sem, ctx):
        messages = sb("messages", [P, RING, C], F32)
        indices = sb("indices", [P, 2, HALF], I32)
        onehot = sb("onehot", [P, LEAD, P], F32)
        partial = ps("partial", [P, SUM_BANKS, 512], F32)
        s_message = [sem(f"s_message{k}") for k in range(RING)]
        s_index = sem("s_index")
        s_onehot = sem("s_onehot")
        s_multiplied = sem("s_multiplied")
        s_added = sem("s_added")
        s_zero = sem("s_zero")
        passed = sem("passed")
        sums = t["sums"]
        block = ctx.enter_context(nc.Block())

        @block.scalar
        def _(act):
            with act.Fori(0, ROUNDS) as i:
                for half in range(2):
                    first = i * RING + half * HALF
                    gate(act, s_multiplied, first + HALF, passed)
                    act.activation(indices[:, half, :], t["edge_src"][:, bass.ds(first, HALF)],
                                   ACT.Copy).then_inc(s_index, 1)

        @block.gpsimd
        def _(pool):
            with pool.Fori(0, ROUNDS) as i:
                for k in range(RING):
                    if k % HALF == 0:
                        gate(pool, s_index, i * 2 + k // HALF + 1, passed)
                    pool.indirect_dma_start(messages[:, k, :], None, source,
                                            bass.IndirectOffsetOnAxis(ap=indices[:, k // HALF, k % HALF:k % HALF + 1],
                                                                      axis=0)).then_inc(s_message[k], 16)

        @block.tensor
        def _(pe):
            pe.sem_inc(s_multiplied, RING)
            with pe.Fori(0, ROUNDS) as i:
                for k in range(RING):
                    n = i * RING + k
                    pe.wait_ge(s_onehot, n + 1)
                    pe.wait_ge(s_added, n + 1)
                    pe.wait_ge(s_message[k], i * 16 + 16)
                    for g in range(CG):
                        last = pe.matmul(partial[:, k % SUM_BANKS, g * P:(g + 1) * P],
                                         messages[:, k, g * P:(g + 1) * P], onehot[:, k % LEAD, :],
                                         start=True, stop=True)
                    last.then_inc(s_multiplied, 1)

        @block.vector
        def _(dve):
            def build(slot, step):
                return dve.tensor_scalar(onehot[:, slot, :], t["iota"][:], t["edge_dst"][:, bass.ds(step, 1)],
                                         t["edge_w"][:, bass.ds(step, 1)], ALU.is_equal, ALU.mult)

            dve.sem_inc(s_added, SUM_BANKS)
            for k in range(LEAD):
                build(k, k).then_inc(s_onehot, 1)
            dve.memset(sums[:], 0.0).then_inc(s_zero, 1)
            dve.wait_ge(s_zero, 1)
            regs = [dve.alloc_register(f"{layer}_node{k}") for k in range(4)]
            with dve.Fori(0, ROUNDS) as i:
                for k in range(RING):
                    n = i * RING + k
                    if k % 4 == 0:
                        dve.load(regs, t["step_nodes"][0:1, bass.ds(n, 4)])
                        nodes = [dve.snap(r, min_val=0, max_val=NODES_PAD - P) for r in regs]
                    where = sums[:, :, bass.ds(nodes[k % 4], P)]
                    dve.wait_ge(s_multiplied, RING + n + 1)
                    dve.wait_ge(s_added, SUM_BANKS + n)
                    dve.tensor_tensor(where, where, partial[:, k % SUM_BANKS, 0:C].rearrange("p (g n) -> p g n", g=CG),
                                      ALU.add).then_inc(s_added, 1)
                    build(k % LEAD, n + LEAD).then_inc(s_onehot, 1)


def normalize_sums(nc, d, t, layer):
    with phase(nc, layer + "_ns") as (sb, ps, sem, ctx):
        U = 2
        sums = t["sums"]
        w2 = sb("w2", [P, CG, C], F32)
        b2 = sb("b2", [P, CG], F32)
        gains = sb("gains", [P, 2, CG], F32)
        shifts = sb("shifts", [P, 2, CG], F32)
        stats = sb("stats", [P, CG, CHUNKS + 1, 6], F32)
        moments = sb("moments", [P, CG, 2], F32)
        scale = sb("scale", [P, CG], F32)
        shift = sb("shift", [P, CG], F32)
        product = sb("product", [P, CG], F32)
        z = ps("z", [P, U * CG, 512], F32)
        s_w = sem("s_w")
        s_z = sem("s_z")
        s_biased = sem("s_biased")
        s_stats = sem("s_stats")
        s_var = sem("s_var")
        s_rstd = sem("s_rstd")
        s_chain = sem("s_chain")
        s_first = sem("s_first")
        s_relu = sem("s_relu")
        passed = sem("passed")
        block = ctx.enter_context(nc.Block())

        def over_chunks(eng, body):
            with eng.Fori(0, CHUNKS // U) as i:
                for u in range(U):
                    body(i * U + u, u, (i * U + u) * COLS, COLS)
            body(CHUNKS, 0, CHUNKS * COLS, REST)

        @block.sync
        def _(sp):
            sp.dma_start(w2[:], d[layer + "_w2"].rearrange("(k p) c -> p k c", p=P)).then_inc(s_w, 16)
            with nc.allow_non_contiguous_dma(reason="256 words, one for each channel"):
                sp.dma_start(b2[:], d[layer + "_b2"].rearrange("(k p) -> p k", p=P)).then_inc(s_w, 16)
                for n, bn in enumerate((layer, {"c1": "bn1", "c2": "bn2"}[layer])):
                    sp.dma_start(gains[:, n, :], d[bn + "_g"].rearrange("(k p) -> p k", p=P)).then_inc(s_w, 16)
                    sp.dma_start(shifts[:, n, :], d[bn + "_b"].rearrange("(k p) -> p k", p=P)).then_inc(s_w, 16)
            sp.wait_ge(s_w, 96)

        @block.tensor
        def _(pe):
            pe.wait_ge(s_w, 96)

            def product_of(chunk, u, col, cols):
                pe.wait_ge(s_biased, (chunk + 1) * CG)
                for co in range(CG):
                    for k in range(CG):
                        last = pe.matmul(z[:, u * CG + co, 0:cols], w2[:, k, co * P:(co + 1) * P],
                                         sums[:, k, bass.ds(col, cols)], start=(k == 0), stop=(k == CG - 1))
                last.then_inc(s_z, 1)

            over_chunks(pe, product_of)

        @block.scalar
        def _(act):
            act.preload_act_table(ACT.Relu)
            act.sem_inc(s_biased, U * CG)
            act.wait_ge(s_w, 96)

            def add_bias(chunk, u, col, cols):
                gate(act, s_z, chunk + 1, passed)
                for co in range(CG):
                    act.activation(sums[:, co, bass.ds(col, cols)], z[:, u * CG + co, 0:cols], ACT.Identity,
                                   bias=b2[:, co:co + 1]).then_inc(s_biased, 1)

            def first_norm(chunk, u, col, cols):
                for co in range(CG):
                    v = sums[:, co, bass.ds(col, cols)]
                    act.activation(v, v, ACT.Relu, bias=shift[:, co:co + 1],
                                   scale=scale[:, co:co + 1]).then_inc(s_relu, 1)

            over_chunks(act, add_bias)
            act.wait_ge(s_first, 1)
            over_chunks(act, first_norm)

        @block.gpsimd
        def _(pool):
            for n in range(2):
                pool.wait_ge(s_var, n + 1)
                for co in range(CG):
                    pool.tensor_tensor(moments[:, co, 1:2], moments[:, co, 1:2], t["minus_half"][:],
                                       ALU.pow).then_inc(s_rstd, 1)

        @block.vector
        def _(dve):
            n = [0]

            def link(ins):
                n[0] += 1
                ins.then_inc(s_chain, 1)
                dve.wait_ge(s_chain, n[0])

            def statistics(ready, counted_from):
                def of_chunk(chunk, u, col, cols):
                    for co in range(CG):
                        gate(dve, ready, chunk * CG + (counted_from + co + 1), passed)
                        dve.bn_stats(stats[:, co, bass.ds(chunk, 1), :].rearrange("p a s -> p (a s)"),
                                     sums[:, co, bass.ds(col, cols)]).then_inc(s_stats, 1)
                return of_chunk

            def coefficients(which, to_scale, to_shift):
                dve.wait_ge(s_stats, (which + 1) * CG * (CHUNKS + 1))
                for co in range(CG):
                    link(dve.bn_aggr(moments[:, co, :], stats[:, co, :, :].rearrange("p a s -> p (a s)")))
                dve.tensor_scalar(moments[:, :, 1], moments[:, :, 1], EPS, None, ALU.add).then_inc(s_var, 1)
                dve.wait_ge(s_rstd, (which + 1) * CG)
                link(dve.tensor_tensor(to_scale, gains[:, which, :], moments[:, :, 1], ALU.mult))
                link(dve.tensor_tensor(product[:], moments[:, :, 0], to_scale, ALU.mult))
                return dve.tensor_tensor(to_shift, shifts[:, which, :], product[:], ALU.subtract)

            over_chunks(dve, statistics(s_biased, U * CG))
            dve.wait_ge(s_w, 96)
            coefficients(0, scale[:], shift[:]).then_inc(s_first, 1)
            over_chunks(dve, statistics(s_relu, 0))
            coefficients(1, t["bn_scale"][:], t["bn_shift"][:])


def project_hidden(nc, d, t):
    with phase(nc, "ph") as (sb, ps, sem, ctx):
        U = 2
        TILES = 4
        a = sb("a", [P, U, CG, COLS], F32)
        biased = sb("biased", [P, U, TILES, C], F32)
        h = sb("h", [P, U, TILES, C], F32)
        w1 = sb("w1", [P, CG, C], F32)
        b1 = sb("b1", [P, C], F32)
        product = ps("product", [P, TILES, 512], F32)
        s_w = sem("s_w")
        s_a = sem("s_a")
        s_product = sem("s_product")
        s_biased = sem("s_biased")
        s_h = sem("s_h")
        s_stored = [sem(f"s_stored{u}") for u in range(U)]
        passed = sem("passed")
        h_view = d["h2"].rearrange("(n p) c -> p n c", p=P)
        LAST = NODE_TILES - CHUNKS * TILES
        block = ctx.enter_context(nc.Block())

        def over_chunks(eng, body):
            with eng.Fori(0, CHUNKS // U) as i:
                for u in range(U):
                    body(i, i * U + u, u, TILES)
            body(CHUNKS // U, CHUNKS, 0, LAST)

        @block.sync
        def _(sp):
            sp.dma_start(w1[:], d["c2_w1"].rearrange("(k p) c -> p k c", p=P)).then_inc(s_w, 16)
            sp.dma_start(b1[:], d["c2_b1"].partition_broadcast(P)).then_inc(s_w, 16)
            for u in range(U):
                sp.sem_inc(s_stored[u], 16)

            def store(i, chunk, u, tiles):
                sp.wait_ge(s_h, (chunk + 1) * TILES if tiles == TILES else CHUNKS * TILES + LAST)
                sp.dma_start(h_view[:, bass.ds(chunk * TILES, tiles), :], h[:, u, 0:tiles, :]
                             ).then_inc(s_stored[u], 16)

            over_chunks(sp, store)
            sp.wait_ge(s_stored[0], 16 * (CHUNKS // U + 2))
            sp.wait_ge(s_stored[1], 16 * (CHUNKS // U + 1))
            sp.wait_ge(s_w, 32)

        @block.scalar
        def _(act):
            act.preload_act_table(ACT.Relu)

            def norm(i, chunk, u, tiles):
                gate(act, s_product, (chunk + 1) * TILES, passed)
                for k in range(CG):
                    act.activation(a[:, u, k, 0:tiles * P], t["sums"][:, k, bass.ds(chunk * COLS, tiles * P)],
                                   ACT.Relu, bias=t["bn_shift"][:, k:k + 1],
                                   scale=t["bn_scale"][:, k:k + 1]).then_inc(s_a, 1)

            over_chunks(act, norm)

        @block.tensor
        def _(pe):
            pe.wait_ge(s_w, 32)
            pe.sem_inc(s_product, U * TILES)

            def multiply(i, chunk, u, tiles):
                for j in range(tiles):
                    n = chunk * TILES + j
                    if j == 0:
                        pe.wait_ge(s_a, (chunk + 1) * CG)
                    pe.wait_ge(s_biased, n + 1)
                    for k in range(CG):
                        last = pe.matmul(product[:, j, 0:C], a[:, u, k, j * P:(j + 1) * P], w1[:, k, :],
                                         start=(k == 0), stop=(k == CG - 1))
                    last.then_inc(s_product, 1)

            over_chunks(pe, multiply)

        @block.vector
        def _(dve):
            dve.wait_ge(s_w, 32)
            dve.sem_inc(s_biased, TILES)

            def bias(i, chunk, u, tiles):
                for j in range(tiles):
                    n = chunk * TILES + j
                    dve.wait_ge(s_product, U * TILES + n + 1)
                    if j == 0:
                        dve.wait_ge(s_stored[u], i * 16 + 16)
                    dve.tensor_tensor(biased[:, u, j, :], product[:, j, 0:C], b1[:], ALU.add).then_inc(s_biased, 1)

            over_chunks(dve, bias)

        @block.gpsimd
        def _(pool):
            def relu(i, chunk, u, tiles):
                for j in range(tiles):
                    gate(pool, s_biased, TILES + chunk * TILES + j + 1, passed)
                    if j == 0:
                        gate(pool, s_stored[u], i * 16 + 16, passed)
                    pool.tensor_scalar(h[:, u, j, :], biased[:, u, j, :], 0.0, None, ALU.max).then_inc(s_h, 1)

            over_chunks(pool, relu)


def route_tokens(nc, d, t):
    with phase(nc, "rt") as (sb, ps, sem, ctx):
        G, E = GROUP, EXPERTS
        BANKS = (G + 1) // 2
        x = sb("x", [P, 2, G, C], F32)
        y = sb("y", [P, G, CG, P], F32)
        residual = sb("residual", [P, G, C], F32)
        x1 = sb("x1", [P, G, C], F32)
        l1 = sb("l1", [P, G, C], F32)
        tokens = sb("tokens", [P, G, C], F32)
        affine = sb("affine", [P, 2, CG, P], F32)
        stats = sb("stats", [P, G, 6], F32)
        moments = sb("moments", [P, 2, G, 2], F32)
        down = sb("down", [P, 2, G], F32)
        wr = sb("wr", [P, CG, E], F32)
        br = sb("br", [P, G, E], F32)
        minus_half = sb("minus_half", [P, G], F32)
        logits = sb("logits", [P, G, E], F32)
        top = sb("top", [P, G, E], F32)
        which = sb("which", [P, G, E], U32)
        which_f = sb("which_f", [P, G, E], F32)
        experts_i = sb("experts_i", [P, G, E], I32)
        experts = sb("experts", [P, G, E], F32)
        slots_of = sb("slots_of", [P, G, E], F32)
        chosen = sb("chosen", [P, 2, G, E], F32)
        both = sb("both", [P, G, E], F32)
        of_group = sb("of_group", [P, E], F32)
        carried = sb("carried", [P, E], F32)
        place = sb("place", [P, G, E], F32)
        picked = sb("picked", [P, 2, G, E], F32)
        slot_f = sb("slot_f", [P, 2, G], F32)
        slot = sb("slot", [P, 2, 2, G], I32)
        gap = sb("gap", [P, G], F32)
        ratio = sb("ratio", [P, G], F32)
        total = sb("total", [P, G], F32)
        token_i = sb("token_i", [P, G], I32)
        entry = sb("entry", [P, 2, 2, G, 2], I32)
        primer = sb("primer", [P, 2, 2], I32)
        ps_y = ps("ps_y", [P, BANKS, 2, C], F32)
        ps_t = ps("ps_t", [P, 2, 512], F32)
        ps_l = ps("ps_l", [P, 512], F32)
        ps_c = ps("ps_c", [P, 512], F32)

        s_w = sem("s_w")
        s_const = sem("s_const")
        s_const2 = sem("s_const2")
        s_x = [sem("s_x_in0"), sem("s_x_in1")]
        s_y = sem("s_y")
        s_turned = sem("s_turned")
        s_read = sem("s_read")
        s_res = sem("s_res")
        s_added = sem("s_added")
        s_x1 = sem("s_x1")
        s_x1_stored = sem("s_x1_stored")
        s_stat = sem("s_stat")
        s_aggr = sem("s_aggr")
        s_var = sem("s_var")
        s_rstd = sem("s_rstd")
        s_down = sem("s_down")
        s_l1 = sem("s_l1")
        s_token = sem("s_token")
        s_token_stored = sem("s_token_stored")
        s_back = sem("s_back")
        s_affine = sem("s_affine")
        s_logit = sem("s_logit")
        s_chain = sem("s_chain")
        s_gap = sem("s_gap")
        s_ratio = sem("s_ratio")
        s_both = sem("s_both")
        s_place = sem("s_place")
        s_entry = sem("s_entry")
        s_scatter = [sem("s_scatter0"), sem("s_scatter1")]
        passed = sem("passed")
        x_view = d["x"].rearrange("(n p) c -> p n c", p=P)
        out_view = d["out"].rearrange("(n p) c -> p n c", p=P)
        token_view = d["tokens"].rearrange("(n p) c -> p n c", p=P)
        block = ctx.enter_context(nc.Block())

        def over_groups(eng, body):
            for g in (0, 1):
                body(0, g, g)
            with eng.Fori(1, GROUPS // 2 - 1) as r:
                for u in range(2):
                    body(r, r * 2 + u, u)
            for g in (GROUPS - 2, GROUPS - 1):
                body(GROUPS // 2 - 1, g, g % 2)

        def is_group(g, which):
            return isinstance(g, int) and g == which

        @block.sync
        def _(sp):
            sp.dma_start(wr[:], d["wr"].rearrange("(k p) e -> p k e", p=P)).then_inc(s_w, 16)
            for g in range(G):
                sp.dma_start(br[:, g, :], d["br"].partition_broadcast(P)).then_inc(s_w, 16)
            sp.sem_inc(s_x1, 2)
            sp.sem_inc(s_x1_stored, 16)
            sp.sem_inc(s_token_stored, 16)

            def move(g, u):
                sp.wait_ge(s_x1, g + 1)
                sp.dma_start(x[:, u, :, :], x_view[:, bass.ds(g * G, G), :]).then_inc(s_x[u], 16)

            def store(g):
                sp.wait_ge(s_x1, 2 + g + 1)
                sp.dma_start(out_view[:, bass.ds(g * G, G), :], x1[:]).then_inc(s_x1_stored, 16)
                sp.wait_ge(s_token, (g + 1) * G)
                sp.dma_start(token_view[:, bass.ds(g * G, G), :], tokens[:]).then_inc(s_token_stored, 16)

            move(0, 0)
            with sp.Fori(0, GROUPS // 2 - 1) as i:
                move(i * 2 + 1, 1)
                store(i * 2)
                move(i * 2 + 2, 0)
                store(i * 2 + 1)
            move(GROUPS - 1, 1)
            store(GROUPS - 2)
            store(GROUPS - 1)
            sp.wait_ge(s_x1_stored, 16 * (GROUPS + 1))
            sp.wait_ge(s_token_stored, 16 * (GROUPS + 1))

        @block.scalar
        def _(act):
            act.wait_ge(s_w, 16 * (G + 1))

            def batch_norm(g):
                gate(act, s_turned, (g + 1) * G, passed)
                for j in range(G):
                    for k in range(CG):
                        act.activation(y[:, j, k, :], t["sums"][:, k, bass.ds((g * G + j) * P, P)], ACT.Identity,
                                       bias=t["bn_shift"][:, k:k + 1], scale=t["bn_scale"][:, k:k + 1]
                                       ).then_inc(s_y, 1)

            def ratio_of(g):
                act.wait_ge(s_gap, g + 1)
                act.activation(ratio[:], gap[:], ACT.Exp).then_inc(s_ratio, 1)

            def turn_affine(g, u, j):
                n = g * G + j
                act.wait_ge(s_back, 2 + n + 1)
                for k in range(CG):
                    act.activation(affine[:, (u + j) % 2, k, :], ps_t[:, (u + j) % 2, k * P:(k + 1) * P], ACT.Identity,
                                   bias=t["beta"][:, k:k + 1], scale=t["gamma"][:, k:k + 1]).then_inc(s_affine, 1)

            def body(r, g, u):
                if not is_group(g, 0):
                    ratio_of(g - 1)
                act.wait_ge(s_down, g * 2 + 1)
                for j in range(G):
                    act.activation(l1[:, j, :], x1[:, j, :], ACT.Identity, bias=down[:, 0, j:j + 1],
                                   scale=moments[:, 0, j, 1:2]).then_inc(s_l1, 1)
                if not is_group(g, GROUPS - 1):
                    batch_norm(g + 1)
                act.wait_ge(s_down, g * 2 + 2)
                gate(act, s_token_stored, g * 16 + 16, passed)
                for j in range(G):
                    act.activation(tokens[:, j, :], l1[:, j, :], ACT.Identity, bias=down[:, 1, j:j + 1],
                                   scale=moments[:, 1, j, 1:2]).then_inc(s_token, 1)
                    if j > 0:
                        turn_affine(g, u, j - 1)
                turn_affine(g, u, G - 1)

            act.preload_act_table(ACT.Exp)
            batch_norm(0)
            over_groups(act, body)
            ratio_of(GROUPS - 1)

        @block.tensor
        def _(pe):
            pe.wait_ge(s_w, 16 * (G + 1))
            pe.sem_inc(s_turned, G)
            pe.sem_inc(s_back, 2)

            def logit(g, u, j):
                n = g * G + j
                pe.wait_ge(s_affine, (n + 1) * CG)
                for k in range(CG):
                    last = pe.matmul(ps_l[:, j * E:(j + 1) * E], affine[:, (u + j) % 2, k, :], wr[:, k, :],
                                     start=(k == 0), stop=(k == CG - 1))
                last.then_inc(s_logit, 1)

            def turn(g):
                for j in range(G):
                    n = g * G + j
                    pe.wait_ge(s_y, (n + 1) * CG)
                    if j % 2 == 0:
                        pe.wait_ge(s_read, g * BANKS + j // 2 + 1)
                    for k in range(CG):
                        last = pe.transpose(ps_y[:, j // 2, j % 2, k * P:(k + 1) * P], y[:, j, k, :], t["ident"][:])
                    last.then_inc(s_turned, 1)

            def count(g):
                pe.wait_ge(s_both, g + 2)
                pe.matmul(ps_c[:, 0:G * E], t["before"][:], both[:].rearrange("p g e -> p (g e)"),
                          start=True, stop=False)
                for j in range(1, G):
                    pe.matmul(ps_c[:, j * E:G * E], t["ones"][:],
                              both[:, 0:G - j, :].rearrange("p g e -> p (g e)"), start=False, stop=False)
                for j in range(G):
                    last = pe.matmul(ps_c[:, j * E:(j + 1) * E], t["ones"][:], carried[:], start=False, stop=j == G - 1)
                last.then_inc(s_place, 1)

            def body(r, g, u):
                if not is_group(g, 0):
                    count(g - 1)
                if not is_group(g, GROUPS - 1):
                    turn(g + 1)
                for j in range(G):
                    n = g * G + j
                    pe.wait_ge(s_token, n + 1)
                    if j == 0:
                        pe.wait_ge(s_both, g + 1)
                    if j > 1:
                        pe.wait_ge(s_affine, (n - 1) * CG)
                    for k in range(CG):
                        last = pe.transpose(ps_t[:, (u + j) % 2, k * P:(k + 1) * P],
                                            tokens[:, j, k * P:(k + 1) * P], t["ident"][:])
                    last.then_inc(s_back, 1)
                    if j > 0:
                        logit(g, u, j - 1)
                logit(g, u, G - 1)

            turn(0)
            over_groups(pe, body)
            count(GROUPS - 1)

        @block.gpsimd
        def _(pool):
            pool.iota(experts_i[:], [[0, G], [1, E]], base=0, channel_multiplier=0).then_inc(s_const, 1)
            pool.iota(token_i[:], [[P, G]], base=-GROUP * P, channel_multiplier=1).then_inc(s_const, 1)
            pool.memset(minus_half[:], -0.5).then_inc(s_const, 1)
            pool.memset(carried[:], 0.0).then_inc(s_const, 1)
            pool.wait_ge(s_const, 4)
            for u in range(2):
                pool.dma_start(primer[:, u, :], d["src"][0:P, 0:2]).then_inc(s_scatter[u], 16 * 2 * G)

            def power(g, norm):
                gate(pool, s_var, g * 2 + norm + 1, passed)
                pool.tensor_tensor(moments[:, norm, :, 1], moments[:, norm, :, 1], minus_half[:],
                                   ALU.pow).then_inc(s_rstd, 1)

            def scatter(g, u, first, end):
                if first == 0:
                    gate(pool, s_entry, g + 1, passed)
                for n in range(first, end):
                    j, c = divmod(n, 2)
                    pool.indirect_dma_start(d["table"], bass.IndirectOffsetOnAxis(ap=slot[:, u, c, j:j + 1], axis=0),
                                            entry[:, u, c, j, :], None).then_inc(s_scatter[u], 16)

            def body(r, g, u):
                power(g, 0)
                if not is_group(g, 0) and not is_group(g, 1):
                    scatter(g - 2, u, SCATTER_FIRST, 2 * G)
                power(g, 1)
                if not is_group(g, 0):
                    scatter(g - 1, 1 - u, 0, SCATTER_FIRST)

            over_groups(pool, body)
            scatter(GROUPS - 2, 0, SCATTER_FIRST, 2 * G)
            scatter(GROUPS - 1, 1, 0, 2 * G)
            for u in range(2):
                pool.wait_ge(s_scatter[u], 16 * 2 * G * (GROUPS // 2 + 1))

        @block.vector
        def _(dve):
            dve.wait_ge(s_const, 4)
            dve.tensor_copy(experts[:], experts_i[:]).then_inc(s_const2, 1)
            dve.wait_ge(s_const2, 1)
            dve.tensor_scalar(slots_of[:], experts[:], float(NODES_PAD), None, ALU.mult).then_inc(s_const2, 1)
            dve.wait_ge(s_const2, 2)
            dve.sem_inc(s_both, 1)
            dve.sem_inc(s_read, BANKS)
            links = LINKS_ROUTE

            n = [0]

            def link(g, ins):
                n[0] += 1
                ins.then_inc(s_chain, 1)
                gate(dve, s_chain, g * links + n[0], passed)

            def add_residual(r, g, u):
                gate(dve, s_x[u], r * 16 + 16, passed)
                for j in range(G):
                    node = g * G + j
                    dve.tensor_scalar(residual[:, j, :], x[:, u, j, :], t["node_stats"][:, bass.ds(node * 2, 1)],
                                      t["node_stats"][:, bass.ds(node * 2 + 1, 1)], ALU.subtract,
                                      ALU.mult).then_inc(s_res, 1)
                for bank in range(BANKS):
                    first, end = bank * 2, min(bank * 2 + 2, G)
                    dve.wait_ge(s_res, g * G + end)
                    dve.wait_ge(s_turned, G + g * G + end)
                    dve.tensor_tensor(residual[:, first:end, :], ps_y[:, bank, 0:end - first, :],
                                      residual[:, first:end, :], ALU.add).then_inc(s_read, 1)
                gate(dve, s_x1_stored, g * 16 + 16, passed)
                dve.wait_ge(s_read, (g + 2) * BANKS)
                dve.scalar_tensor_tensor(x1[:], residual[:], 0.0, x[:, u, :, :], ALU.max, ALU.add).then_inc(s_x1, 1)

            def variances(g, which, rows):
                for j in range(G):
                    if which == 0 and j == 0:
                        gate(dve, s_x1, 2 + g + 1, passed)
                    if which == 1:
                        gate(dve, s_l1, g * G + j + 1, passed)
                    dve.bn_stats(stats[:, j, :], rows[:, j, :]).then_inc(s_stat, 1)
                for j in range(G):
                    gate(dve, s_stat, g * 2 * G + which * G + j + 1, passed)
                    dve.bn_aggr(moments[:, which, j, :], stats[:, j, :]).then_inc(s_aggr, 1)
                gate(dve, s_aggr, (g * 2 + which + 1) * G, passed)
                var = moments[:, which, :, 1]
                dve.tensor_scalar(var, var, EPS, None, ALU.add).then_inc(s_var, 1)

            def shift_down(g, which):
                gate(dve, s_rstd, g * 2 + which + 1, passed)
                dve.scalar_tensor_tensor(down[:, which, :], moments[:, which, :, 0], -1.0, moments[:, which, :, 1],
                                         ALU.mult, ALU.mult).then_inc(s_down, 1)

            def choose(g):
                n[0] = 0
                gate(dve, s_logit, (g + 1) * G, passed)
                link(g, dve.tensor_tensor(logits[:], ps_l[:, 0:G * E].rearrange("p (g e) -> p g e", g=G), br[:],
                                          ALU.add))
                for j in range(G):
                    dve.max(top[:, j, :], logits[:, j, :]).then_inc(s_chain, 1)
                n[0] += G
                gate(dve, s_chain, g * links + n[0], passed)
                dve.tensor_tensor(gap[:], top[:, :, 1], top[:, :, 0], ALU.subtract).then_inc(s_gap, 1)
                for j in range(G):
                    dve.max_index(which[:, j, :], top[:, j, :], logits[:, j, :]).then_inc(s_chain, 1)
                n[0] += G
                gate(dve, s_chain, g * links + n[0], passed)
                link(g, dve.tensor_copy(which_f[:], which[:]))
                for c in range(2):
                    dve.tensor_tensor(chosen[:, c, :, :], experts[:], which_f[:, :, c:c + 1].to_broadcast([P, G, E]),
                                      ALU.is_equal).then_inc(s_chain, 1)
                n[0] += 2
                gate(dve, s_chain, g * links + n[0], passed)
                dve.tensor_tensor(both[:], chosen[:, 0, :, :], chosen[:, 1, :, :], ALU.add).then_inc(s_both, 1)

            def weigh(r, g, u):
                gate(dve, s_ratio, g + 1, passed)
                link(g, dve.tensor_scalar(total[:], ratio[:], 1.0, None, ALU.add))
                gate(dve, s_scatter[u], (r + 1) * (16 * 2 * G), passed)
                weight = entry[:, u, :, :, :].bitcast(F32)
                link(g, dve.reciprocal(weight[:, 0, :, 1], total[:]))
                dve.tensor_tensor(weight[:, 1, :, 1], weight[:, 0, :, 1], ratio[:], ALU.mult).then_inc(s_chain, 1)
                dve.tensor_scalar(token_i[:], token_i[:], float(G * P), None, ALU.add).then_inc(s_chain, 1)
                n[0] += 2
                gate(dve, s_chain, g * links + n[0], passed)
                for c in range(2):
                    dve.tensor_copy(entry[:, u, c, :, 0], token_i[:]).then_inc(s_chain, 1)
                gate(dve, s_both, g + 2, passed)
                dve.tensor_reduce(of_group[:], both[:].rearrange("p g e -> p e g"), mybir.AxisListType.X,
                                  ALU.add).then_inc(s_chain, 1)
                n[0] += 3

            def find_slots(g, u):
                gate(dve, s_place, g + 1, passed)
                link(g, dve.tensor_tensor(place[:], ps_c[:, 0:G * E].rearrange("p (g e) -> p g e", g=G), slots_of[:],
                                          ALU.add))
                for c in range(2):
                    dve.tensor_tensor(picked[:, c, :, :], place[:], chosen[:, c, :, :], ALU.mult).then_inc(s_chain, 1)
                dve.tensor_tensor(carried[:], carried[:], of_group[:], ALU.add).then_inc(s_chain, 1)
                n[0] += 3
                gate(dve, s_chain, g * links + n[0], passed)
                link(g, dve.tensor_reduce(slot_f[:], picked[:], mybir.AxisListType.X, ALU.add))
                dve.tensor_copy(slot[:, u, :, :], slot_f[:]).then_inc(s_entry, 1)
                assert n[0] == links, n[0]

            def body(r, g, u):
                former = r if u == 1 else r - 1
                routes = not is_group(g, 0)
                add_residual(r, g, u)
                variances(g, 0, x1)
                if routes:
                    choose(g - 1)
                shift_down(g, 0)
                if routes:
                    weigh(former, g - 1, 1 - u)
                variances(g, 1, l1)
                if routes:
                    find_slots(g - 1, 1 - u)
                shift_down(g, 1)

            over_groups(dve, body)
            choose(GROUPS - 1)
            weigh(GROUPS // 2 - 1, GROUPS - 1, 1)
            find_slots(GROUPS - 1, 1)
            dve.tensor_copy(t["chosen_by"][:], carried[:]).then_inc(s_const2, 1)
            dve.wait_ge(s_const2, 3)


LINKS_ROUTE = 4 + 2 * GROUP + 7 + 5
SCATTER_FIRST = 9


def list_tiles(nc, d, t):
    with phase(nc, "lt") as (sb, ps, sem, ctx):
        E, L = EXPERTS, FFN_LIST
        counts_ps = ps("counts_ps", [P, 512], F32)
        counts = sb("counts", [P, E], I32)
        tiles_i = sb("tiles_i", [P, E], I32)
        tiles = sb("tiles", [P, E], F32)
        base = sb("base", [P, E], F32)
        tile_i = sb("tile_i", [P, L], I32)
        tile_no = sb("tile_no", [P, L], F32)
        within = sb("within", [P, L], F32)
        entered = sb("entered", [P, L], F32)
        expert = sb("expert", [P, L], F32)
        first = sb("first", [P, L], F32)
        s_counts = sem("s_counts")
        s_iota = sem("s_iota")
        s_chain = sem("s_chain")
        block = ctx.enter_context(nc.Block())

        @block.sync
        def _(sp):
            sp.dma_start(t["ffn_b1"][:], d["b1"].rearrange("e h -> (e h)").partition_broadcast(P)
                         ).then_inc(t["ffn_loaded"], 16)
            sp.dma_start(t["ffn_w1"][:].rearrange("p (e k h) -> p e k h", e=E, k=CG),
                         d["w1"].rearrange("e (k p) h -> p e k h", p=P)).then_inc(t["ffn_loaded"], 16)
            sp.dma_start(t["ffn_b2"][:], d["b2"].rearrange("e c -> (e c)").partition_broadcast(P)
                         ).then_inc(t["ffn_loaded"], 16)
            sp.dma_start(t["ffn_w2"][:].rearrange("p (e k c) -> p e k c", e=E, k=HG),
                         d["w2"].rearrange("e (k p) c -> p e k c", p=P)).then_inc(t["ffn_loaded"], 16)

        @block.tensor
        def _(pe):
            pe.matmul(counts_ps[:, 0:E], t["ones"][:], t["chosen_by"][:], start=True, stop=True).then_inc(s_counts, 1)

        @block.gpsimd
        def _(pool):
            pool.iota(tile_i[:], [[1, L]], base=0, channel_multiplier=0).then_inc(s_iota, 1)

        @block.vector
        def _(dve):
            n = [0]

            def link(ins):
                n[0] += 1
                ins.then_inc(s_chain, 1)
                dve.wait_ge(s_chain, n[0])

            dve.wait_ge(s_counts, 1)
            link(dve.tensor_scalar(counts[:], counts_ps[:, 0:E], float(P - 1), None, ALU.add))
            link(dve.tensor_scalar(tiles_i[:], counts[:], 7, None, ALU.logical_shift_right))
            link(dve.tensor_copy(tiles[:], tiles_i[:]))
            dve.wait_ge(s_iota, 1)
            link(dve.tensor_copy(tile_no[:], tile_i[:]))
            link(dve.tensor_copy(within[:], tile_i[:]))
            link(dve.memset(expert[:], 0.0))
            link(dve.memset(base[:], 0.0))
            for e in range(1, E):
                link(dve.tensor_tensor(base[:, e:e + 1], base[:, e - 1:e], tiles[:, e - 1:e], ALU.add))
                link(dve.tensor_scalar(entered[:], tile_no[:], base[:, e:e + 1], None, ALU.is_ge))
                link(dve.tensor_tensor(expert[:], expert[:], entered[:], ALU.add))
                link(dve.tensor_scalar(entered[:], entered[:], tiles[:, e - 1:e], None, ALU.mult))
                link(dve.tensor_tensor(within[:], within[:], entered[:], ALU.subtract))
            link(dve.tensor_scalar(first[:], within[:], float(P), None, ALU.mult))
            link(dve.scalar_tensor_tensor(first[:], expert[:], float(NODES_PAD), first[:], ALU.mult, ALU.add))
            link(dve.tensor_copy(t["tile_slot"][:], first[0:1, :]))
            link(dve.tensor_copy(t["tile_expert"][:], expert[0:1, :]))


TABLES = 12
ROWS_HELD = 6
GATHER_AHEAD = 4
TABLE_AHEAD = 6
FFN_ROUNDS = FFN_TILES // TABLES
assert FFN_ROUNDS * TABLES == FFN_TILES


def run_experts(nc, d, t):
    with phase(nc, "ffn") as (sb, ps, sem, ctx):
        E = EXPERTS
        w1, w2, b1, b2 = (t[f"ffn_{n}"] for n in ("w1", "w2", "b1", "b2"))
        table = sb("table", [P, TABLES, 2], I32)
        rows = sb("rows", [P, ROWS_HELD, C], F32)
        xT = sb("xT", [P, 2, CG, P], F32)
        pre = sb("pre", [P, 2, HIDDEN], F32)
        hidden = sb("hidden", [P, 2, HIDDEN], F32)
        hT = sb("hT", [P, 2, HIDDEN], F32)
        yb = sb("yb", [P, 2, C], F32)
        result = sb("result", [P, 2, C], F32)
        primer = sb("primer", [P, 2], I32)
        ps_x = ps("ps_x", [P, 512], F32)
        ps_1 = ps("ps_1", [P, 2, 512], F32)
        ps_h = ps("ps_h", [P, 2, 512], F32)
        ps_2 = ps("ps_2", [P, 2, 512], F32)
        s_w = t["ffn_loaded"]
        s_table = [sem(f"s_table{k}") for k in range(TABLES)]
        s_rows = [sem(f"s_rows{k}") for k in range(ROWS_HELD)]
        s_xturn = sem("s_xturn")
        s_xT = sem("s_xT")
        s_one = sem("s_one")
        s_pre = sem("s_pre")
        s_hidden = sem("s_hidden")
        s_hturn = sem("s_hturn")
        s_hT = sem("s_hT")
        s_two = sem("s_two")
        s_yb = sem("s_yb")
        s_result = sem("s_result")
        s_scatter = sem("s_scatter")
        s_free = sem("s_free")
        passed = sem("passed")
        block = ctx.enter_context(nc.Block())
        F = TABLES
        W = 16 * 4

        @block.sync
        def _(sp):
            def load(tile, k):
                first = sp.value_load(t["tile_slot"][0:1, bass.ds(tile, 1)], min_val=0, max_val=TABLE_ROWS - P)
                sp.dma_start(table[:, k, :], d["table"][bass.ds(first, P), :]).then_inc(s_table[k], 16)

            for k in range(TABLE_AHEAD):
                load(k, k)
            with sp.Fori(0, FFN_ROUNDS) as i:
                for k in range(F):
                    s = i * F + k
                    gate(sp, s_free, s + TABLE_AHEAD + 2, passed)
                    load(s + TABLE_AHEAD, (k + TABLE_AHEAD) % F)
            for k in range(F):
                sp.wait_ge(s_table[k], 16 * (FFN_ROUNDS + (1 if k < TABLE_AHEAD else 0)))

        @block.gpsimd
        def _(pool):
            def gather(k, round_, row_slot):
                gate(pool, s_table[k], round_ * 16 + 16, passed)
                pool.indirect_dma_start(rows[:, row_slot, :], None, d["tokens"],
                                        bass.IndirectOffsetOnAxis(ap=table[:, k, 0:1], axis=0)
                                        ).then_inc(s_rows[row_slot], 16)

            pool.dma_start(primer[:], d["src"][0:P, 0:2]).then_inc(s_scatter, 16)
            pool.sem_inc(s_free, TABLES)
            for k in range(GATHER_AHEAD):
                gather(k, 0, k)
            with pool.Fori(0, FFN_ROUNDS) as i:
                for k in range(F):
                    s = i * F + k
                    ahead = k + GATHER_AHEAD
                    gate(pool, s_xturn, s + GATHER_AHEAD + 1, passed)
                    gather(ahead % F, i + ahead // F, ahead % ROWS_HELD)
                    gate(pool, s_scatter, (s + 1) * 16, s_free)
                    gate(pool, s_result, 2 + s + 1, passed)
                    pool.indirect_dma_start(d["out"], bass.IndirectOffsetOnAxis(ap=table[:, k, 0:1], axis=0),
                                            result[:, k % 2, :], None, compute_op=ALU.add).then_inc(s_scatter, 16)
            pool.wait_ge(s_scatter, 16 * (1 + FFN_TILES))
            for k in range(ROWS_HELD):
                pool.wait_ge(s_rows[k], 16 * (2 * FFN_ROUNDS + (1 if k < GATHER_AHEAD else 0)))

        @block.tensor
        def _(pe):
            def turn_rows(s, k, round_):
                pe.wait_ge(s_rows[k % ROWS_HELD], round_ * 16 + 16)
                if not isinstance(s, int) or s > 0:
                    pe.wait_ge(s_xT, s * CG)
                for g in range(CG):
                    last = pe.transpose(ps_x[:, g * P:(g + 1) * P], rows[:, k % ROWS_HELD, g * P:(g + 1) * P],
                                        t["ident"][:])
                last.then_inc(s_xturn, 1)

            def expert_of(s):
                return pe.value_load(t["tile_expert"][0:1, bass.ds(s, 1)], min_val=0, max_val=E - 1)

            def first_product(s, q, e):
                pe.wait_ge(s_xT, (s + 1) * CG)
                pe.wait_ge(s_pre, s + 1)
                for g in range(CG):
                    last = pe.matmul(ps_1[:, q, :], xT[:, q, g, :],
                                     w1[:, bass.ds(e * (CG * HIDDEN) + g * HIDDEN, HIDDEN)],
                                     start=(g == 0), stop=(g == CG - 1))
                last.then_inc(s_one, 1)

            def turn_hidden(s, q):
                pe.wait_ge(s_hidden, 2 + s + 1)
                for g in range(HG):
                    last = pe.transpose(ps_h[:, q, g * P:(g + 1) * P], hidden[:, q, g * P:(g + 1) * P], t["ident"][:])
                last.then_inc(s_hturn, 1)

            def second_product(s, q, e):
                pe.wait_ge(s_hT, s + 1)
                pe.wait_ge(s_yb, s + 1)
                for g in range(HG):
                    last = pe.matmul(ps_2[:, q, 0:C], hT[:, q, g * P:(g + 1) * P],
                                     w2[:, bass.ds(e * (HG * C) + g * C, C)], start=(g == 0), stop=(g == HG - 1))
                last.then_inc(s_two, 1)

            pe.wait_ge(s_w, W)
            pe.sem_inc(s_xturn, ROWS_HELD)
            pe.sem_inc(s_one, 2)
            pe.sem_inc(s_two, 2)
            turn_rows(0, 0, 0)
            turn_rows(1, 1, 0)
            first_product(0, 0, expert_of(0))
            with pe.Fori(0, FFN_ROUNDS) as i:
                for k in range(F):
                    s = i * F + k
                    expert = expert_of(s) if k == 0 else next_expert
                    next_expert = expert_of(s + 1)
                    turn_hidden(s, k % 2)
                    first_product(s + 1, (k + 1) % 2, next_expert)
                    turn_rows(s + 2, k + 2, i * 2 + (k + 2) // ROWS_HELD)
                    second_product(s, k % 2, expert)

        @block.scalar
        def _(act):
            act.wait_ge(s_w, W)
            act.sem_inc(s_hidden, 2)
            act.sem_inc(s_result, 2)
            act.preload_act_table(ACT.Gelu)

            def scale_rows(s, q):
                gate(act, s_xturn, ROWS_HELD + s + 1, passed)
                gate(act, s_one, s + 1, passed)
                for g in range(CG):
                    act.activation(xT[:, q, g, :], ps_x[:, g * P:(g + 1) * P], ACT.Identity,
                                   bias=t["beta"][:, g:g + 1], scale=t["gamma"][:, g:g + 1]).then_inc(s_xT, 1)

            def activate(s, q):
                gate(act, s_pre, 2 + s + 1, passed)
                act.activation(hidden[:, q, :], pre[:, q, :], ACT.Gelu).then_inc(s_hidden, 1)

            scale_rows(0, 0)
            scale_rows(1, 1)
            activate(0, 0)
            with act.Fori(0, FFN_ROUNDS) as i:
                for k in range(F):
                    s = i * F + k
                    q = k % 2
                    gate(act, s_hturn, s + 1, passed)
                    gate(act, s_two, s + 1, passed)
                    act.activation(hT[:, q, :], ps_h[:, q, :], ACT.Copy).then_inc(s_hT, 1)
                    scale_rows(s + 2, q)
                    activate(s + 1, 1 - q)
                    gate(act, s_yb, 2 + s + 1, passed)
                    gate(act, s_free, s + TABLES, passed)
                    act.activation(result[:, q, :], yb[:, q, :], ACT.Copy,
                                   scale=table[:, k, 1:2].bitcast(F32)).then_inc(s_result, 1)

        @block.vector
        def _(dve):
            dve.wait_ge(s_w, W)
            dve.sem_inc(s_pre, 2)
            dve.sem_inc(s_yb, 2)

            def bias_one(s, q):
                e = dve.value_load(t["tile_expert"][0:1, bass.ds(s, 1)], min_val=0, max_val=E - 1)
                gate(dve, s_one, 2 + s + 1, passed)
                gate(dve, s_hidden, s + 1, passed)
                dve.tensor_tensor(pre[:, q, :], ps_1[:, q, :], b1[:, bass.ds(e * HIDDEN, HIDDEN)],
                                  ALU.add).then_inc(s_pre, 1)

            bias_one(0, 0)
            with dve.Fori(0, FFN_ROUNDS) as i:
                for k in range(F):
                    s = i * F + k
                    q = k % 2
                    bias_one(s + 1, (k + 1) % 2)
                    e = dve.value_load(t["tile_expert"][0:1, bass.ds(s, 1)], min_val=0, max_val=E - 1)
                    gate(dve, s_two, 2 + s + 1, passed)
                    gate(dve, s_result, s + 1, passed)
                    dve.tensor_tensor(yb[:, q, :], ps_2[:, q, 0:C], b2[:, bass.ds(e * C, C)],
                                      ALU.add).then_inc(s_yb, 1)


def kernel_program(nc, d):
    with ExitStack() as ctx:
        sb = lambda n, s, dt: ctx.enter_context(nc.sbuf_tensor(n, s, dt))
        t = {
            "ident": sb("ident", [P, P], F32),
            "ones": sb("ones", [P, P], F32),
            "before": sb("before", [P, P], F32),
            "minus_half": sb("minus_half", [P, 1], F32),
            "zeros": sb("zeros", [P, C], F32),
            "iota_i": sb("iota_i", [P, P], I32),
            "iota": sb("iota", [P, P], F32),
            "bn_scale": sb("bn_scale", [P, CG], F32),
            "bn_shift": sb("bn_shift", [P, CG], F32),
            "gamma": sb("gamma", [P, CG], F32),
            "beta": sb("beta", [P, CG], F32),
            "chosen_by": sb("chosen_by", [P, EXPERTS], F32),
            "tile_slot": sb("tile_slot", [1, FFN_LIST], I32),
            "tile_expert": sb("tile_expert", [1, FFN_LIST], I32),
            "node_mean": sb("node_mean", [P, 2, 2], F32),
            "node_stats": sb("node_stats", [P, NODE_TILES * 2], F32),
        }
        with ExitStack() as edges:
            for name, dt in (("edge_src", I32), ("edge_dst", F32), ("edge_w", F32)):
                t[name] = edges.enter_context(nc.sbuf_tensor(name, [P, EDGE_ROWS], dt))
            t["step_nodes"] = edges.enter_context(nc.sbuf_tensor("step_nodes", [1, EDGE_ROWS], I32))
            with nc.sbuf_tensor("pad_slots", [P, TABLE_ROWS // P, 2], I32) as pad:
                t["pad_slots"] = pad
                plan_steps(nc, d, t)
            project_input(nc, d, t)
            t["sums"] = edges.enter_context(nc.sbuf_tensor("sums", [P, CG, NODES_PAD], F32))
            sum_messages(nc, d, t, d["h"], "c1")
            normalize_sums(nc, d, t, "c1")
            project_hidden(nc, d, t)
            sum_messages(nc, d, t, d["h2"], "c2")
            normalize_sums(nc, d, t, "c2")
            route_tokens(nc, d, t)
        for name, size in (("w1", EXPERTS * CG * HIDDEN), ("w2", EXPERTS * HG * C), ("b1", EXPERTS * HIDDEN),
                           ("b2", EXPERTS * C)):
            t[f"ffn_{name}"] = sb(f"ffn_{name}", [P, size], F32)
        t["ffn_loaded"] = nc.alloc_semaphore(name="ffn_loaded")
        list_tiles(nc, d, t)
        run_experts(nc, d, t)
        nc.clear_and_free_semaphores([t["ffn_loaded"]])
        nc.all_engine_barrier()


INPUTS = {
    "x": "x", "src": "src", "dst": "dst", "ew": "edge_weight",
    "c1_w1": "L0_gnn_c1_w1", "c1_b1": "L0_gnn_c1_b1", "c1_w2": "L0_gnn_c1_w2", "c1_b2": "L0_gnn_c1_b2",
    "c1_g": "L0_gnn_c1_g", "c1_b": "L0_gnn_c1_b", "bn1_g": "L0_gnn_bn1_g", "bn1_b": "L0_gnn_bn1_b",
    "c2_w1": "L0_gnn_c2_w1", "c2_b1": "L0_gnn_c2_b1", "c2_w2": "L0_gnn_c2_w2", "c2_b2": "L0_gnn_c2_b2",
    "c2_g": "L0_gnn_c2_g", "c2_b": "L0_gnn_c2_b", "bn2_g": "L0_gnn_bn2_g", "bn2_b": "L0_gnn_bn2_b",
    "gamma": "L0_ffn_gamma", "beta": "L0_ffn_beta", "wr": "L0_ffn_Wr", "br": "L0_ffn_br",
    "w1": "L0_ffn_W1", "b1": "L0_ffn_b1", "w2": "L0_ffn_W2", "b2": "L0_ffn_b2",
}


def kernel(**inputs):
    import numpy as np
    import concourse.bacc as bacc
    from concourse.bass_utils import run_bass_kernel_spmd

    nc = bacc.Bacc("TRN2", target_bir_lowering=False, num_devices=1)
    arrays, d = {}, {}
    pad_edges = EDGE_ROWS * P - EDGES
    for name, key in INPUTS.items():
        a = np.asarray(inputs[key])
        if name == "x":
            a = np.concatenate([a, np.zeros((NODES_PAD - NODES, C), a.dtype)])
        if name in ("src", "ew"):
            a = np.concatenate([a, np.zeros(pad_edges, a.dtype)]).reshape(EDGE_ROWS, P)
        if name == "dst":
            a = np.concatenate([a, np.full(pad_edges, NODES_PAD - 1, a.dtype)]).reshape(EDGE_ROWS, P)
        a = np.ascontiguousarray(a)
        arrays[f"in_{name}"] = a
        d[name] = nc.dram_tensor(f"in_{name}", a.shape, mybir.dt.from_np(a.dtype), kind="ExternalInput").ap()
    scratch = {
        "h": ((NODES_PAD, C), F32), "h2": ((NODES_PAD, C), F32), "step_list": ((EDGE_ROWS,), I32),
        "table": ((TABLE_ROWS, 2), I32), "tokens": ((OUT_ROWS, C), F32),
    }
    for name, (shape, dt) in scratch.items():
        d[name] = nc.dram_tensor(name, shape, dt, kind="Internal").ap()
    d["out"] = nc.dram_tensor("out", (OUT_ROWS, C), F32, kind="ExternalOutput").ap()
    kernel_program(nc, d)
    r = run_bass_kernel_spmd(nc, [arrays], core_ids=[0])
    return r.results[0]["out"][:NODES]
```

```python
from contextlib import ExitStack, contextmanager

import concourse.bass as bass
from concourse import mybir

ALU = mybir.AluOpType
ACT = mybir.ActivationFunctionType
F32 = mybir.dt.float32
F32R = mybir.dt.float32r
BF16 = mybir.dt.bfloat16
I32 = mybir.dt.int32
U32 = mybir.dt.uint32

P = 128
EPS = 1e-5
NODES = 12500
C = 256
CG = C // P
NODE_TILES = -(-NODES // P)
NODES_PAD = NODE_TILES * P
EDGES = 200000
EDGE_TILES = -(-EDGES // P)
STEPS = EDGE_TILES + NODE_TILES - 1
STEP_CHUNKS = -(-STEPS // P)
EDGE_ROWS = STEP_CHUNKS * P

RING = 16
HALF = RING // 2
SUM_BANKS = 4
LEAD = 4
ROUNDS = -(-EDGE_TILES // RING)
MORE_ROUNDS = EDGE_ROWS // RING - ROUNDS
assert EDGE_ROWS % RING == 0 and EDGE_ROWS >= STEPS and RING % SUM_BANKS == 0 and RING % LEAD == 0
STEP_ROOM = EDGE_ROWS + LEAD

COLS = 512
CHUNKS = NODES // COLS
REST = NODES - CHUNKS * COLS

GROUP = 7
GROUPS = NODE_TILES // GROUP
assert GROUPS * GROUP == NODE_TILES and GROUPS % 2 == 0

EXPERTS = 8
HIDDEN = 512
HG = HIDDEN // P
PAIRS = 2 * NODES_PAD
FFN_TILES = PAIRS // P + EXPERTS
FFN_LIST = FFN_TILES + 8
TABLE_TILES = EXPERTS * NODE_TILES + 16
TABLE_ROWS = TABLE_TILES * P
OUT_ROWS = NODES_PAD + P


def gate(eng, sem, value, passed):
    eng.wait_ge(sem, value)
    eng.sem_inc(passed, 1)


@contextmanager
def phase(nc, name):
    held = []

    def semaphore(n):
        held.append(nc.alloc_semaphore(name=f"{name}_{n}"))
        return held[-1]

    with ExitStack() as ctx:
        yield (lambda n, shape, dt: ctx.enter_context(nc.sbuf_tensor(f"{name}_{n}", shape, dt)),
               lambda n, shape, dt: ctx.enter_context(nc.psum_tensor(f"{name}_{n}", shape, dt)),
               semaphore, ctx)
    nc.clear_and_free_semaphores(held)
    nc.all_engine_barrier()


def plan_tiles(nc, d, t):
    with phase(nc, "pt") as (sb, ps, sem, ctx):
        K = STEP_CHUNKS
        exceeds = sb("exceeds", [P, K], F32)
        exceeding = sb("exceeding", [P, 1], F32)
        g_src = sb("g_src", [P, K, P], I32)
        g_dst = sb("g_dst", [P, K, P], I32)
        g_ew = sb("g_ew", [P, K, P], F32)
        f_src = sb("f_src", [P, K, P], F32)
        f_dst = sb("f_dst", [P, K, P], F32)
        wide_tiles = ps("wide_tiles", [P, 512], F32)
        turned = ps("turned", [P, 4, 512], F32)

        s_iota = sem("iota")
        s_chain = sem("chain")
        s_exceeding = sem("exceeding")
        s_wide = sem("wide")
        s_list = sem("list")
        s_row = sem("row")
        s_rows = [sem(f"rows{a}") for a in range(3)]
        s_float = [sem(f"float{a}") for a in range(2)]
        s_turned = sem("turned")
        s_out = sem("out")
        s_ident = sem("ident")
        s_pad = sem("pad")
        s_mask = sem("mask")
        s_table = sem("table")
        s_columns = sem("columns")

        groups = [(a, c, min(c + 4, K)) for a in range(3) for c in range(0, K, 4)]
        block = ctx.enter_context(nc.Block())

        @block.sync
        def _(sp):
            for a, (rows, dest) in enumerate(((d["src"], g_src), (d["dst"], g_dst), (d["ew"], g_ew))):
                sp.dma_start(dest[:], rows.rearrange("(c p) e -> p c e", p=P)).then_inc(s_rows[a], 16)
            with nc.allow_non_contiguous_dma(reason="256 words, one for each channel"):
                sp.dma_start(t["gamma"][:], d["gamma"].rearrange("(k p) -> p k", p=P)).then_inc(s_columns, 16)
                sp.dma_start(t["beta"][:], d["beta"].rearrange("(k p) -> p k", p=P)).then_inc(s_columns, 16)
            sp.wait_ge(s_rows[1], 16)
            with nc.allow_non_contiguous_dma(reason="1664 words"):
                sp.dma_start(d["step_list"].rearrange("(c p) -> p c", p=P), g_dst[:, :, 0]).then_inc(s_list, 16)
            sp.wait_ge(s_list, 16)
            sp.dma_start(t["step_nodes"][0:1, :], d["step_list"].rearrange("(a n) -> a n", a=1)).then_inc(s_row, 16)
            sp.wait_ge(s_mask, 2)
            sp.dma_start(d["table"].rearrange("(p b) w -> p b w", p=P), t["pad_slots"][:]).then_inc(s_table, 16)
            sp.wait_ge(s_pad, 1)
            sp.dma_start(d["tokens"][NODES_PAD:OUT_ROWS, :], t["zeros"][:]).then_inc(s_table, 16)
            sp.dma_start(d["out"][NODES_PAD:OUT_ROWS, :], t["zeros"][:]).then_inc(s_table, 16)
            sp.wait_ge(s_row, 16)
            sp.wait_ge(s_table, 48)
            sp.wait_ge(s_columns, 32)

        @block.gpsimd
        def _(pool):
            pool.memset(t["ident"][:], 0.0).then_inc(s_ident, 1)
            pool.wait_ge(s_ident, 1)
            pool.affine_select(out=t["ident"][:], in_=t["ident"][:], compare_op=ALU.not_equal, fill=1.0, base=0,
                               pattern=[[-1, P]], channel_multiplier=1).then_inc(s_ident, 1)
            pool.iota(t["pad_slots"][:, :, 0], [[1, TABLE_ROWS // P]], base=0,
                      channel_multiplier=TABLE_ROWS // P).then_inc(s_iota, 1)
            pool.memset(t["pad_slots"][:, :, 1], 0).then_inc(s_iota, 1)
            pool.iota(t["iota_i"][:], [[1, P]], base=0, channel_multiplier=0).then_inc(s_iota, 1)
            pool.memset(t["zeros"][:], 0.0).then_inc(s_pad, 1)
            pool.memset(t["minus_half"][:], -0.5)
            pool.memset(t["ones"][:], 1.0).then_inc(s_pad, 1)
            pool.wait_ge(s_pad, 2)
            pool.affine_select(out=t["before"][:], in_=t["ones"][:], compare_op=ALU.is_gt, fill=0.0, base=0,
                               pattern=[[1, P]], channel_multiplier=-1).then_inc(s_pad, 1)

        @block.vector
        def _(dve):
            n = [0]

            def link(ins):
                n[0] += 1
                ins.then_inc(s_chain, 1)
                dve.wait_ge(s_chain, n[0])

            dve.memset(t["edge_dst"][:, EDGE_ROWS:], 0.0)
            dve.memset(t["edge_w"][:, EDGE_ROWS:], 0.0)
            dve.wait_ge(s_rows[0], 16)
            dve.tensor_copy(f_src[:], g_src[:]).then_inc(s_float[0], 1)
            dve.wait_ge(s_rows[1], 16)
            link(dve.tensor_tensor(f_dst[:], g_dst[:], g_dst[:, :, 0:1].to_broadcast([P, K, P]), ALU.subtract))
            dve.tensor_scalar(exceeds[:], f_dst[:, :, P - 1], float(P), None, ALU.is_ge).then_inc(s_float[1], 1)
            dve.wait_ge(s_float[1], 1)
            dve.tensor_reduce(exceeding[:], exceeds[:], mybir.AxisListType.X, ALU.add).then_inc(s_exceeding, 1)
            dve.wait_ge(s_iota, 3)
            dve.tensor_copy(t["iota"][:], t["iota_i"][:]).then_inc(s_mask, 1)
            dve.tensor_scalar(t["pad_slots"][:, :, 0], t["pad_slots"][:, :, 0], P - 1, NODES_PAD,
                              ALU.bitwise_and, ALU.bitwise_or).then_inc(s_mask, 1)
            dve.wait_ge(s_wide, 1)
            dve.tensor_scalar(t["wide"][:], wide_tiles[0:1, 0:1], 0.5, None, ALU.is_gt).then_inc(s_mask, 1)
            for g, (a, c0, c1) in enumerate(groups):
                dve.wait_ge(s_turned, g + 1)
                dest = (t["edge_src"], t["edge_dst"], t["edge_w"])[a]
                dve.tensor_copy(dest[:, c0 * P:c1 * P], turned[:, g % 4, 0:(c1 - c0) * P]).then_inc(s_out, 1)

        @block.tensor
        def _(pe):
            pe.wait_ge(s_pad, 2)
            pe.wait_ge(s_exceeding, 1)
            pe.matmul(wide_tiles[:, 0:1], t["ones"][:], exceeding[:], start=True, stop=True).then_inc(s_wide, 1)
            pe.wait_ge(s_ident, 2)
            for g, (a, c0, c1) in enumerate(groups):
                if g == 0:
                    pe.wait_ge(s_float[0], 1)
                if c0 == 0 and a == 1:
                    pe.wait_ge(s_float[1], 1)
                if c0 == 0 and a == 2:
                    pe.wait_ge(s_rows[2], 16)
                if g >= 4:
                    pe.wait_ge(s_out, g - 3)
                rows = (f_src, f_dst, g_ew)[a]
                for c in range(c0, c1):
                    last = pe.transpose(turned[:, g % 4, (c - c0) * P:(c - c0 + 1) * P], rows[:, c, :], t["ident"][:])
                last.then_inc(s_turned, 1)


def plan_steps(nc, d, t):
    with phase(nc, "pl") as (sb, ps, sem, ctx):
        K = STEP_CHUNKS
        last_dst = sb("last_dst", [P, K], I32)
        block_of_last = sb("block_of_last", [P, K], I32)
        tile_no_i = sb("tile_no_i", [P, K], I32)
        tile_no = sb("tile_no", [P, K], F32)
        entry = sb("entry", [P, K], F32)
        step_row_i = sb("step_row_i", [P, K * P], I32)
        step_row = sb("step_row", [P, K * P], F32)
        entered = sb("entered", [P, K, K * P], BF16)
        ones_bf = sb("ones_bf", [P, 1], BF16)
        step_tile = sb("step_tile", [P, K], F32)
        step_tile_i = sb("step_tile_i", [P, K], I32)
        step_no = sb("step_no", [P, K], F32)
        step_node = sb("step_node", [P, K], F32)
        step_node_i = sb("step_node_i", [P, K], I32)
        g_src = sb("g_src", [P, K, P], I32)
        g_dst = sb("g_dst", [P, K, P], I32)
        g_ew = sb("g_ew", [P, K, P], F32)
        f_src = sb("f_src", [P, K, P], F32)
        f_dst = sb("f_dst", [P, K, P], F32)
        count = ps("count", [P, 512], F32)
        turned = ps("turned", [P, 4, 512], F32)

        s_in = sem("in")
        s_iota = sem("iota")
        s_chain = sem("chain")
        s_entered = sem("entered")
        s_count = sem("count")
        s_tile = sem("tile")
        s_node = sem("node")
        s_list = sem("list")
        s_row = sem("row")
        s_rows = [sem(f"rows{a}") for a in range(3)]
        s_float = [sem(f"float{a}") for a in range(2)]
        s_turned = sem("turned")
        s_out = sem("out")

        groups = [(a, c, min(c + 4, K)) for a in range(3) for c in range(0, K, 4)]
        block = ctx.enter_context(nc.Block())

        @block.sync
        def _(sp):
            with nc.allow_non_contiguous_dma(reason="one word of each row, 1664 in all"):
                sp.dma_start(last_dst[:], d["dst"].rearrange("(c p) e -> p c e", p=P)[:, :, P - 1]).then_inc(s_in, 16)
            sp.wait_ge(s_node, 1)
            with nc.allow_non_contiguous_dma(reason="1664 words"):
                sp.dma_start(d["step_list"].rearrange("(c p) -> p c", p=P), step_node_i[:]).then_inc(s_list, 16)
            sp.wait_ge(s_list, 16)

        @block.scalar
        def _(act):
            act.wait_ge(s_list, 16)
            act.dma_start(t["step_nodes"][0:1, :], d["step_list"].rearrange("(a n) -> a n", a=1)).then_inc(s_row, 16)
            act.wait_ge(s_row, 16)

        @block.gpsimd
        def _(pool):
            pool.iota(tile_no_i[:], [[P, K]], base=1, channel_multiplier=1).then_inc(s_iota, 1)
            pool.iota(step_row_i[:], [[1, K * P]], base=0, channel_multiplier=0).then_inc(s_iota, 1)
            pool.wait_ge(s_tile, 2)
            for c in range(K):
                for a, (rows, dest) in enumerate(((d["src"], g_src), (d["dst"], g_dst), (d["ew"], g_ew))):
                    pool.indirect_dma_start(dest[:, c, :], None, rows,
                                            bass.IndirectOffsetOnAxis(ap=step_tile_i[:, c:c + 1], axis=0)
                                            ).then_inc(s_rows[a], 16)

        @block.vector
        def _(dve):
            n = [0]

            def link(ins):
                n[0] += 1
                ins.then_inc(s_chain, 1)
                dve.wait_ge(s_chain, n[0])

            dve.memset(ones_bf[:], 1.0).then_inc(s_entered, 1)
            dve.wait_ge(s_in, 16)
            link(dve.tensor_scalar(block_of_last[:], last_dst[:], 7, None, ALU.logical_shift_right))
            dve.wait_ge(s_iota, 2)
            link(dve.tensor_copy(tile_no[:], tile_no_i[:]))
            dve.tensor_copy(step_row[:], step_row_i[:]).then_inc(s_chain, 1)
            n[0] += 1
            link(dve.tensor_tensor(entry[:], block_of_last[:], tile_no[:], ALU.add))
            for c in range(K):
                dve.tensor_scalar(entered[:, c, :], step_row[:], entry[:, c:c + 1], None,
                                  ALU.is_ge).then_inc(s_entered, 1)
            link(dve.tensor_scalar(step_no[:], tile_no[:], -1.0, None, ALU.add))
            dve.wait_ge(s_count, 1)
            dve.tensor_copy(step_tile[:], count[:, 0:K]).then_inc(s_tile, 1)
            dve.tensor_copy(step_tile_i[:], count[:, 0:K]).then_inc(s_tile, 1)
            dve.wait_ge(s_tile, 2)
            link(dve.tensor_tensor(step_node[:], step_no[:], step_tile[:], ALU.subtract))
            link(dve.tensor_scalar(step_node[:], step_node[:], float(P), None, ALU.mult))
            dve.tensor_copy(step_node_i[:], step_node[:]).then_inc(s_node, 1)
            dve.wait_ge(s_rows[0], 16 * K)
            dve.tensor_copy(f_src[:], g_src[:]).then_inc(s_float[0], 1)
            dve.wait_ge(s_rows[1], 16 * K)
            for c in range(K):
                dve.tensor_scalar(f_dst[:, c, :], g_dst[:, c, :], step_node[:, c:c + 1], None,
                                  ALU.subtract).then_inc(s_float[1], 1)
            for g, (a, c0, c1) in enumerate(groups):
                dve.wait_ge(s_turned, g + 1)
                dest = (t["edge_src"], t["edge_dst"], t["edge_w"])[a]
                dve.tensor_copy(dest[:, c0 * P:c1 * P], turned[:, g % 4, 0:(c1 - c0) * P]).then_inc(s_out, 1)

        @block.tensor
        def _(pe):
            pe.wait_ge(s_entered, 1 + K)
            for c in range(K):
                for k in range(K):
                    last = pe.matmul(count[:, c:c + 1], entered[:, k, c * P:(c + 1) * P], ones_bf[:],
                                     start=(k == 0), stop=(k == K - 1))
            last.then_inc(s_count, 1)
            for g, (a, c0, c1) in enumerate(groups):
                if g == 0:
                    pe.wait_ge(s_float[0], 1)
                if c0 == 0 and a == 1:
                    pe.wait_ge(s_float[1], K)
                if c0 == 0 and a == 2:
                    pe.wait_ge(s_rows[2], 16 * K)
                if g >= 4:
                    pe.wait_ge(s_out, g - 3)
                rows = (f_src, f_dst, g_ew)[a]
                for c in range(c0, c1):
                    last = pe.transpose(turned[:, g % 4, (c - c0) * P:(c - c0 + 1) * P], rows[:, c, :], t["ident"][:])
                last.then_inc(s_turned, 1)


def project_input(nc, d, t):
    with phase(nc, "pi") as (sb, ps, sem, ctx):
        G = GROUP
        x = sb("x", [P, 2, G, C], F32)
        stats = sb("stats", [P, G, 6], F32)
        moments = sb("moments", [P, G, 2], F32)
        xn = sb("xn", [P, 2, G, C], F32)
        xnT = sb("xnT", [P, G, C], F32)
        biased = sb("biased", [P, 2, G, C], F32)
        h = sb("h", [P, 2, G, C], F32)
        w1 = sb("w1", [P, CG, C], F32)
        b1 = sb("b1", [P, C], F32)
        minus_half = sb("minus_half", [P, G], F32)
        turned = ps("turned", [P, 3, 512], F32)
        product = ps("product", [P, 4, 512], F32)
        s_w = sem("s_w")
        s_x = [sem("s_x0"), sem("s_x1")]
        s_stat = sem("s_stat")
        s_aggr = sem("s_aggr")
        s_var = sem("s_var")
        s_rstd = sem("s_rstd")
        s_kept = sem("s_kept")
        s_xn = sem("s_xn")
        s_turned = sem("s_turned")
        s_xnT = sem("s_xnT")
        s_product = sem("s_product")
        s_biased = sem("s_biased")
        s_h = sem("s_h")
        s_stored = [sem("s_stored0"), sem("s_stored1")]
        s_half = sem("s_half")
        passed = sem("passed")
        x_view = d["x"].rearrange("(n p) c -> p n c", p=P)
        h_view = d["h"].rearrange("(n p) c -> p n c", p=P)
        block = ctx.enter_context(nc.Block())

        @block.sync
        def _(sp):
            sp.dma_start(w1[:], d["c1_w1"].rearrange("(k p) c -> p k c", p=P)).then_inc(s_w, 16)
            sp.dma_start(b1[:], d["c1_b1"].partition_broadcast(P)).then_inc(s_w, 16)
            sp.sem_inc(s_xn, 2 * G)
            with sp.Fori(0, GROUPS // 2) as i:
                for u in range(2):
                    sp.wait_ge(s_xn, (i * 2 + u + 1) * G)
                    sp.dma_start(x[:, u, :, :], x_view[:, bass.ds((i * 2 + u) * G, G), :]).then_inc(s_x[u], 16)
            sp.wait_ge(s_w, 32)

        @block.vector
        def _(dve):
            dve.wait_ge(s_w, 32)
            dve.sem_inc(s_biased, 4)

            def normalize(i, g, u):
                gate(dve, s_x[u], i * 16 + 16, passed)
                for j in range(G):
                    dve.bn_stats(stats[:, j, :], x[:, u, j, :]).then_inc(s_stat, 1)
                for j in range(G):
                    gate(dve, s_stat, g * G + j + 1, passed)
                    dve.bn_aggr(moments[:, j, :], stats[:, j, :]).then_inc(s_aggr, 1)
                gate(dve, s_aggr, (g + 1) * G, passed)
                dve.tensor_scalar(moments[:, :, 1], moments[:, :, 1], EPS, None, ALU.add).then_inc(s_var, 1)

            def scale(i, g, u):
                gate(dve, s_rstd, g + 1, passed)
                dve.tensor_copy(t["node_stats"][:, bass.ds(g * (2 * G), 2 * G)],
                                moments[:].rearrange("p g s -> p (g s)")).then_inc(s_kept, 1)
                for j in range(G):
                    dve.tensor_scalar(xn[:, u, j, :], x[:, u, j, :], moments[:, j, 0:1], moments[:, j, 1:2],
                                      ALU.subtract, ALU.mult).then_inc(s_xn, 1)
                gate(dve, s_kept, g + 1, passed)
                gate(dve, s_xn, (g + 3) * G, passed)

            def bias(g, u):
                for j in range(G):
                    n = g * G + j
                    dve.wait_ge(s_product, G + n + 1)
                    dve.wait_ge(s_h, n + 1)
                    dve.tensor_tensor(biased[:, u, j, :], product[:, j % 4, 0:C], b1[:], ALU.add).then_inc(s_biased, 1)

            normalize(0, 0, 0)
            scale(0, 0, 0)
            with dve.Fori(0, GROUPS // 2 - 1) as i:
                normalize(i, i * 2 + 1, 1)
                bias(i * 2, 0)
                scale(i, i * 2 + 1, 1)
                normalize(i + 1, i * 2 + 2, 0)
                bias(i * 2 + 1, 1)
                scale(i + 1, i * 2 + 2, 0)
            normalize(GROUPS // 2 - 1, GROUPS - 1, 1)
            bias(GROUPS - 2, 0)
            scale(GROUPS // 2 - 1, GROUPS - 1, 1)
            bias(GROUPS - 1, 1)

        @block.gpsimd
        def _(pool):
            pool.memset(minus_half[:], -0.5).then_inc(s_half, 1)
            pool.wait_ge(s_half, 1)

            def zero_sums(tile, tiles):
                pool.memset(t["sums"][:, :, tile * P:(tile + tiles) * P], 0.0)

            zero_sums(NODE_TILES, 1)
            for g in range(GROUPS):
                gate(pool, s_var, g + 1, passed)
                pool.tensor_tensor(moments[:, :, 1], moments[:, :, 1], minus_half[:], ALU.pow).then_inc(s_rstd, 1)
                zero_sums(g * G, G)

        @block.tensor
        def _(pe):
            pe.wait_ge(s_w, 32)
            pe.sem_inc(s_product, G)

            def multiply(g, u, j):
                n = g * G + j
                pe.wait_ge(s_xnT, 3 + n + 1)
                pe.wait_ge(s_biased, bank_free(g, j))
                for k in range(CG):
                    last = pe.matmul(product[:, j % 4, 0:C], xnT[:, j, k * P:(k + 1) * P], w1[:, k, :],
                                     start=(k == 0), stop=(k == CG - 1))
                last.then_inc(s_product, 1)

            def bank_free(g, j):
                return 4 + g * G + (j - 3 if j > 3 else 0)

            with pe.Fori(0, GROUPS // 2) as i:
                for u in range(2):
                    g = i * 2 + u
                    for j in range(G):
                        n = g * G + j
                        pe.wait_ge(s_xn, 2 * G + n + 1)
                        pe.wait_ge(s_xnT, 3 + g * G + (j - 2 if j > 2 else 0))
                        for k in range(CG):
                            last = pe.transpose(turned[:, j % 3, k * P:(k + 1) * P], xn[:, u, j, k * P:(k + 1) * P],
                                                t["ident"][:])
                        last.then_inc(s_turned, 1)
                        if j > 0:
                            multiply(g, u, j - 1)
                    multiply(g, u, G - 1)

        @block.scalar
        def _(act):
            act.preload_act_table(ACT.Relu)
            act.sem_inc(s_xnT, 3)
            act.sem_inc(s_h, 2 * G)
            for u in range(2):
                act.sem_inc(s_stored[u], 16)

            def relu(i, g, u, j):
                n = g * G + j
                act.wait_ge(s_biased, 4 + n + 1)
                act.activation(h[:, u, j, :], biased[:, u, j, :], ACT.Relu).then_inc(s_h, 1)

            def copy_out(g, j):
                n = g * G + j
                act.wait_ge(s_turned, n + 1)
                act.wait_ge(s_product, n + 1)
                act.activation(xnT[:, j, :], turned[:, j % 3, 0:C], ACT.Copy).then_inc(s_xnT, 1)

            def store(g, u):
                act.wait_ge(s_h, (g + 3) * G)
                act.dma_start(h_view[:, bass.ds(g * G, G), :], h[:, u, :, :]).then_inc(s_stored[u], 16)

            def group(i, g, u, former):
                for j in range(G):
                    copy_out(g, j)
                if former is not None:
                    gate(act, s_stored[1 - u], former * 16 + 16, passed)
                    for j in range(G):
                        relu(i, g - 1, 1 - u, j)
                    store(g - 1, 1 - u)

            group(0, 0, 0, None)
            with act.Fori(0, GROUPS // 2 - 1) as i:
                group(i, i * 2 + 1, 1, i)
                group(i, i * 2 + 2, 0, i)
            group(0, GROUPS - 1, 1, GROUPS // 2 - 1)
            gate(act, s_stored[1], (GROUPS // 2 - 1) * 16 + 16, passed)
            for j in range(G):
                relu(0, GROUPS - 1, 1, j)
            store(GROUPS - 1, 1)
            for u in range(2):
                act.wait_ge(s_stored[u], 16 * (GROUPS // 2 + 1))


def sum_messages(nc, d, t, source, name, first_step, rounds):
    with phase(nc, name) as (sb, ps, sem, ctx):
        messages = sb("messages", [P, RING, C], F32)
        indices = sb("indices", [P, 2, HALF], I32)
        onehot = sb("onehot", [P, LEAD, P], F32)
        partial = ps("partial", [P, SUM_BANKS, 512], F32)
        s_message = [sem(f"s_message{k}") for k in range(RING)]
        s_index = sem("s_index")
        s_onehot = sem("s_onehot")
        s_multiplied = sem("s_multiplied")
        s_added = sem("s_added")
        passed = sem("passed")
        sums = t["sums"]
        block = ctx.enter_context(nc.Block())

        @block.sync
        def _(sp):
            sp.wait_ge(s_added, SUM_BANKS + rounds * RING)

        @block.scalar
        def _(act):
            with act.Fori(0, rounds) as i:
                for half in range(2):
                    first = i * RING + half * HALF
                    gate(act, s_multiplied, first + HALF, passed)
                    act.activation(indices[:, half, :], t["edge_src"][:, bass.ds(first_step + first, HALF)],
                                   ACT.Copy).then_inc(s_index, 1)

        @block.gpsimd
        def _(pool):
            with pool.Fori(0, rounds) as i:
                for k in range(RING):
                    if k % HALF == 0:
                        gate(pool, s_index, i * 2 + k // HALF + 1, passed)
                    pool.indirect_dma_start(messages[:, k, :], None, source,
                                            bass.IndirectOffsetOnAxis(ap=indices[:, k // HALF, k % HALF:k % HALF + 1],
                                                                      axis=0)).then_inc(s_message[k], 16)

        @block.tensor
        def _(pe):
            pe.sem_inc(s_multiplied, RING)
            with pe.Fori(0, rounds) as i:
                for k in range(RING):
                    n = i * RING + k
                    pe.wait_ge(s_onehot, n + 1)
                    pe.wait_ge(s_added, n + 1)
                    pe.wait_ge(s_message[k], i * 16 + 16)
                    for g in range(CG):
                        last = pe.matmul(partial[:, k % SUM_BANKS, g * P:(g + 1) * P],
                                         messages[:, k, g * P:(g + 1) * P], onehot[:, k % LEAD, :],
                                         start=True, stop=True)
                    last.then_inc(s_multiplied, 1)

        @block.vector
        def _(dve):
            def build(slot, step):
                return dve.tensor_scalar(onehot[:, slot, :], t["iota"][:], t["edge_dst"][:, bass.ds(first_step + step, 1)],
                                         t["edge_w"][:, bass.ds(first_step + step, 1)], ALU.is_equal, ALU.mult)

            dve.sem_inc(s_added, SUM_BANKS)
            for k in range(LEAD):
                build(k, k).then_inc(s_onehot, 1)
            regs = [dve.alloc_register(f"{name}_node{k}") for k in range(4)]
            with dve.Fori(0, rounds) as i:
                for k in range(RING):
                    n = i * RING + k
                    if k % 4 == 0:
                        dve.load(regs, t["step_nodes"][0:1, bass.ds(first_step + n, 4)])
                        nodes = [dve.snap(r, min_val=0, max_val=NODES_PAD - 1) for r in regs]
                    where = sums[:, :, bass.ds(nodes[k % 4], P)]
                    dve.wait_ge(s_multiplied, RING + n + 1)
                    dve.wait_ge(s_added, SUM_BANKS + n)
                    dve.tensor_tensor(where, where, partial[:, k % SUM_BANKS, 0:C].rearrange("p (g n) -> p g n", g=CG),
                                      ALU.add).then_inc(s_added, 1)
                    build(k % LEAD, n + LEAD).then_inc(s_onehot, 1)


def normalize_sums(nc, d, t, layer):
    with phase(nc, layer + "_ns") as (sb, ps, sem, ctx):
        U = 2
        sums = t["sums"]
        w2 = sb("w2", [P, CG, C], F32)
        w2_high = sb("w2_high", [P, CG, C], F32R)
        w2_low = sb("w2_low", [P, CG, C], F32R)
        high = sb("high", [P, U, CG, COLS], F32R)
        low = sb("low", [P, U, CG, COLS], F32R)
        b2 = sb("b2", [P, CG], F32)
        gains = sb("gains", [P, 2, CG], F32)
        shifts = sb("shifts", [P, 2, CG], F32)
        stats = sb("stats", [P, CG, CHUNKS + 1, 6], F32)
        moments = sb("moments", [P, CG, 2], F32)
        scale = sb("scale", [P, CG], F32)
        shift = sb("shift", [P, CG], F32)
        product = sb("product", [P, CG], F32)
        z = ps("z", [P, U * CG, 512], F32)
        s_w = sem("s_w")
        s_w_high = sem("s_w_high")
        s_w_low = sem("s_w_low")
        s_high = sem("s_high")
        s_low = sem("s_low")
        s_z = sem("s_z")
        s_biased = sem("s_biased")
        s_stats = sem("s_stats")
        s_var = sem("s_var")
        s_rstd = sem("s_rstd")
        s_chain = sem("s_chain")
        s_first = sem("s_first")
        s_relu = sem("s_relu")
        passed = sem("passed")
        block = ctx.enter_context(nc.Block())

        def over_chunks(eng, body):
            with eng.Fori(0, CHUNKS // U) as i:
                for u in range(U):
                    body(i * U + u, u, (i * U + u) * COLS, COLS)
            body(CHUNKS, 0, CHUNKS * COLS, REST)

        def over_chunks_lagging(eng, split, finish):
            for u in range(U):
                split(u, u, u * COLS, COLS)
            with eng.Fori(1, CHUNKS // U) as i:
                for u in range(U):
                    chunk = i * U + u
                    split(chunk, u, chunk * COLS, COLS)
                    finish(chunk - U, u, (chunk - U) * COLS, COLS)
            split(CHUNKS, 0, CHUNKS * COLS, REST)
            for u in range(U):
                finish(CHUNKS - U + u, u, (CHUNKS - U + u) * COLS, COLS)
            finish(CHUNKS, 0, CHUNKS * COLS, REST)

        @block.sync
        def _(sp):
            sp.dma_start(w2[:], d[layer + "_w2"].rearrange("(k p) c -> p k c", p=P)).then_inc(s_w, 16)
            with nc.allow_non_contiguous_dma(reason="256 words, one for each channel"):
                sp.dma_start(b2[:], d[layer + "_b2"].rearrange("(k p) -> p k", p=P)).then_inc(s_w, 16)
                for n, bn in enumerate((layer, {"c1": "bn1", "c2": "bn2"}[layer])):
                    sp.dma_start(gains[:, n, :], d[bn + "_g"].rearrange("(k p) -> p k", p=P)).then_inc(s_w, 16)
                    sp.dma_start(shifts[:, n, :], d[bn + "_b"].rearrange("(k p) -> p k", p=P)).then_inc(s_w, 16)
            sp.wait_ge(s_w, 96)

        @block.tensor
        def _(pe):
            pe.wait_ge(s_w_low, 1)
            pe.sem_inc(s_z, U)

            def product_of(chunk, u, col, cols):
                pe.wait_ge(s_low, chunk + 1)
                pe.wait_ge(s_biased, (chunk + 1) * CG)
                parts = ((w2_high, high), (w2_low, high), (w2_high, low))
                for co in range(CG):
                    for k in range(CG):
                        for n, (w_part, part) in enumerate(parts):
                            last = pe.matmul(z[:, u * CG + co, 0:cols], w_part[:, k, co * P:(co + 1) * P],
                                             part[:, u, k, 0:cols], start=(k == 0 and n == 0),
                                             stop=(k == CG - 1 and n == 2))
                last.then_inc(s_z, 1)

            over_chunks(pe, product_of)

        @block.scalar
        def _(act):
            act.preload_act_table(ACT.Relu)
            act.sem_inc(s_biased, U * CG)
            act.wait_ge(s_w, 96)
            act.activation(w2_high[:], w2[:], ACT.Copy).then_inc(s_w_high, 1)

            def split_high(chunk, u, col, cols):
                gate(act, s_z, chunk + 1, passed)
                act.activation(high[:, u, :, 0:cols], sums[:, :, bass.ds(col, cols)], ACT.Copy).then_inc(s_high, 1)

            def add_bias(chunk, u, col, cols):
                gate(act, s_z, U + chunk + 1, passed)
                for co in range(CG):
                    act.activation(sums[:, co, bass.ds(col, cols)], z[:, u * CG + co, 0:cols], ACT.Identity,
                                   bias=b2[:, co:co + 1]).then_inc(s_biased, 1)

            def first_norm(chunk, u, col, cols):
                for co in range(CG):
                    v = sums[:, co, bass.ds(col, cols)]
                    act.activation(v, v, ACT.Relu, bias=shift[:, co:co + 1],
                                   scale=scale[:, co:co + 1]).then_inc(s_relu, 1)

            over_chunks_lagging(act, split_high, add_bias)
            act.wait_ge(s_first, 1)
            over_chunks(act, first_norm)

        @block.gpsimd
        def _(pool):
            for n in range(2):
                pool.wait_ge(s_var, n + 1)
                for co in range(CG):
                    pool.tensor_tensor(moments[:, co, 1:2], moments[:, co, 1:2], t["minus_half"][:],
                                       ALU.pow).then_inc(s_rstd, 1)

        @block.vector
        def _(dve):
            n = [0]

            def link(ins):
                n[0] += 1
                ins.then_inc(s_chain, 1)
                dve.wait_ge(s_chain, n[0])

            def statistics(ready, counted_from):
                def of_chunk(chunk, u, col, cols):
                    for co in range(CG):
                        gate(dve, ready, chunk * CG + (counted_from + co + 1), passed)
                        dve.bn_stats(stats[:, co, bass.ds(chunk, 1), :].rearrange("p a s -> p (a s)"),
                                     sums[:, co, bass.ds(col, cols)]).then_inc(s_stats, 1)
                return of_chunk

            def coefficients(which, to_scale, to_shift):
                dve.wait_ge(s_stats, (which + 1) * CG * (CHUNKS + 1))
                for co in range(CG):
                    link(dve.bn_aggr(moments[:, co, :], stats[:, co, :, :].rearrange("p a s -> p (a s)")))
                dve.tensor_scalar(moments[:, :, 1], moments[:, :, 1], EPS, None, ALU.add).then_inc(s_var, 1)
                dve.wait_ge(s_rstd, (which + 1) * CG)
                link(dve.tensor_tensor(to_scale, gains[:, which, :], moments[:, :, 1], ALU.mult))
                link(dve.tensor_tensor(product[:], moments[:, :, 0], to_scale, ALU.mult))
                return dve.tensor_tensor(to_shift, shifts[:, which, :], product[:], ALU.subtract)

            def split_low(chunk, u, col, cols):
                dve.wait_ge(s_high, chunk + 1)
                dve.tensor_tensor(low[:, u, :, 0:cols], sums[:, :, bass.ds(col, cols)],
                                  high[:, u, :, 0:cols].bitcast(F32), ALU.subtract).then_inc(s_low, 1)

            dve.wait_ge(s_w, 96)
            dve.wait_ge(s_w_high, 1)
            dve.tensor_tensor(w2_low[:], w2[:], w2_high[:].bitcast(F32), ALU.subtract).then_inc(s_w_low, 1)
            over_chunks_lagging(dve, split_low, statistics(s_biased, U * CG))
            coefficients(0, scale[:], shift[:]).then_inc(s_first, 1)
            over_chunks(dve, statistics(s_relu, 0))
            coefficients(1, t["bn_scale"][:], t["bn_shift"][:])


def project_hidden(nc, d, t):
    with phase(nc, "ph") as (sb, ps, sem, ctx):
        U = 2
        TILES = 4
        a = sb("a", [P, U, CG, COLS], F32)
        biased = sb("biased", [P, U, TILES, C], F32)
        h = sb("h", [P, U, TILES, C], F32)
        w1 = sb("w1", [P, CG, C], F32)
        b1 = sb("b1", [P, C], F32)
        product = ps("product", [P, TILES, 512], F32)
        s_w = sem("s_w")
        s_a = sem("s_a")
        s_product = sem("s_product")
        s_biased = sem("s_biased")
        s_h = sem("s_h")
        s_stored = [sem(f"s_stored{u}") for u in range(U)]
        passed = sem("passed")
        h_view = d["h2"].rearrange("(n p) c -> p n c", p=P)
        LAST = NODE_TILES - CHUNKS * TILES
        block = ctx.enter_context(nc.Block())

        def over_chunks(eng, body):
            with eng.Fori(0, CHUNKS // U) as i:
                for u in range(U):
                    body(i, i * U + u, u, TILES)
            body(CHUNKS // U, CHUNKS, 0, LAST)

        @block.sync
        def _(sp):
            sp.dma_start(w1[:], d["c2_w1"].rearrange("(k p) c -> p k c", p=P)).then_inc(s_w, 16)
            sp.dma_start(b1[:], d["c2_b1"].partition_broadcast(P)).then_inc(s_w, 16)
            for u in range(U):
                sp.sem_inc(s_stored[u], 16)

            def store(i, chunk, u, tiles):
                sp.wait_ge(s_h, (chunk + 1) * TILES if tiles == TILES else CHUNKS * TILES + LAST)
                sp.dma_start(h_view[:, bass.ds(chunk * TILES, tiles), :], h[:, u, 0:tiles, :]
                             ).then_inc(s_stored[u], 16)

            over_chunks(sp, store)
            sp.wait_ge(s_stored[0], 16 * (CHUNKS // U + 2))
            sp.wait_ge(s_stored[1], 16 * (CHUNKS // U + 1))
            sp.wait_ge(s_w, 32)

        @block.scalar
        def _(act):
            act.preload_act_table(ACT.Relu)

            def norm(i, chunk, u, tiles):
                gate(act, s_product, (chunk + 1) * TILES, passed)
                for k in range(CG):
                    act.activation(a[:, u, k, 0:tiles * P], t["sums"][:, k, bass.ds(chunk * COLS, tiles * P)],
                                   ACT.Relu, bias=t["bn_shift"][:, k:k + 1],
                                   scale=t["bn_scale"][:, k:k + 1]).then_inc(s_a, 1)

            over_chunks(act, norm)

        @block.tensor
        def _(pe):
            pe.wait_ge(s_w, 32)
            pe.sem_inc(s_product, U * TILES)

            def multiply(i, chunk, u, tiles):
                for j in range(tiles):
                    n = chunk * TILES + j
                    if j == 0:
                        pe.wait_ge(s_a, (chunk + 1) * CG)
                    pe.wait_ge(s_biased, n + 1)
                    for k in range(CG):
                        last = pe.matmul(product[:, j, 0:C], a[:, u, k, j * P:(j + 1) * P], w1[:, k, :],
                                         start=(k == 0), stop=(k == CG - 1))
                    last.then_inc(s_product, 1)

            over_chunks(pe, multiply)

        @block.vector
        def _(dve):
            dve.wait_ge(s_w, 32)
            dve.sem_inc(s_biased, TILES)

            def bias(i, chunk, u, tiles):
                for j in range(tiles):
                    n = chunk * TILES + j
                    dve.wait_ge(s_product, U * TILES + n + 1)
                    if j == 0:
                        dve.wait_ge(s_stored[u], i * 16 + 16)
                    dve.tensor_tensor(biased[:, u, j, :], product[:, j, 0:C], b1[:], ALU.add).then_inc(s_biased, 1)
                dve.wait_ge(s_a, (chunk + 1) * CG)
                dve.tensor_scalar(t["sums"][:, :, bass.ds(chunk * COLS, tiles * P)],
                                  t["zeros"][:, 0:1].unsqueeze(1).to_broadcast([P, CG, tiles * P]), 0.0, None, ALU.add)

            over_chunks(dve, bias)

        @block.gpsimd
        def _(pool):
            def relu(i, chunk, u, tiles):
                for j in range(tiles):
                    gate(pool, s_biased, TILES + chunk * TILES + j + 1, passed)
                    if j == 0:
                        gate(pool, s_stored[u], i * 16 + 16, passed)
                    pool.tensor_scalar(h[:, u, j, :], biased[:, u, j, :], 0.0, None, ALU.max).then_inc(s_h, 1)

            over_chunks(pool, relu)


def route_tokens(nc, d, t):
    with phase(nc, "rt") as (sb, ps, sem, ctx):
        G, E = GROUP, EXPERTS
        BANKS = (G + 1) // 2
        x = sb("x", [P, 2, G, C], F32)
        y = sb("y", [P, G, CG, P], F32)
        residual = sb("residual", [P, G, C], F32)
        x1 = sb("x1", [P, G, C], F32)
        l1 = sb("l1", [P, G, C], F32)
        tokens = sb("tokens", [P, G, C], F32)
        affine = sb("affine", [P, 2, CG, P], F32)
        stats = sb("stats", [P, G, 6], F32)
        moments = sb("moments", [P, 2, G, 2], F32)
        down = sb("down", [P, 2, G], F32)
        wr = sb("wr", [P, CG, E], F32)
        br = sb("br", [P, G, E], F32)
        minus_half = sb("minus_half", [P, G], F32)
        logits = sb("logits", [P, G, E], F32)
        top = sb("top", [P, G, E], F32)
        which = sb("which", [P, G, E], U32)
        which_f = sb("which_f", [P, G, E], F32)
        experts_i = sb("experts_i", [P, G, E], I32)
        experts = sb("experts", [P, G, E], F32)
        slots_of = sb("slots_of", [P, G, E], F32)
        chosen = sb("chosen", [P, 2, G, E], F32)
        both = sb("both", [P, G, E], F32)
        of_group = sb("of_group", [P, E], F32)
        carried = sb("carried", [P, E], F32)
        place = sb("place", [P, G, E], F32)
        picked = sb("picked", [P, 2, G, E], F32)
        slot_f = sb("slot_f", [P, 2, G], F32)
        slot = sb("slot", [P, 2, 2, G], I32)
        gap = sb("gap", [P, G], F32)
        ratio = sb("ratio", [P, G], F32)
        total = sb("total", [P, G], F32)
        token_i = sb("token_i", [P, G], I32)
        entry = sb("entry", [P, 2, 2, G, 2], I32)
        primer = sb("primer", [P, 2, 2], I32)
        ps_y = ps("ps_y", [P, BANKS, 2, C], F32)
        ps_t = ps("ps_t", [P, 2, 512], F32)
        ps_l = ps("ps_l", [P, 512], F32)
        ps_c = ps("ps_c", [P, 512], F32)

        s_w = sem("s_w")
        s_const = sem("s_const")
        s_const2 = sem("s_const2")
        s_x = [sem("s_x_in0"), sem("s_x_in1")]
        s_y = sem("s_y")
        s_turned = sem("s_turned")
        s_read = sem("s_read")
        s_res = sem("s_res")
        s_x1 = sem("s_x1")
        s_x1_stored = sem("s_x1_stored")
        s_stat = sem("s_stat")
        s_aggr = sem("s_aggr")
        s_var = sem("s_var")
        s_rstd = sem("s_rstd")
        s_down = sem("s_down")
        s_l1 = sem("s_l1")
        s_token = sem("s_token")
        s_token_stored = sem("s_token_stored")
        s_back = sem("s_back")
        s_affine = sem("s_affine")
        s_logit = sem("s_logit")
        s_chain = sem("s_chain")
        s_gap = sem("s_gap")
        s_ratio = sem("s_ratio")
        s_both = sem("s_both")
        s_place = sem("s_place")
        s_entry = sem("s_entry")
        s_scatter = [sem("s_scatter0"), sem("s_scatter1")]
        passed = sem("passed")
        x_view = d["x"].rearrange("(n p) c -> p n c", p=P)
        out_view = d["out"].rearrange("(n p) c -> p n c", p=P)
        token_view = d["tokens"].rearrange("(n p) c -> p n c", p=P)
        block = ctx.enter_context(nc.Block())

        def over_groups(eng, body):
            for g in (0, 1):
                body(0, g, g)
            with eng.Fori(1, GROUPS // 2 - 1) as r:
                for u in range(2):
                    body(r, r * 2 + u, u)
            for g in (GROUPS - 2, GROUPS - 1):
                body(GROUPS // 2 - 1, g, g % 2)

        def is_group(g, which):
            return isinstance(g, int) and g == which

        @block.sync
        def _(sp):
            sp.dma_start(wr[:], d["wr"].rearrange("(k p) e -> p k e", p=P)).then_inc(s_w, 16)
            for g in range(G):
                sp.dma_start(br[:, g, :], d["br"].partition_broadcast(P)).then_inc(s_w, 16)
            sp.sem_inc(s_x1, 2)
            sp.sem_inc(s_x1_stored, 16)
            sp.sem_inc(s_token_stored, 16)

            def move(g, u):
                sp.wait_ge(s_x1, g + 1)
                sp.dma_start(x[:, u, :, :], x_view[:, bass.ds(g * G, G), :]).then_inc(s_x[u], 16)

            def store(g):
                sp.wait_ge(s_x1, 2 + g + 1)
                sp.dma_start(out_view[:, bass.ds(g * G, G), :], x1[:]).then_inc(s_x1_stored, 16)
                sp.wait_ge(s_token, (g + 1) * G)
                sp.dma_start(token_view[:, bass.ds(g * G, G), :], tokens[:]).then_inc(s_token_stored, 16)

            move(0, 0)
            with sp.Fori(0, GROUPS // 2 - 1) as i:
                move(i * 2 + 1, 1)
                store(i * 2)
                move(i * 2 + 2, 0)
                store(i * 2 + 1)
            move(GROUPS - 1, 1)
            store(GROUPS - 2)
            store(GROUPS - 1)
            sp.wait_ge(s_x1_stored, 16 * (GROUPS + 1))
            sp.wait_ge(s_token_stored, 16 * (GROUPS + 1))

        @block.scalar
        def _(act):
            act.wait_ge(s_w, 16 * (G + 1))

            def batch_norm(g):
                gate(act, s_turned, (g + 1) * G, passed)
                for j in range(G):
                    for k in range(CG):
                        act.activation(y[:, j, k, :], t["sums"][:, k, bass.ds((g * G + j) * P, P)], ACT.Identity,
                                       bias=t["bn_shift"][:, k:k + 1], scale=t["bn_scale"][:, k:k + 1]
                                       ).then_inc(s_y, 1)

            def ratio_of(g):
                act.wait_ge(s_gap, g + 1)
                act.activation(ratio[:], gap[:], ACT.Exp).then_inc(s_ratio, 1)

            def turn_affine(g, u, j):
                n = g * G + j
                act.wait_ge(s_back, 2 + n + 1)
                for k in range(CG):
                    act.activation(affine[:, (u + j) % 2, k, :], ps_t[:, (u + j) % 2, k * P:(k + 1) * P], ACT.Identity,
                                   bias=t["beta"][:, k:k + 1], scale=t["gamma"][:, k:k + 1]).then_inc(s_affine, 1)

            def body(r, g, u):
                if not is_group(g, 0):
                    ratio_of(g - 1)
                act.wait_ge(s_down, g * 2 + 1)
                for j in range(G):
                    act.activation(l1[:, j, :], x1[:, j, :], ACT.Identity, bias=down[:, 0, j:j + 1],
                                   scale=moments[:, 0, j, 1:2]).then_inc(s_l1, 1)
                if not is_group(g, GROUPS - 1):
                    batch_norm(g + 1)
                act.wait_ge(s_down, g * 2 + 2)
                gate(act, s_token_stored, g * 16 + 16, passed)
                for j in range(G):
                    act.activation(tokens[:, j, :], l1[:, j, :], ACT.Identity, bias=down[:, 1, j:j + 1],
                                   scale=moments[:, 1, j, 1:2]).then_inc(s_token, 1)
                    if j > 0:
                        turn_affine(g, u, j - 1)
                turn_affine(g, u, G - 1)

            act.preload_act_table(ACT.Exp)
            batch_norm(0)
            over_groups(act, body)
            ratio_of(GROUPS - 1)

        @block.tensor
        def _(pe):
            pe.wait_ge(s_w, 16 * (G + 1))
            pe.sem_inc(s_turned, G)
            pe.sem_inc(s_back, 2)

            def logit(g, u, j):
                n = g * G + j
                pe.wait_ge(s_affine, (n + 1) * CG)
                for k in range(CG):
                    last = pe.matmul(ps_l[:, j * E:(j + 1) * E], affine[:, (u + j) % 2, k, :], wr[:, k, :],
                                     start=(k == 0), stop=(k == CG - 1))
                last.then_inc(s_logit, 1)

            def turn(g):
                for j in range(G):
                    n = g * G + j
                    pe.wait_ge(s_y, (n + 1) * CG)
                    if j % 2 == 0:
                        pe.wait_ge(s_read, g * BANKS + j // 2 + 1)
                    for k in range(CG):
                        last = pe.transpose(ps_y[:, j // 2, j % 2, k * P:(k + 1) * P], y[:, j, k, :], t["ident"][:])
                    last.then_inc(s_turned, 1)

            def count(g):
                pe.wait_ge(s_both, g + 2)
                pe.matmul(ps_c[:, 0:G * E], t["before"][:], both[:].rearrange("p g e -> p (g e)"),
                          start=True, stop=False)
                for j in range(1, G):
                    pe.matmul(ps_c[:, j * E:G * E], t["ones"][:],
                              both[:, 0:G - j, :].rearrange("p g e -> p (g e)"), start=False, stop=False)
                for j in range(G):
                    last = pe.matmul(ps_c[:, j * E:(j + 1) * E], t["ones"][:], carried[:], start=False, stop=j == G - 1)
                last.then_inc(s_place, 1)

            def body(r, g, u):
                if not is_group(g, 0):
                    count(g - 1)
                if not is_group(g, GROUPS - 1):
                    turn(g + 1)
                for j in range(G):
                    n = g * G + j
                    pe.wait_ge(s_token, n + 1)
                    if j == 0:
                        pe.wait_ge(s_both, g + 1)
                    if j > 1:
                        pe.wait_ge(s_affine, (n - 1) * CG)
                    for k in range(CG):
                        last = pe.transpose(ps_t[:, (u + j) % 2, k * P:(k + 1) * P],
                                            tokens[:, j, k * P:(k + 1) * P], t["ident"][:])
                    last.then_inc(s_back, 1)
                    if j > 0:
                        logit(g, u, j - 1)
                logit(g, u, G - 1)

            turn(0)
            over_groups(pe, body)
            count(GROUPS - 1)

        @block.gpsimd
        def _(pool):
            pool.iota(experts_i[:], [[0, G], [1, E]], base=0, channel_multiplier=0).then_inc(s_const, 1)
            pool.iota(token_i[:], [[P, G]], base=-GROUP * P, channel_multiplier=1).then_inc(s_const, 1)
            pool.memset(minus_half[:], -0.5).then_inc(s_const, 1)
            pool.memset(carried[:], 0.0).then_inc(s_const, 1)
            pool.wait_ge(s_const, 4)
            for u in range(2):
                pool.dma_start(primer[:, u, :], d["src"][0:P, 0:2]).then_inc(s_scatter[u], 16 * 2 * G)

            def power(g, norm):
                gate(pool, s_var, g * 2 + norm + 1, passed)
                pool.tensor_tensor(moments[:, norm, :, 1], moments[:, norm, :, 1], minus_half[:],
                                   ALU.pow).then_inc(s_rstd, 1)

            def scatter(g, u, first, end):
                if first == 0:
                    gate(pool, s_entry, g + 1, passed)
                for n in range(first, end):
                    j, c = divmod(n, 2)
                    pool.indirect_dma_start(d["table"], bass.IndirectOffsetOnAxis(ap=slot[:, u, c, j:j + 1], axis=0),
                                            entry[:, u, c, j, :], None).then_inc(s_scatter[u], 16)

            def body(r, g, u):
                power(g, 0)
                if not is_group(g, 0) and not is_group(g, 1):
                    scatter(g - 2, u, SCATTER_FIRST, 2 * G)
                power(g, 1)
                if not is_group(g, 0):
                    scatter(g - 1, 1 - u, 0, SCATTER_FIRST)

            over_groups(pool, body)
            scatter(GROUPS - 2, 0, SCATTER_FIRST, 2 * G)
            scatter(GROUPS - 1, 1, 0, 2 * G)
            for u in range(2):
                pool.wait_ge(s_scatter[u], 16 * 2 * G * (GROUPS // 2 + 1))

        @block.vector
        def _(dve):
            dve.wait_ge(s_const, 4)
            dve.tensor_copy(experts[:], experts_i[:]).then_inc(s_const2, 1)
            dve.wait_ge(s_const2, 1)
            dve.tensor_scalar(slots_of[:], experts[:], float(NODES_PAD), None, ALU.mult).then_inc(s_const2, 1)
            dve.wait_ge(s_const2, 2)
            dve.sem_inc(s_both, 1)
            dve.sem_inc(s_read, BANKS)
            links = LINKS_ROUTE

            n = [0]

            def link(g, ins):
                n[0] += 1
                ins.then_inc(s_chain, 1)
                dve.wait_ge(s_chain, g * links + n[0])

            def add_residual(r, g, u):
                gate(dve, s_x[u], r * 16 + 16, passed)
                for j in range(G):
                    node = g * G + j
                    dve.tensor_scalar(residual[:, j, :], x[:, u, j, :], t["node_stats"][:, bass.ds(node * 2, 1)],
                                      t["node_stats"][:, bass.ds(node * 2 + 1, 1)], ALU.subtract,
                                      ALU.mult).then_inc(s_res, 1)
                for bank in range(BANKS):
                    first, end = bank * 2, min(bank * 2 + 2, G)
                    dve.wait_ge(s_res, g * G + end)
                    dve.wait_ge(s_turned, G + g * G + end)
                    dve.tensor_tensor(residual[:, first:end, :], ps_y[:, bank, 0:end - first, :],
                                      residual[:, first:end, :], ALU.add).then_inc(s_read, 1)
                gate(dve, s_x1_stored, g * 16 + 16, passed)
                dve.wait_ge(s_read, (g + 2) * BANKS)
                dve.scalar_tensor_tensor(x1[:], residual[:], 0.0, x[:, u, :, :], ALU.max, ALU.add).then_inc(s_x1, 1)

            def variances(g, which, rows):
                for j in range(G):
                    if which == 0 and j == 0:
                        gate(dve, s_x1, 2 + g + 1, passed)
                    if which == 1:
                        dve.wait_ge(s_l1, g * G + j + 1)
                    dve.bn_stats(stats[:, j, :], rows[:, j, :]).then_inc(s_stat, 1)
                for j in range(G):
                    gate(dve, s_stat, g * 2 * G + which * G + j + 1, passed)
                    dve.bn_aggr(moments[:, which, j, :], stats[:, j, :]).then_inc(s_aggr, 1)
                dve.wait_ge(s_aggr, (g * 2 + which + 1) * G)
                var = moments[:, which, :, 1]
                dve.tensor_scalar(var, var, EPS, None, ALU.add).then_inc(s_var, 1)

            def shift_down(g, which):
                dve.wait_ge(s_rstd, g * 2 + which + 1)
                dve.scalar_tensor_tensor(down[:, which, :], moments[:, which, :, 0], -1.0, moments[:, which, :, 1],
                                         ALU.mult, ALU.mult).then_inc(s_down, 1)

            def choose(g):
                n[0] = 0
                gate(dve, s_logit, (g + 1) * G, passed)
                dve.tensor_tensor(logits[:], ps_l[:, 0:G * E].rearrange("p (g e) -> p g e", g=G), br[:],
                                  ALU.add).then_inc(s_chain, 1)
                n[0] += 1
                gate(dve, s_chain, g * links + n[0], passed)
                for j in range(G):
                    dve.max(top[:, j, :], logits[:, j, :]).then_inc(s_chain, 1)
                n[0] += G
                dve.wait_ge(s_chain, g * links + n[0])
                dve.tensor_tensor(gap[:], top[:, :, 1], top[:, :, 0], ALU.subtract).then_inc(s_gap, 1)
                for j in range(G):
                    dve.max_index(which[:, j, :], top[:, j, :], logits[:, j, :]).then_inc(s_chain, 1)
                n[0] += G
                dve.wait_ge(s_chain, g * links + n[0])
                link(g, dve.tensor_copy(which_f[:], which[:]))
                for c in range(2):
                    dve.tensor_tensor(chosen[:, c, :, :], experts[:], which_f[:, :, c:c + 1].to_broadcast([P, G, E]),
                                      ALU.is_equal).then_inc(s_chain, 1)
                n[0] += 2
                dve.wait_ge(s_chain, g * links + n[0])
                dve.tensor_tensor(both[:], chosen[:, 0, :, :], chosen[:, 1, :, :], ALU.add).then_inc(s_both, 1)

            def weigh(r, g, u):
                dve.wait_ge(s_ratio, g + 1)
                link(g, dve.tensor_scalar(total[:], ratio[:], 1.0, None, ALU.add))
                gate(dve, s_scatter[u], (r + 1) * (16 * 2 * G), passed)
                weight = entry[:, u, :, :, :].bitcast(F32)
                link(g, dve.reciprocal(weight[:, 0, :, 1], total[:]))
                dve.tensor_tensor(weight[:, 1, :, 1], weight[:, 0, :, 1], ratio[:], ALU.mult).then_inc(s_chain, 1)
                dve.tensor_scalar(token_i[:], token_i[:], float(G * P), None, ALU.add).then_inc(s_chain, 1)
                n[0] += 2
                dve.wait_ge(s_chain, g * links + n[0])
                for c in range(2):
                    dve.tensor_copy(entry[:, u, c, :, 0], token_i[:]).then_inc(s_chain, 1)
                dve.wait_ge(s_both, g + 2)
                dve.tensor_reduce(of_group[:], both[:].rearrange("p g e -> p e g"), mybir.AxisListType.X,
                                  ALU.add).then_inc(s_chain, 1)
                n[0] += 3

            def find_slots(g, u):
                dve.wait_ge(s_place, g + 1)
                link(g, dve.tensor_tensor(place[:], ps_c[:, 0:G * E].rearrange("p (g e) -> p g e", g=G), slots_of[:],
                                          ALU.add))
                for c in range(2):
                    dve.tensor_tensor(picked[:, c, :, :], place[:], chosen[:, c, :, :], ALU.mult).then_inc(s_chain, 1)
                dve.tensor_tensor(carried[:], carried[:], of_group[:], ALU.add).then_inc(s_chain, 1)
                n[0] += 3
                dve.wait_ge(s_chain, g * links + n[0])
                link(g, dve.tensor_reduce(slot_f[:], picked[:], mybir.AxisListType.X, ALU.add))
                dve.tensor_copy(slot[:, u, :, :], slot_f[:]).then_inc(s_entry, 1)
                assert n[0] == links, n[0]

            def body(r, g, u):
                former = r if u == 1 else r - 1
                routes = not is_group(g, 0)
                add_residual(r, g, u)
                variances(g, 0, x1)
                if routes:
                    choose(g - 1)
                shift_down(g, 0)
                if routes:
                    weigh(former, g - 1, 1 - u)
                variances(g, 1, l1)
                if routes:
                    find_slots(g - 1, 1 - u)
                shift_down(g, 1)

            over_groups(dve, body)
            choose(GROUPS - 1)
            weigh(GROUPS // 2 - 1, GROUPS - 1, 1)
            find_slots(GROUPS - 1, 1)
            dve.tensor_copy(t["chosen_by"][:], carried[:]).then_inc(s_const2, 1)
            dve.wait_ge(s_const2, 3)


LINKS_ROUTE = 4 + 2 * GROUP + 7 + 5
SCATTER_FIRST = 9


def list_tiles(nc, d, t):
    with phase(nc, "lt") as (sb, ps, sem, ctx):
        E, L = EXPERTS, FFN_LIST
        counts_ps = ps("counts_ps", [P, 512], F32)
        counts = sb("counts", [P, E], I32)
        tiles_i = sb("tiles_i", [P, E], I32)
        tiles = sb("tiles", [P, E], F32)
        base = sb("base", [P, E], F32)
        tile_i = sb("tile_i", [P, L], I32)
        tile_no = sb("tile_no", [P, L], F32)
        within = sb("within", [P, L], F32)
        entered = sb("entered", [P, L], F32)
        expert = sb("expert", [P, L], F32)
        first = sb("first", [P, L], F32)
        s_counts = sem("s_counts")
        s_iota = sem("s_iota")
        s_chain = sem("s_chain")
        block = ctx.enter_context(nc.Block())

        @block.sync
        def _(sp):
            biases, *weights = t["ffn_loaded"]
            sp.dma_start(t["ffn_b1"][:], d["b1"].rearrange("e h -> (e h)").partition_broadcast(P)).then_inc(biases, 16)
            sp.dma_start(t["ffn_b2"][:], d["b2"].rearrange("e c -> (e c)").partition_broadcast(P)).then_inc(biases, 16)
            for e in range(E):
                sp.dma_start(t["ffn_w1"][:, e * CG * HIDDEN:(e + 1) * CG * HIDDEN].rearrange("p (k h) -> p k h", k=CG),
                             d["w1"][e].rearrange("(k p) h -> p k h", p=P)).then_inc(weights[e], 16)
                sp.dma_start(t["ffn_w2"][:, e * HG * C:(e + 1) * HG * C].rearrange("p (k c) -> p k c", k=HG),
                             d["w2"][e].rearrange("(k p) c -> p k c", p=P)).then_inc(weights[e], 16)

        @block.tensor
        def _(pe):
            pe.matmul(counts_ps[:, 0:E], t["ones"][:], t["chosen_by"][:], start=True, stop=True).then_inc(s_counts, 1)

        @block.gpsimd
        def _(pool):
            pool.iota(tile_i[:], [[1, L]], base=0, channel_multiplier=0).then_inc(s_iota, 1)

        @block.vector
        def _(dve):
            n = [0]

            def link(ins):
                n[0] += 1
                ins.then_inc(s_chain, 1)
                dve.wait_ge(s_chain, n[0])

            dve.wait_ge(s_counts, 1)
            link(dve.tensor_scalar(counts[:], counts_ps[:, 0:E], float(P - 1), None, ALU.add))
            link(dve.tensor_scalar(tiles_i[:], counts[:], 7, None, ALU.logical_shift_right))
            link(dve.tensor_copy(tiles[:], tiles_i[:]))
            dve.wait_ge(s_iota, 1)
            link(dve.tensor_copy(tile_no[:], tile_i[:]))
            link(dve.tensor_copy(within[:], tile_i[:]))
            link(dve.memset(expert[:], 0.0))
            link(dve.memset(base[:], 0.0))
            for e in range(1, E):
                link(dve.tensor_tensor(base[:, e:e + 1], base[:, e - 1:e], tiles[:, e - 1:e], ALU.add))
                link(dve.tensor_scalar(entered[:], tile_no[:], base[:, e:e + 1], None, ALU.is_ge))
                link(dve.tensor_tensor(expert[:], expert[:], entered[:], ALU.add))
                link(dve.tensor_scalar(entered[:], entered[:], tiles[:, e - 1:e], None, ALU.mult))
                link(dve.tensor_tensor(within[:], within[:], entered[:], ALU.subtract))
            link(dve.tensor_scalar(first[:], within[:], float(P), None, ALU.mult))
            link(dve.scalar_tensor_tensor(first[:], expert[:], float(NODES_PAD), first[:], ALU.mult, ALU.add))
            link(dve.tensor_copy(t["tile_slot"][:], first[0:1, :]))
            link(dve.tensor_copy(t["tile_expert"][:], expert[0:1, :]))


TABLES = 12
ROWS_HELD = 6
GATHER_AHEAD = 5
TABLE_AHEAD = 8
FFN_ROUNDS = FFN_TILES // TABLES
assert FFN_ROUNDS * TABLES == FFN_TILES


def run_experts(nc, d, t):
    with phase(nc, "ffn") as (sb, ps, sem, ctx):
        E = EXPERTS
        w1, w2, b1, b2 = (t[f"ffn_{n}"] for n in ("w1", "w2", "b1", "b2"))
        w1_high = sb("w1_high", [P, E * CG * HIDDEN], F32R)
        w2_high = sb("w2_high", [P, E * HG * C], F32R)
        w1_low, w2_low = w1[:].bitcast(F32R), w2[:].bitcast(F32R)
        table = sb("table", [P, TABLES, 2], I32)
        rows = sb("rows", [P, ROWS_HELD, C], F32)
        xT = sb("xT", [P, 2, CG, P], F32)
        pre = sb("pre", [P, 2, HIDDEN], F32)
        hidden = sb("hidden", [P, 2, HIDDEN], F32)
        xT_high = sb("xT_high", [P, 2, CG, P], F32R)
        xT_low = sb("xT_low", [P, 2, CG, P], F32R)
        hT_high = sb("hT_high", [P, 2, HIDDEN], F32R)
        hT_low = sb("hT_low", [P, 2, HIDDEN], F32R)
        yb = sb("yb", [P, 2, C], F32)
        result = sb("result", [P, 2, C], F32)
        primer = sb("primer", [P, 2], I32)
        ps_x = ps("ps_x", [P, 512], F32)
        ps_1 = ps("ps_1", [P, 2, 512], F32)
        ps_h = ps("ps_h", [P, 2, 512], F32)
        ps_2 = ps("ps_2", [P, 2, 512], F32)
        s_biases, *s_weights = t["ffn_loaded"]
        s_high = sem("s_high")
        s_split = sem("s_split")
        s_xT_high = sem("s_xT_high")
        s_xT_low = sem("s_xT_low")
        s_hT_low = sem("s_hT_low")
        s_table = [sem(f"s_table{k}") for k in range(TABLES)]
        s_rows = [sem(f"s_rows{k}") for k in range(ROWS_HELD)]
        s_xturn = sem("s_xturn")
        s_xT = sem("s_xT")
        s_one = sem("s_one")
        s_pre = sem("s_pre")
        s_hidden = sem("s_hidden")
        s_hturn = sem("s_hturn")
        s_hT = sem("s_hT")
        s_two = sem("s_two")
        s_yb = sem("s_yb")
        s_result = sem("s_result")
        s_scatter = sem("s_scatter")
        s_free = sem("s_free")
        passed = sem("passed")
        block = ctx.enter_context(nc.Block())
        F = TABLES

        @block.sync
        def _(sp):
            def load(tile, k):
                first = sp.value_load(t["tile_slot"][0:1, bass.ds(tile, 1)], min_val=0, max_val=TABLE_ROWS - P)
                sp.dma_start(table[:, k, :], d["table"][bass.ds(first, P), :]).then_inc(s_table[k], 16)

            for k in range(TABLE_AHEAD):
                load(k, k)
            with sp.Fori(0, FFN_ROUNDS) as i:
                for k in range(F):
                    s = i * F + k
                    gate(sp, s_free, s + TABLE_AHEAD + 2, passed)
                    load(s + TABLE_AHEAD, (k + TABLE_AHEAD) % F)
            for k in range(F):
                sp.wait_ge(s_table[k], 16 * (FFN_ROUNDS + (1 if k < TABLE_AHEAD else 0)))

        @block.gpsimd
        def _(pool):
            def gather(k, round_, row_slot):
                gate(pool, s_table[k], round_ * 16 + 16, passed)
                pool.indirect_dma_start(rows[:, row_slot, :], None, d["tokens"],
                                        bass.IndirectOffsetOnAxis(ap=table[:, k, 0:1], axis=0)
                                        ).then_inc(s_rows[row_slot], 16)

            pool.dma_start(primer[:], d["src"][0:P, 0:2]).then_inc(s_scatter, 16)
            pool.sem_inc(s_free, TABLES)
            for k in range(GATHER_AHEAD):
                gather(k, 0, k)
            with pool.Fori(0, FFN_ROUNDS) as i:
                for k in range(F):
                    s = i * F + k
                    ahead = k + GATHER_AHEAD
                    gate(pool, s_xturn, s + GATHER_AHEAD + 1, passed)
                    gather(ahead % F, i + ahead // F, ahead % ROWS_HELD)
                    gate(pool, s_scatter, (s + 1) * 16, s_free)
                    gate(pool, s_result, 2 + s + 1, passed)
                    pool.indirect_dma_start(d["out"], bass.IndirectOffsetOnAxis(ap=table[:, k, 0:1], axis=0),
                                            result[:, k % 2, :], None, compute_op=ALU.add).then_inc(s_scatter, 16)
            pool.wait_ge(s_scatter, 16 * (1 + FFN_TILES))
            for k in range(ROWS_HELD):
                pool.wait_ge(s_rows[k], 16 * (2 * FFN_ROUNDS + (1 if k < GATHER_AHEAD else 0)))

        @block.tensor
        def _(pe):
            def turn_rows(s, k, round_):
                pe.wait_ge(s_rows[k % ROWS_HELD], round_ * 16 + 16)
                if not isinstance(s, int) or s > 0:
                    pe.wait_ge(s_xT, s * CG)
                for g in range(CG):
                    last = pe.transpose(ps_x[:, g * P:(g + 1) * P], rows[:, k % ROWS_HELD, g * P:(g + 1) * P],
                                        t["ident"][:])
                last.then_inc(s_xturn, 1)

            def expert_of(s):
                return pe.value_load(t["tile_expert"][0:1, bass.ds(s, 1)], min_val=0, max_val=E - 1)

            def first_product(s, q, e):
                pe.wait_ge(s_xT_low, s + 1)
                pe.wait_ge(s_pre, s + 1)
                parts = ((xT_high, w1_high), (xT_high, w1_low), (xT_low, w1_high))
                for g in range(CG):
                    for n, (rows_part, w_part) in enumerate(parts):
                        last = pe.matmul(ps_1[:, q, :], rows_part[:, q, g, :],
                                         w_part[:, bass.ds(e * (CG * HIDDEN) + g * HIDDEN, HIDDEN)],
                                         start=(g == 0 and n == 0), stop=(g == CG - 1 and n == 2))
                last.then_inc(s_one, 1)

            def turn_hidden(s, q):
                pe.wait_ge(s_hidden, 2 + s + 1)
                for g in range(HG):
                    last = pe.transpose(ps_h[:, q, g * P:(g + 1) * P], hidden[:, q, g * P:(g + 1) * P], t["ident"][:])
                last.then_inc(s_hturn, 1)

            def second_product(s, q, e):
                pe.wait_ge(s_hT_low, s + 1)
                pe.wait_ge(s_yb, s + 1)
                parts = ((hT_high, w2_high), (hT_high, w2_low), (hT_low, w2_high))
                for g in range(HG):
                    for n, (rows_part, w_part) in enumerate(parts):
                        last = pe.matmul(ps_2[:, q, 0:C], rows_part[:, q, g * P:(g + 1) * P],
                                         w_part[:, bass.ds(e * (HG * C) + g * C, C)],
                                         start=(g == 0 and n == 0), stop=(g == HG - 1 and n == 2))
                last.then_inc(s_two, 1)

            pe.wait_ge(s_split, 2 * E)
            pe.sem_inc(s_xturn, ROWS_HELD)
            pe.sem_inc(s_one, 2)
            pe.sem_inc(s_two, 2)
            turn_rows(0, 0, 0)
            turn_rows(1, 1, 0)
            first_product(0, 0, expert_of(0))
            first_product(1, 1, expert_of(1))
            turn_rows(2, 2, 0)
            turn_hidden(0, 0)
            with pe.Fori(0, FFN_ROUNDS) as i:
                for k in range(F):
                    s = i * F + k
                    if k == 0:
                        experts = [expert_of(s + n) for n in range(3)]
                    turn_rows(s + 3, k + 3, i * 2 + (k + 3) // ROWS_HELD)
                    first_product(s + 2, k % 2, experts[2])
                    turn_hidden(s + 1, (k + 1) % 2)
                    second_product(s, k % 2, experts[0])
                    if k < F - 1:
                        experts = experts[1:] + [expert_of(s + 3)]
            turn_rows(FFN_TILES + 3, FFN_TILES + 3, (FFN_TILES + 3) // ROWS_HELD)

        @block.scalar
        def _(act):
            act.wait_ge(s_biases, 32)
            for e in range(E):
                act.wait_ge(s_weights[e], 32)
                a, b = e * CG * HIDDEN, (e + 1) * CG * HIDDEN
                act.activation(w1_high[:, a:b], w1[:, a:b], ACT.Copy).then_inc(s_high, 1)
                act.activation(w2_high[:, a:b], w2[:, a:b], ACT.Copy).then_inc(s_high, 1)
            act.sem_inc(s_hidden, 2)
            act.sem_inc(s_result, 2)
            act.preload_act_table(ACT.Gelu)

            def scale_rows(s, q):
                act.wait_ge(s_xturn, ROWS_HELD + s + 1)
                if not isinstance(s, int) or s > 1:
                    act.wait_ge(s_xT_low, s - 1)
                for g in range(CG):
                    act.activation(xT[:, q, g, :], ps_x[:, g * P:(g + 1) * P], ACT.Identity,
                                   bias=t["beta"][:, g:g + 1], scale=t["gamma"][:, g:g + 1]).then_inc(s_xT, 1)

            def activate(s, q):
                act.wait_ge(s_pre, 2 + s + 1)
                act.activation(hidden[:, q, :], pre[:, q, :], ACT.Gelu).then_inc(s_hidden, 1)

            def take_hidden(s, q):
                act.wait_ge(s_hturn, s + 1)
                act.wait_ge(s_two, s + 1)
                act.activation(hT_high[:, q, :], ps_h[:, q, :], ACT.Copy).then_inc(s_hT, 1)

            scale_rows(0, 0)
            scale_rows(1, 1)
            scale_rows(2, 0)
            activate(0, 0)
            activate(1, 1)
            take_hidden(0, 0)
            scale_rows(3, 1)
            with act.Fori(0, FFN_ROUNDS) as i:
                for k in range(F):
                    s = i * F + k
                    q = k % 2
                    take_hidden(s + 1, 1 - q)
                    activate(s + 2, q)
                    scale_rows(s + 4, q)
                    act.wait_ge(s_yb, 2 + s + 1)
                    act.wait_ge(s_free, s + TABLES)
                    act.activation(result[:, q, :], yb[:, q, :], ACT.Copy,
                                   scale=table[:, k, 1:2].bitcast(F32)).then_inc(s_result, 1)

        @block.vector
        def _(dve):
            for e in range(E):
                a, b = e * CG * HIDDEN, (e + 1) * CG * HIDDEN
                for n, (low, full, high) in enumerate(((w1_low, w1, w1_high), (w2_low, w2, w2_high))):
                    dve.wait_ge(s_high, 2 * e + n + 1)
                    dve.tensor_tensor(low[:, a:b], full[:, a:b], high[:, a:b].bitcast(F32),
                                      ALU.subtract).then_inc(s_split, 1)
            dve.sem_inc(s_pre, 2)
            dve.sem_inc(s_yb, 2)

            def expert_of(s):
                return dve.value_load(t["tile_expert"][0:1, bass.ds(s, 1)], min_val=0, max_val=E - 1)

            def bias_one(s, q, e):
                dve.wait_ge(s_one, 2 + s + 1)
                dve.wait_ge(s_hidden, s + 1)
                dve.tensor_tensor(pre[:, q, :], ps_1[:, q, :], b1[:, bass.ds(e * HIDDEN, HIDDEN)],
                                  ALU.add).then_inc(s_pre, 1)

            def split_rows(s, q):
                dve.wait_ge(s_xT, (s + 1) * CG)
                dve.wait_ge(s_one, s + 1)
                dve.tensor_copy(xT_high[:, q, :, :], xT[:, q, :, :]).then_inc(s_xT_high, 1)
                dve.wait_ge(s_xT_high, s + 1)
                dve.tensor_tensor(xT_low[:, q, :, :], xT[:, q, :, :], xT_high[:, q, :, :].bitcast(F32),
                                  ALU.subtract).then_inc(s_xT_low, 1)

            def split_hidden(s, q):
                dve.wait_ge(s_hT, s + 1)
                dve.tensor_tensor(hT_low[:, q, :], ps_h[:, q, :], hT_high[:, q, :].bitcast(F32),
                                  ALU.subtract).then_inc(s_hT_low, 1)

            split_rows(0, 0)
            split_rows(1, 1)
            bias_one(0, 0, expert_of(0))
            split_rows(2, 0)
            bias_one(1, 1, expert_of(1))
            split_hidden(0, 0)
            with dve.Fori(0, FFN_ROUNDS) as i:
                for k in range(F):
                    s = i * F + k
                    q = k % 2
                    if k == 0:
                        experts = [expert_of(s + n) for n in range(3)]
                    split_rows(s + 3, 1 - q)
                    bias_one(s + 2, q, experts[2])
                    expert = experts[0]
                    if k < F - 1:
                        experts = experts[1:] + [expert_of(s + 3)]
                    split_hidden(s + 1, 1 - q)
                    dve.wait_ge(s_two, 2 + s + 1)
                    dve.wait_ge(s_result, s + 1)
                    dve.tensor_tensor(yb[:, q, :], ps_2[:, q, 0:C], b2[:, bass.ds(expert * C, C)],
                                      ALU.add).then_inc(s_yb, 1)


def kernel_program(nc, d):
    with ExitStack() as ctx:
        sb = lambda n, s, dt: ctx.enter_context(nc.sbuf_tensor(n, s, dt))
        t = {
            "ident": sb("ident", [P, P], F32),
            "ones": sb("ones", [P, P], F32),
            "before": sb("before", [P, P], F32),
            "minus_half": sb("minus_half", [P, 1], F32),
            "zeros": sb("zeros", [P, C], F32),
            "iota_i": sb("iota_i", [P, P], I32),
            "iota": sb("iota", [P, P], F32),
            "bn_scale": sb("bn_scale", [P, CG], F32),
            "bn_shift": sb("bn_shift", [P, CG], F32),
            "gamma": sb("gamma", [P, CG], F32),
            "beta": sb("beta", [P, CG], F32),
            "chosen_by": sb("chosen_by", [P, EXPERTS], F32),
            "wide": sb("wide", [1, 1], I32),
            "tile_slot": sb("tile_slot", [1, FFN_LIST], I32),
            "tile_expert": sb("tile_expert", [1, FFN_LIST], I32),
            "node_mean": sb("node_mean", [P, 2, 2], F32),
            "node_stats": sb("node_stats", [P, NODE_TILES * 2], F32),
        }
        with ExitStack() as edges:
            for name, dt in (("edge_src", I32), ("edge_dst", F32), ("edge_w", F32)):
                t[name] = edges.enter_context(nc.sbuf_tensor(name, [P, STEP_ROOM], dt))
            t["step_nodes"] = edges.enter_context(nc.sbuf_tensor("step_nodes", [1, EDGE_ROWS], I32))
            with nc.sbuf_tensor("pad_slots", [P, TABLE_ROWS // P, 2], I32) as pad:
                t["pad_slots"] = pad
                plan_tiles(nc, d, t)
            wide = nc.values_load(t["wide"][0:1, 0:1], min_val=0, max_val=1)
            with nc.If(wide > 0):
                plan_steps(nc, d, t)
            t["sums"] = edges.enter_context(nc.sbuf_tensor("sums", [P, CG, NODES_PAD + P], F32))
            project_input(nc, d, t)
            sum_messages(nc, d, t, d["h"], "c1", 0, ROUNDS)
            with nc.If(wide > 0):
                sum_messages(nc, d, t, d["h"], "c1_more", ROUNDS * RING, MORE_ROUNDS)
            normalize_sums(nc, d, t, "c1")
            project_hidden(nc, d, t)
            sum_messages(nc, d, t, d["h2"], "c2", 0, ROUNDS)
            with nc.If(wide > 0):
                sum_messages(nc, d, t, d["h2"], "c2_more", ROUNDS * RING, MORE_ROUNDS)
            normalize_sums(nc, d, t, "c2")
            route_tokens(nc, d, t)
        for name, size in (("w1", EXPERTS * CG * HIDDEN), ("w2", EXPERTS * HG * C), ("b1", EXPERTS * HIDDEN),
                           ("b2", EXPERTS * C)):
            t[f"ffn_{name}"] = sb(f"ffn_{name}", [P, size], F32)
        t["ffn_loaded"] = [nc.alloc_semaphore(name=f"ffn_loaded{n}") for n in range(1 + EXPERTS)]
        list_tiles(nc, d, t)
        run_experts(nc, d, t)
        nc.clear_and_free_semaphores(t["ffn_loaded"])
        nc.all_engine_barrier()


INPUTS = {
    "x": "x", "src": "src", "dst": "dst", "ew": "edge_weight",
    "c1_w1": "L0_gnn_c1_w1", "c1_b1": "L0_gnn_c1_b1", "c1_w2": "L0_gnn_c1_w2", "c1_b2": "L0_gnn_c1_b2",
    "c1_g": "L0_gnn_c1_g", "c1_b": "L0_gnn_c1_b", "bn1_g": "L0_gnn_bn1_g", "bn1_b": "L0_gnn_bn1_b",
    "c2_w1": "L0_gnn_c2_w1", "c2_b1": "L0_gnn_c2_b1", "c2_w2": "L0_gnn_c2_w2", "c2_b2": "L0_gnn_c2_b2",
    "c2_g": "L0_gnn_c2_g", "c2_b": "L0_gnn_c2_b", "bn2_g": "L0_gnn_bn2_g", "bn2_b": "L0_gnn_bn2_b",
    "gamma": "L0_ffn_gamma", "beta": "L0_ffn_beta", "wr": "L0_ffn_Wr", "br": "L0_ffn_br",
    "w1": "L0_ffn_W1", "b1": "L0_ffn_b1", "w2": "L0_ffn_W2", "b2": "L0_ffn_b2",
}


def kernel(**inputs):
    import numpy as np
    import concourse.bacc as bacc
    from concourse.bass_utils import run_bass_kernel_spmd

    nc = bacc.Bacc("TRN2", target_bir_lowering=False, num_devices=1)
    arrays, d = {}, {}
    pad_edges = EDGE_ROWS * P - EDGES
    for name, key in INPUTS.items():
        a = np.asarray(inputs[key])
        if name == "x":
            a = np.concatenate([a, np.zeros((NODES_PAD - NODES, C), a.dtype)])
        if name in ("src", "ew"):
            a = np.concatenate([a, np.zeros(pad_edges, a.dtype)]).reshape(EDGE_ROWS, P)
        if name == "dst":
            a = np.concatenate([a, np.full(pad_edges, NODES_PAD - 1, a.dtype)]).reshape(EDGE_ROWS, P)
        a = np.ascontiguousarray(a)
        arrays[f"in_{name}"] = a
        d[name] = nc.dram_tensor(f"in_{name}", a.shape, mybir.dt.from_np(a.dtype), kind="ExternalInput").ap()
    scratch = {
        "h": ((NODES_PAD, C), F32), "h2": ((NODES_PAD, C), F32), "step_list": ((EDGE_ROWS,), I32),
        "table": ((TABLE_ROWS, 2), I32), "tokens": ((OUT_ROWS, C), F32),
    }
    for name, (shape, dt) in scratch.items():
        d[name] = nc.dram_tensor(name, shape, dt, kind="Internal").ap()
    d["out"] = nc.dram_tensor("out", (OUT_ROWS, C), F32, kind="ExternalOutput").ap()
    kernel_program(nc, d)
    r = run_bass_kernel_spmd(nc, [arrays], core_ids=[0])
    return r.results[0]["out"][:NODES]
```
